# Optimizing a Trainium2 kernel written in Bass

```python
import numpy as np
import jax
import jax.numpy as jnp

def _softmax(x, axis=-1):
    return jax.nn.softmax(x, axis=axis)

def _gelu(x):
    return jax.nn.gelu(x, approximate=True)

def _silu(x):
    return jax.nn.silu(x)

def _sigmoid(x):
    return jax.nn.sigmoid(x)

def _layernorm(x, axis=-1, eps=1e-05):
    m = jnp.mean(x, axis=axis, keepdims=True)
    v = jnp.var(x, axis=axis, keepdims=True)
    return (x - m) / jnp.sqrt(v + eps)

def _scatter_add(tgt, idx, src, axis=0):
    return tgt.at[idx].add(src)

def _segment_sum(src, seg, n):
    return jax.ops.segment_sum(src, seg, n)
kernel_name = 'mk_decoder_preln_d1_seqx_r8_217c9c'

def setup_inputs(seed: int=0):
    np.random.seed(seed)
    _w = jnp.asarray

    def _rec_inputs():
        import jax
        import jax.numpy as jnp
        _rk = jax.random.key(seed)
        x = -0.0002928 + 1 * jax.random.normal(jax.random.fold_in(_rk, 1), (64, 128, 128), jnp.float32)
        _lenS = 128 - jax.random.randint(jax.random.fold_in(_rk, 7), (64,), 0, max(1, 128 // 4) + 1, jnp.int32)
        _lenS2 = 77 - jax.random.randint(jax.random.fold_in(_rk, 8), (64,), 0, max(1, 77 // 4) + 1, jnp.int32)
        _ctx_1024P = jax.random.normal(jax.random.fold_in(_rk, 11), (64, 16, 128), jnp.float32)
        _ctx_1024c = jax.random.dirichlet(jax.random.fold_in(_rk, 511), 0.3 * jnp.ones((16,), jnp.float32), (64, 77))
        _ctx_1024t = jnp.einsum('bsk,bkd->bsd', _ctx_1024c, _ctx_1024P)
        _ctx_1024t = _ctx_1024t * jax.lax.rsqrt(jnp.mean(jnp.square(_ctx_1024t)) + 1e-12) * 0.953939
        ctx_1024 = -1.39393e-06 + 0.999914 * (_ctx_1024t + 0.3 * jax.random.normal(jax.random.fold_in(_rk, 611), (64, 77, 128), jnp.float32))
        _validS = jnp.arange(128)[None, :] < _lenS[:, None]
        _validS2 = jnp.arange(77)[None, :] < _lenS2[:, None]
        _causal = jnp.tril(jnp.ones((128, 128), dtype=bool))
        mask_BxSxS2_if1 = jnp.where(jnp.ones((64, 128, 77), dtype=bool), 1, 0).astype(jnp.int32)
        return (x, ctx_1024, mask_BxSxS2_if1)
    x, ctx_1024, mask_BxSxS2_if1 = _rec_inputs()

    def _L0_attn_setup():
        import jax, jax.numpy as jnp
        import numpy as np
        NUM_HEADS = 16
        key = jax.random.key(seed)
        ks = jax.random.split(key, 6)
        B, S, D = (2, 256, 128)
        x = jax.random.normal(ks[0], (B, S, D), dtype=jnp.float32)
        s = 1.0 / np.sqrt(D)
        Wq = jax.random.normal(ks[1], (D, D), dtype=jnp.float32) * s
        Wk = jax.random.normal(ks[2], (D, D), dtype=jnp.float32) * s
        Wv = jax.random.normal(ks[3], (D, D), dtype=jnp.float32) * s
        Wff = jax.random.normal(ks[4], (D, D), dtype=jnp.float32) * s
        bff = jax.random.normal(ks[5], (D,), dtype=jnp.float32) * 0.01
        return {'x': x, 'Wq': Wq, 'Wk': Wk, 'Wv': Wv, 'Wff': Wff, 'bff': bff}
    _L0_attn_all = _L0_attn_setup()
    _L0_attn_in = {k: v for k, v in _L0_attn_all.items() if k in ('Wq', 'Wk', 'Wv', 'Wff', 'bff')}
    del _L0_attn_all

    def _L0_xattn_setup():
        import jax, jax.numpy as jnp
        import numpy as np
        NUM_HEADS = 16
        D_MODEL = 128
        D_K = D_MODEL // NUM_HEADS

        def _split_heads(x):
            B, S, _ = x.shape
            return x.reshape(B, S, NUM_HEADS, D_K).transpose(0, 2, 1, 3)
        key = jax.random.key(seed)
        ks = jax.random.split(key, 12)
        B, S = (2, 256)
        scale = 1.0 / np.sqrt(D_MODEL)
        inp = {'query': jax.random.normal(ks[0], (B, S, D_MODEL), jnp.float32), 'key': jax.random.normal(ks[1], (B, S, D_MODEL), jnp.float32), 'value': jax.random.normal(ks[2], (B, S, D_MODEL), jnp.float32), 'mask': jnp.ones((B, S, S), jnp.int32), 'Wq': jax.random.normal(ks[3], (D_MODEL, D_MODEL), jnp.float32) * scale, 'bq': jax.random.normal(ks[4], (D_MODEL,), jnp.float32) * scale, 'Wk': jax.random.normal(ks[5], (D_MODEL, D_MODEL), jnp.float32) * scale, 'bk': jax.random.normal(ks[6], (D_MODEL,), jnp.float32) * scale, 'Wv': jax.random.normal(ks[7], (D_MODEL, D_MODEL), jnp.float32) * scale, 'bv': jax.random.normal(ks[8], (D_MODEL,), jnp.float32) * scale, 'Wo': jax.random.normal(ks[9], (D_MODEL, D_MODEL), jnp.float32) * scale, 'bo': jax.random.normal(ks[10], (D_MODEL,), jnp.float32) * scale}
        return inp
    _L0_xattn_all = _L0_xattn_setup()
    _L0_xattn_in = {k: v for k, v in _L0_xattn_all.items() if k in ('Wq', 'bq', 'Wk', 'bk', 'Wv', 'bv', 'Wo', 'bo')}
    del _L0_xattn_all

    def _L0_ffn_setup():
        import jax, jax.numpy as jnp
        import numpy as np
        EPS = 1e-12

        def _l2norm(v):
            n = jnp.sqrt(jnp.sum(v * v, axis=-1, keepdims=True))
            return v / jnp.maximum(n, EPS)
        key = jax.random.key(seed)
        ks = jax.random.split(key, 6)
        B, S, D, F, E = (2, 256, 128, 512, 8)
        std = 0.02
        return {'x': jax.random.normal(ks[0], (B, S, D), jnp.float32), 'Wp': jax.random.normal(ks[1], (D, D), jnp.float32) * (1.0 / np.sqrt(D)), 'sim_matrix': jax.random.normal(ks[2], (E, D), jnp.float32) * std, 'temperature': jnp.asarray(1.0, jnp.float32), 'W1': jax.random.normal(ks[3], (E, D, F), jnp.float32) * (1.0 / np.sqrt(D)), 'b1': jnp.zeros((E, F), jnp.float32), 'W2': jax.random.normal(ks[4], (E, F, D), jnp.float32) * (1.0 / np.sqrt(F)), 'b2': jnp.zeros((E, D), jnp.float32)}
    _L0_ffn_all = _L0_ffn_setup()
    _L0_ffn_in = {k: v for k, v in _L0_ffn_all.items() if k in ('Wp', 'sim_matrix', 'temperature', 'W1', 'b1', 'W2', 'b2')}
    del _L0_ffn_all
    return {'x': x, 'ctx_1024': ctx_1024, 'mask_BxSxS2_if1': mask_BxSxS2_if1, 'L0_attn_Wq': _L0_attn_in['Wq'], 'L0_attn_Wk': _L0_attn_in['Wk'], 'L0_attn_Wv': _L0_attn_in['Wv'], 'L0_attn_Wff': _L0_attn_in['Wff'], 'L0_attn_bff': _L0_attn_in['bff'], 'L0_xattn_Wq': _L0_xattn_in['Wq'], 'L0_xattn_bq': _L0_xattn_in['bq'], 'L0_xattn_Wk': _L0_xattn_in['Wk'], 'L0_xattn_bk': _L0_xattn_in['bk'], 'L0_xattn_Wv': _L0_xattn_in['Wv'], 'L0_xattn_bv': _L0_xattn_in['bv'], 'L0_xattn_Wo': _L0_xattn_in['Wo'], 'L0_xattn_bo': _L0_xattn_in['bo'], 'L0_ffn_Wp': _L0_ffn_in['Wp'], 'L0_ffn_sim_matrix': _L0_ffn_in['sim_matrix'], 'L0_ffn_temperature': _L0_ffn_in['temperature'], 'L0_ffn_W1': _L0_ffn_in['W1'], 'L0_ffn_b1': _L0_ffn_in['b1'], 'L0_ffn_W2': _L0_ffn_in['W2'], 'L0_ffn_b2': _L0_ffn_in['b2']}

def reference(x, ctx_1024, mask_BxSxS2_if1, L0_attn_Wq, L0_attn_Wk, L0_attn_Wv, L0_attn_Wff, L0_attn_bff, L0_xattn_Wq, L0_xattn_bq, L0_xattn_Wk, L0_xattn_bk, L0_xattn_Wv, L0_xattn_bv, L0_xattn_Wo, L0_xattn_bo, L0_ffn_Wp, L0_ffn_sim_matrix, L0_ffn_temperature, L0_ffn_W1, L0_ffn_b1, L0_ffn_W2, L0_ffn_b2):
    import jax
    import jax.numpy as jnp

    def _L0_attn_ref(x, Wq, Wk, Wv, Wff, bff):
        import jax, jax.numpy as jnp
        import numpy as np
        NUM_HEADS = 16
        B, S, D = x.shape
        H = NUM_HEADS
        Dh = D // H
        q = x @ Wq.T * (1.0 / jnp.sqrt(jnp.asarray(D, x.dtype)))
        k = x @ Wk.T
        v = x @ Wv.T
        q = q.reshape(B, S, H, Dh)
        k = k.reshape(B, S, H, Dh)
        v = v.reshape(B, S, H, Dh)
        scores = jnp.einsum('bqhd,bkhd->bhqk', q, k)
        attn = jax.nn.softmax(scores, axis=-1)
        out = jnp.einsum('bhqk,bkhd->bqhd', attn, v).reshape(B, S, D)
        return out @ Wff.T + bff

    def _L0_xattn_ref(query, key, value, mask, Wq, bq, Wk, bk, Wv, bv, Wo, bo):
        import jax, jax.numpy as jnp
        import numpy as np
        NUM_HEADS = 16
        D_MODEL = 128
        D_K = D_MODEL // NUM_HEADS

        def _split_heads(x):
            B, S, _ = x.shape
            return x.reshape(B, S, NUM_HEADS, D_K).transpose(0, 2, 1, 3)
        q = _split_heads(query @ Wq.T + bq)
        k = _split_heads(key @ Wk.T + bk)
        v = _split_heads(value @ Wv.T + bv)
        scores = jnp.einsum('bhqd,bhkd->bhqk', q, k) / np.sqrt(D_K)
        scores = jnp.where(mask[:, None, :, :] == 0, jnp.float32(-1000000000.0), scores)
        p_attn = jax.nn.softmax(scores, axis=-1)
        attn = jnp.einsum('bhqk,bhkd->bhqd', p_attn, v)
        B, _, S, _ = attn.shape
        x = attn.transpose(0, 2, 1, 3).reshape(B, S, D_MODEL)
        return x @ Wo.T + bo

    def _L0_ffn_ref(x, Wp, sim_matrix, temperature, W1, b1, W2, b2):
        import jax, jax.numpy as jnp
        import numpy as np
        EPS = 1e-12

        def _l2norm(v):
            n = jnp.sqrt(jnp.sum(v * v, axis=-1, keepdims=True))
            return v / jnp.maximum(n, EPS)
        E = sim_matrix.shape[0]
        top_k = 2
        proj = jnp.einsum('bsd,ed->bse', x, Wp)
        pn = _l2norm(proj)
        sn = _l2norm(sim_matrix)
        gate_scores = jnp.einsum('bsd,ed->bse', pn, sn) / temperature
        top_v, top_i = jax.lax.top_k(gate_scores, top_k)
        gate_probs = jax.nn.softmax(top_v, axis=-1)
        comb = jnp.sum(jax.nn.one_hot(top_i, E, dtype=x.dtype) * gate_probs[..., None], axis=-2)
        h = jax.nn.gelu(jnp.einsum('bsd,edf->ebsf', x, W1) + b1[:, None, None, :], approximate=False)
        eo = jnp.einsum('ebsf,efd->ebsd', h, W2) + b2[:, None, None, :]
        out = jnp.einsum('ebsd,bse->bsd', eo, comb)
        return out
    x = x + _L0_attn_ref(_layernorm(x, axis=-1), L0_attn_Wq, L0_attn_Wk, L0_attn_Wv, L0_attn_Wff, L0_attn_bff)
    x = x + _L0_xattn_ref(_layernorm(x, axis=-1), ctx_1024, ctx_1024, mask_BxSxS2_if1, L0_xattn_Wq, L0_xattn_bq, L0_xattn_Wk, L0_xattn_bk, L0_xattn_Wv, L0_xattn_bv, L0_xattn_Wo, L0_xattn_bo)
    x = x + _L0_ffn_ref(_layernorm(x, axis=-1), L0_ffn_Wp, L0_ffn_sim_matrix, L0_ffn_temperature, L0_ffn_W1, L0_ffn_b1, L0_ffn_W2, L0_ffn_b2)
    return x

_drawn_inputs = setup_inputs


def setup_inputs(seed=0):
    import zlib

    import numpy as np

    out = dict(_drawn_inputs(seed))
    spreads = {'L0_ffn_b1': (0.0, 0.1), 'L0_ffn_b2': (0.0, 0.1)}
    factors = {}
    for name, (base, spread) in spreads.items():
        noise = np.random.default_rng([zlib.crc32(name.encode()), seed]).standard_normal(out[name].shape)
        drawn = base * np.exp(spread * noise) if base else spread * noise
        out[name] = jnp.asarray(drawn.astype(out[name].dtype))
    for name, factor in factors.items():
        out[name] = (out[name] * factor).astype(out[name].dtype)
    return out
```

```python
import concourse.bass as bass
from concourse import mybir
from contextlib import ExitStack

F32 = mybir.dt.float32
F32R = mybir.dt.float32r
BF16 = mybir.dt.bfloat16
I32 = mybir.dt.int32
U32 = mybir.dt.uint32
ALU = mybir.AluOpType
ACT = mybir.ActivationFunctionType
AX = mybir.AxisListType

B, S, D = 64, 128, 128
SC = 77
H, DH = 16, 8
E, F = 8, 512
NS = 4
NB = B // NS
T = NS * S
TC = NS * SC
FC = F // 128
NPAIR = 6
KS = NPAIR * DH
KM = KS + 3
HG = H // 2
MASKED = -(2.0 ** 100)
LN_EPS = 1e-5
L2_EPS2 = 1e-24
VW = 32


class Steps:

    def __init__(self, sem, per):
        self.sem, self.per = sem, per

    def val(self, block, k=None):
        return block * self.per + (self.per if k is None else k)


def program(nc, x, ctx_in, mask, Wq, Wk, Wv, Wff, bff, xWq, xbq, xWk, xbk, xWv, xbv, xWo, xbo,
            Wp, WpT, sim, temp, W1, b1, W2, b2, out):
    ctx = ExitStack()
    with ctx:
        def sb(name, shape, dt=F32):
            return ctx.enter_context(nc.sbuf_tensor(name, shape, dt))

        def pb(name, shape):
            return ctx.enter_context(nc.psum_tensor(name, shape, F32))

        def sem(name, per=1):
            return Steps(ctx.enter_context(nc.semaphore(name)), per)

        def dram(name, shape, dt=F32):
            return nc.dram_tensor(name, shape, dt, kind="Internal").ap()

        x_v = x.rearrange("(n s) p d -> n p s d", s=NS)
        ctx_v = ctx_in.rearrange("(n s) p d -> n p s d", s=NS)
        mask_v = mask.rearrange("(n s) p k -> n p s k", s=NS)
        out_v = out.rearrange("(n s) p d -> n p s d", s=NS)
        stk = {"q": dram("stk_q", [NPAIR, D, T], BF16), "k": dram("stk_k", [NPAIR, D, T], BF16),
               "cq": dram("stk_cq", [NPAIR, D, T], BF16), "ck": dram("stk_ck", [NPAIR, D, TC], BF16)}
        mscr = {"m": dram("mscr", [3, H, T], BF16), "cm": dram("cmscr", [3, H, T], BF16)}
        x3_d = dram("x3_d", [NB, 128, NS, D])
        xt_d = dram("xt_d", [NB, 128, T])
        comb_d = dram("comb_d", [NB, E, T])

        ident = sb("ident", [128, 128])
        identb = sb("identb", [128, 128], BF16)
        mhalf = sb("mhalf", [128, NS])
        iota8 = sb("iota8", [128, E])
        w_q, w_k, w_v, w_ff = (sb(n, [128, 128]) for n in ("w_q", "w_k", "w_v", "w_ff"))
        cw_q, cw_k, cw_v, cw_o = (sb(n, [128, 128]) for n in ("cw_q", "cw_k", "cw_v", "cw_o"))
        bff_b, bo_b = sb("bff_b", [128, D]), sb("bo_b", [128, D])
        bv_b = sb("bv_b", [SC, D])
        bq_c, bk_c = sb("bq_c", [128, 1]), sb("bk_c", [128, 1])
        wp_n = sb("wp_n", [128, 128])
        wpx = sb("wpx", [128, D + E])
        sim_n, sim_u, sim_j = sb("sim_n", [E, D]), sb("sim_u", [E, D]), sb("sim_j", [E, D])
        sim_sq_sum, sim_ss, sim_rn = sb("sim_sq_sum", [E, 1]), sb("sim_ss", [E, 1]), sb("sim_rn", [E, 1])
        sim_sum = sem("sim_sum")
        simT = sb("simT", [128, E])
        temp_b, itemp = sb("temp_b", [128, 1]), sb("itemp", [128, 1])
        b1_c = sb("b1_c", [128, E, FC])
        b2_r = sb("b2_r", [E, D])

        phase_a = ctx.enter_context(ExitStack())

        def sa(name, shape, dt=F32):
            return phase_a.enter_context(nc.sbuf_tensor(name, shape, dt))

        xin = sa("xin", [128, NS, D])
        cin = sa("cin", [SC, NS, D])
        mk = sa("mk", [128, NS, SC], I32)
        mbias = sa("mbias", [128, NS, SC], BF16)
        xres, x2, x2res, x3 = (sa(n, [128, NS, D]) for n in ("xres", "x2", "x2res", "x3"))
        xn = {n: sa(f"xn_{n}", [128, NS, D]) for n in ("1", "2", "3")}
        xnT = {n: sa(f"xnT_{n}", [128, T]) for n in ("1", "2", "3")}
        cT = sa("cT", [128, TC])
        lnst = {n: sa(f"lnst_{n}", [128, NS, 6]) for n in ("1", "2", "3")}
        lnmv = {n: sa(f"lnmv_{n}", [128, NS, 2]) for n in ("1", "2", "3")}
        lnve = {n: sa(f"lnve_{n}", [128, NS]) for n in ("1", "2", "3")}
        lnrs = {n: sa(f"lnrs_{n}", [128, NS]) for n in ("1", "2", "3")}
        parts = {n: sa(f"parts_{n}", [128, 3, T], BF16) for n in ("q", "k", "cq")}
        parts["ck"] = sa("parts_ck", [128, 3, TC], BF16)
        parts["m"] = sa("parts_m", [H, 3, T], BF16)
        parts["cm"] = sa("parts_cm", [H, 3, T], BF16)
        rest = {n: sa(f"rest_{n}", [128, T]) for n in ("q", "k", "cq")}
        rest["ck"] = sa("rest_ck", [128, TC])
        rest["m"] = sa("rest_m", [H, T])
        rest["cm"] = sa("rest_cm", [H, T])
        qs, ks, cqs = (sa(n, [128, HG, T], BF16) for n in ("qs", "ks", "cqs"))
        cks = sa("cks", [128, HG, TC], BF16)
        vaug = sa("vaug", [128, NS, H, VW])
        cvaug = sa("cvaug", [SC, NS, H, VW])
        negm = {n: sa(f"negm_{n}", [128, NS, 2, HG]) for n in ("m", "cm")}
        probs = [sa(f"probs{i}", [128, 2, T]) for i in range(2)]
        oT = {n: sa(f"oT_{n}", [128, NS, T]) for n in ("s", "c")}
        rden = {n: sa(f"rden_{n}", [128, NS, H]) for n in ("s", "c")}
        on = {n: sa(f"on_{n}", [128, NS, H, DH]) for n in ("s", "c")}
        onT = {n: sa(f"onT_{n}", [128, T]) for n in ("s", "c")}
        sq_junk = sa("sq_junk", [128, NS, D])
        ss, ssc, rn = sa("ss", [128, NS]), sa("ssc", [128, NS]), sa("rn", [128, NS])
        gs = sa("gs", [128, NS, E])
        top_v = sa("top_v", [128, NS, 8])
        top_i = sa("top_i", [128, NS, 8], U32)
        top_f = sa("top_f", [128, NS, 2])
        dv, ev, den, p1, p2 = (sa(n, [128, NS]) for n in ("dv", "ev", "den", "p1", "p2"))
        eq1, eq2, c1, c2, comb = (sa(n, [128, NS, E]) for n in ("eq1", "eq2", "c1", "c2", "comb"))
        combT = sa("combT", [E, T])

        sc = [pb(f"sc{i}", [128, 2, 512]) for i in range(2)]
        pv = [pb(f"pv{i}", [128, 512]) for i in range(2)]
        wb = [pb(f"wb{i}", [128, 512]) for i in range(2)]

        const_in = sem("const_in")
        ident_ok, ones_ok, vones_ok = sem("ident_ok"), sem("ones_ok"), sem("vones_ok")
        sim_sq, sim_pow, sim_ok, simT_f, simT_ok, wps_f, wps_ok, itemp_ok = (
            sem(n) for n in ("sim_sq", "sim_pow", "sim_ok", "simT_f", "simT_ok", "wps_f", "wps_ok", "itemp_ok"))
        x_in, c_in, mk_in = sem("x_in", 16), sem("c_in", 16), sem("mk_in", 16)
        mb_ok = sem("mb_ok")
        xres_ok, x2res_ok = sem("xres_ok"), sem("x2res_ok")
        ln_st = {n: sem(f"ln{n}_st", 2) for n in "123"}
        ln_ve = {n: sem(f"ln{n}_ve") for n in "123"}
        ln_rs = {n: sem(f"ln{n}_rs") for n in "123"}
        ln_ok = {n: sem(f"ln{n}_ok") for n in "123"}
        ONE = ("x1T", "x2T", "x3T", "cT", "q", "k", "v", "cq", "ck", "cv", "m", "cm", "onT_s", "onT_c",
               "y_s", "y_c", "pj0", "pj1", "combT")
        filled = {n: sem(f"{n}_filled") for n in ONE}
        drained = {n: sem(f"{n}_drained") for n in ONE}
        for n in ("s", "c"):
            filled[f"oTT_{n}"] = sem(f"oTT_{n}_filled", NS)
            drained[f"oTT_{n}"] = sem(f"oTT_{n}_drained", NS)
        part1 = {n: sem(f"{n}_part1") for n in ("q", "k", "cq", "ck", "m", "cm")}
        part2 = {n: sem(f"{n}_part2") for n in part1}
        part3 = {n: sem(f"{n}_part3") for n in part1}
        dumped = {n: sem(f"{n}_dumped", 48) for n in ("q", "k", "cq", "ck")}
        dumped["m"], dumped["cm"] = sem("m_dumped", 16), sem("cm_dumped", 16)
        stacked = {n: sem(f"{n}_stacked", 32) for n in part1}
        max_f = {n: sem(f"{n}_sc_filled", 2 * NS) for n in ("m", "cm")}
        max_ok = {n: sem(f"{n}_max_ok", 2 * NS) for n in ("m", "cm")}
        st_f = {n: sem(f"st_{n}_filled", 2 * NS) for n in ("s", "c")}
        exp_ok = {n: sem(f"exp_{n}_ok", 2 * NS) for n in ("s", "c")}
        pv_ok = {n: sem(f"pv_{n}_ok", 2 * NS) for n in ("s", "c")}
        oT_ok = {n: sem(f"oT_{n}_ok", NS) for n in ("s", "c")}
        rden_ok = {n: sem(f"rden_{n}_ok", NS) for n in ("s", "c")}
        ss_ok, ssc_ok, rn_ok, dv_ok, ev_ok, comb_ok = (
            sem(n) for n in ("ss_ok", "ssc_ok", "rn_ok", "dv_ok", "ev_ok", "comb_ok"))
        gate_step = sem("gate_step", 8)
        x3_st, xt_st, comb_st = sem("x3_st", 16), sem("xt_st", 16), sem("comb_st", 16)

        CONSTS = [(w_q, Wq), (w_k, Wk), (w_v, Wv), (w_ff, Wff), (cw_q, xWq), (cw_k, xWk), (cw_v, xWv), (cw_o, xWo),
                  (bff_b, bff.unsqueeze(0).broadcast_to([128, D])), (bo_b, xbo.unsqueeze(0).broadcast_to([128, D])),
                  (bv_b, xbv.unsqueeze(0).broadcast_to([SC, D])),
                  (bq_c, xbq.unsqueeze(1)), (bk_c, xbk.unsqueeze(1)), (wp_n, Wp), (wpx[:, 0:D], WpT), (sim_n, sim),
                  (temp_b, temp.unsqueeze(0).broadcast_to([128, 1])),
                  (b1_c, b1), (b2_r, b2)]

        def heads_of(tile, n):
            return tile[:, :, 0:4 * n].rearrange("p g (j k) -> p g j k", j=4)

        def steps(run):
            run(0, False, True, True)
            run(1, True, True, True)
            with run.engine.Fori(2, NB - 2) as t:
                run(t, True, True, True)
            run(NB - 2, True, True, True)
            run(NB - 1, True, True, False)
            run(NB, True, False, False)

        class Run:
            def __init__(self, engine, body):
                self.engine, self.body = engine, body

            def __call__(self, t, cross, own, nxt):
                self.body(t, cross, own, nxt)

        with nc.Block() as block:
            @block.sync
            def _(sp):
                for dst, src in CONSTS:
                    sp.dma_start(dst[:, :, :] if len(dst.shape) == 3 else dst[:, :], src).then_inc(const_in.sem, 16)
                sp.dma_start(xin[:], x_v[0]).then_inc(x_in.sem, 16)
                sp.dma_start(cin[:], ctx_v[0]).then_inc(c_in.sem, 16)
                sp.dma_start(mk[:], mask_v[0]).then_inc(mk_in.sem, 16)

                def dump(n, t, first):
                    sp.wait_ge(part3[n].sem, part3[n].val(t))
                    scr, p = stk[n], parts[n]
                    cols = p.shape[2]
                    if n in ("q", "cq"):
                        runs = [(0, 3, p[:, 0:1, :].broadcast_to([128, 3, cols])),
                                (3, 5, p[:, 1:2, :].broadcast_to([128, 2, cols])), (5, 6, p[:, 2:3, :])]
                    else:
                        runs = [(0, 3, p[:, 0:3, :]), (3, 5, p[:, 0:2, :]), (5, 6, p[:, 0:1, :])]
                    for a, b, src in runs:
                        sp.dma_start(scr[a:b].rearrange("c r t -> r c t"), src).then_inc(dumped[n].sem, 16)

                def stack(n, t, dst):
                    sp.wait_ge(dumped[n].sem, dumped[n].val(t))
                    view = stk[n].rearrange("c (i g j) t -> g (c i) j t", i=DH, g=2)
                    for g in range(2):
                        sp.dma_start(dst[64 * g:64 * g + KS, :, :], view[g]).then_inc(stacked[n].sem, 16)

                def fold(n, t, dst):
                    sp.wait_ge(part3[n].sem, part3[n].val(t))
                    sp.dma_start(mscr[n].rearrange("c h t -> h c t"), parts[n][:]).then_inc(dumped[n].sem, 16)
                    sp.wait_ge(dumped[n].sem, dumped[n].val(t))
                    view = mscr[n].rearrange("c (g j) t -> g c j t", g=2)
                    for g in range(2):
                        sp.dma_start(dst[64 * g + KS:64 * g + KM, :, :], view[g]).then_inc(stacked[n].sem, 16)

                def self_stacks(t, first=False):
                    for n, dst in (("q", qs), ("k", ks)):
                        dump(n, t, first)
                    for n, dst in (("q", qs), ("k", ks)):
                        if not first:
                            sp.wait_ge(st_f["s"].sem, st_f["s"].val(t - 1))
                        stack(n, t, dst)

                def body(t, cross, own, nxt):
                    if cross:
                        dump("cq", t - 1, False)
                        stack("cq", t - 1, cqs)
                    if own:
                        fold("m", t, qs)
                    if cross:
                        fold("cm", t - 1, cqs)
                    if own:
                        if nxt:
                            sp.wait_ge(ln_ok["1"].sem, ln_ok["1"].val(t + 1))
                            sp.wait_ge(xres_ok.sem, xres_ok.val(t + 1))
                            if isinstance(t, int):
                                if t + 2 < NB:
                                    sp.dma_start(xin[:], x_v[t + 2]).then_inc(x_in.sem, 16)
                            else:
                                sp.dma_start(xin[:], x_v[t + 2]).then_inc(x_in.sem, 16)
                            self_stacks(t + 1)
                        dump("ck", t, False)
                        stack_ck(t, cross)
                        if nxt:
                            sp.wait_ge(mb_ok.sem, mb_ok.val(t))
                            sp.dma_start(mk[:], mask_v[t + 1]).then_inc(mk_in.sem, 16)
                            sp.wait_ge(filled["cT"].sem, filled["cT"].val(t))
                            sp.dma_start(cin[:], ctx_v[t + 1]).then_inc(c_in.sem, 16)
                    if cross:
                        sp.wait_ge(drained["x3T"].sem, drained["x3T"].val(t - 1))
                        sp.dma_start(x3_d[t - 1], x3[:]).then_inc(x3_st.sem, 16)
                        sp.dma_start(xt_d[t - 1], xnT["3"][:]).then_inc(xt_st.sem, 16)
                        sp.wait_ge(drained["combT"].sem, drained["combT"].val(t - 1))
                        sp.dma_start(comb_d[t - 1], combT[:]).then_inc(comb_st.sem, 16)

                def stack_ck(t, cross):
                    if cross:
                        sp.wait_ge(st_f["c"].sem, st_f["c"].val(t - 1))
                    stack("ck", t, cks)

                sp.wait_ge(ln_ok["1"].sem, ln_ok["1"].val(0))
                sp.wait_ge(xres_ok.sem, xres_ok.val(0))
                sp.dma_start(xin[:], x_v[1]).then_inc(x_in.sem, 16)
                sp.wait_ge(ones_ok.sem, 4)
                self_stacks(0, first=True)
                steps(Run(sp, body))
                for s_ in (x3_st, xt_st, comb_st):
                    sp.wait_ge(s_.sem, s_.val(NB - 1))

            @block.gpsimd
            def _(pool):
                nc.gpsimd.memset(ident[:], 0.0).then_inc(ident_ok.sem, 1)
                nc.gpsimd.memset(identb[:], 0.0).then_inc(ident_ok.sem, 1)
                pool.wait_ge(ident_ok.sem, 2)
                for m in (ident, identb):
                    nc.gpsimd.affine_select(out=m[:], in_=m[:], compare_op=ALU.not_equal, fill=1.0, base=0,
                                            pattern=[[-1, 128]], channel_multiplier=1).then_inc(ident_ok.sem, 1)
                nc.gpsimd.memset(mhalf[:], -0.5).then_inc(ident_ok.sem, 1)
                pool.wait_ge(ident_ok.sem, 5)
                pool.wait_ge(const_in.sem, 16 * len(CONSTS))

                def power(n, t):
                    pool.wait_ge(ln_ve[n].sem, ln_ve[n].val(t))
                    nc.gpsimd.tensor_tensor(out=lnrs[n][:], in0=lnve[n][:], in1=mhalf[:], op=ALU.pow)\
                        .then_inc(ln_rs[n].sem, 1)

                def residual(dst, src, bias, done, t):
                    nc.gpsimd.tensor_tensor(out=dst[:], in0=src[:], in1=bias[:].unsqueeze(1).broadcast_to([128, NS, D]),
                                            op=ALU.add).then_inc(done.sem, 1)

                def third(n, t):
                    pool.wait_ge(part2[n].sem, part2[n].val(t))
                    nc.gpsimd.tensor_tensor(out=parts[n][:, 2, :], in0=rest[n][:], in1=parts[n][:, 1, :],
                                            op=ALU.subtract).then_inc(part3[n].sem, 1)

                def mask_bias(t):
                    pool.wait_ge(mk_in.sem, mk_in.val(t))
                    pool.nop(nofuse=True)
                    nc.gpsimd.tensor_scalar(out=mbias[:], in0=mk[:], scalar1=0.0, scalar2=MASKED,
                                            op0=ALU.is_equal, op1=ALU.mult).then_inc(mb_ok.sem, 1)

                power("1", 0)
                residual(xres, xin, bff_b, xres_ok, 0)
                third("q", 0)
                third("k", 0)
                pool.wait_ge(sim_sq.sem, 1)
                nc.gpsimd.tensor_tensor(out=sim_rn[:], in0=sim_ss[:], in1=mhalf[0:E, 0:1], op=ALU.pow)\
                    .then_inc(sim_pow.sem, 1)

                def body(t, cross, own, nxt):
                    if cross:
                        third("cq", t - 1)
                    if nxt:
                        power("1", t + 1)
                    if own:
                        third("m", t)
                    if cross:
                        third("cm", t - 1)
                    if own:
                        power("2", t)
                    if nxt:
                        pool.wait_ge(drained["y_s"].sem, drained["y_s"].val(t))
                        residual(xres, xin, bff_b, xres_ok, t + 1)
                        third("q", t + 1)
                        third("k", t + 1)
                    if own:
                        if cross:
                            pool.wait_ge(drained["y_c"].sem, drained["y_c"].val(t - 1))
                        residual(x2res, x2, bo_b, x2res_ok, t)
                        mask_bias(t)
                        third("ck", t)
                    if cross:
                        power("3", t - 1)
                        pool.wait_ge(ssc_ok.sem, ssc_ok.val(t - 1))
                        nc.gpsimd.tensor_tensor(out=rn[:], in0=ssc[:], in1=mhalf[:], op=ALU.pow).then_inc(rn_ok.sem, 1)

                steps(Run(pool, body))

            @block.scalar
            def _(act):
                act.wait_ge(const_in.sem, 16 * len(CONSTS))

                def evac(dst, n, t, bank, cols=T, rows=128):
                    act.wait_ge(filled[n].sem, filled[n].val(t))
                    nc.scalar.activation(dst, wb[bank][0:rows, 0:cols], ACT.Copy).then_inc(drained[n].sem, 1)

                def first(n, t, bank, bias=None):
                    p = parts[n]
                    act.wait_ge(filled[n].sem, filled[n].val(t))
                    src = wb[bank][0:p.shape[0], 0:p.shape[2]]
                    if bias is None:
                        i = nc.scalar.activation(p[:, 0, :], src, ACT.Copy)
                    else:
                        i = nc.scalar.activation(p[:, 0, :], src, ACT.Identity, bias=bias[:, 0:1])
                    i.then_inc(part1[n].sem, 1)

                def self_proj(t):
                    evac(xnT["1"][:], "x1T", t, 0)
                    first("q", t, 1)
                    first("k", t, 0)
                    act.wait_ge(filled["v"].sem, filled["v"].val(t))
                    nc.scalar.activation(vaug[:, :, :, 0:DH], wb[1][:].rearrange("p (s h i) -> p s h i", s=NS, h=H),
                                         ACT.Copy).then_inc(drained["v"].sem, 1)

                def attend(n, t, rows, scale):
                    for u in range(2 * NS):
                        act.wait_ge(st_f[n].sem, st_f[n].val(t, u + 1))
                        if u >= 2:
                            act.wait_ge(pv_ok[n].sem, pv_ok[n].val(t, u - 1))
                        nc.scalar.activation(probs[u % 2][0:rows], sc[u % 2][0:rows], ACT.Exp, scale=scale)\
                            .then_inc(exp_ok[n].sem, 1)
                        if u % 2 == 0 and u > 0:
                            out_T(n, t, u // 2 - 1)
                    out_T(n, t, NS - 1)

                def out_T(n, t, s):
                    act.wait_ge(pv_ok[n].sem, pv_ok[n].val(t, 2 * s + 2))
                    nc.scalar.activation(oT[n][:, s, :], pv[s % 2][:], ACT.Copy).then_inc(oT_ok[n].sem, 1)

                self_proj(0)
                act.wait_ge(simT_f.sem, 1)
                nc.scalar.activation(simT[:], wb[0][:, 0:E], ACT.Copy).then_inc(simT_ok.sem, 1)
                act.wait_ge(wps_f.sem, 1)
                nc.scalar.activation(wpx[:, D:D + E], wb[0][:, 0:E], ACT.Copy).then_inc(wps_ok.sem, 1)

                def body(t, cross, own, nxt):
                    if cross:
                        evac(xnT["2"][:], "x2T", t - 1, 0)
                        first("cq", t - 1, 1, bq_c)
                    if own:
                        first("m", t, 0)
                    if cross:
                        first("cm", t - 1, 1)
                    if own:
                        attend("s", t, 128, float(D) ** -0.5)
                        evac(onT["s"][:], "onT_s", t, 0)
                    if nxt:
                        self_proj(t + 1)
                    if cross:
                        attend("c", t - 1, SC, float(DH) ** -0.5)
                        evac(onT["c"][:], "onT_c", t - 1, 0)
                    if own:
                        evac(cT[:], "cT", t, 0, TC)
                        first("ck", t, 1, bk_c)
                    if cross:
                        evac(xnT["3"][:], "x3T", t - 1, 1)
                        for s in range(NS):
                            if s % 2 == 0:
                                n = f"pj{s // 2}"
                                act.wait_ge(filled[n].sem, filled[n].val(t - 1))
                            a = (D + E) * (s % 2)
                            i = nc.scalar.activation(sq_junk[:, s, :], wb[s // 2][:, a:a + D], ACT.Square,
                                                     accum_out=ss[:, s:s + 1])
                        i.then_inc(ss_ok.sem, 1)
                        act.wait_ge(dv_ok.sem, dv_ok.val(t - 1))
                        nc.scalar.activation(ev[:], dv[:], ACT.Exp).then_inc(ev_ok.sem, 1)
                        evac(combT[:], "combT", t - 1, 0, T, E)

                steps(Run(act, body))

            @block.vector
            def _(dve):
                for tile in (qs, ks, cqs, cks):
                    nc.vector.memset(tile[:], 1.0).then_inc(ones_ok.sem, 1)
                for tile in (vaug, cvaug):
                    nc.vector.memset(tile[:], 0.0).then_inc(vones_ok.sem, 1)
                dve.wait_ge(vones_ok.sem, 2)
                for tile in (vaug, cvaug):
                    nc.vector.memset(tile[:, :, :, DH:DH + 1], 1.0).then_inc(vones_ok.sem, 1)
                for e in range(E):
                    i = nc.vector.memset(iota8[:, e:e + 1], float(e))
                i.then_inc(itemp_ok.sem, 1)
                dve.wait_ge(const_in.sem, 16 * len(CONSTS))
                nc.vector.reciprocal(itemp[:], temp_b[:]).then_inc(itemp_ok.sem, 1)
                dve.wait_ge(itemp_ok.sem, 2)

                def stats(n, t, src):
                    for s in range(NS):
                        i = nc.vector.bn_stats(lnst[n][:, s, :], src[:, s, :])
                    i.then_inc(ln_st[n].sem, 1)
                    dve.wait_ge(ln_st[n].sem, ln_st[n].val(t, 1))
                    dve.nop(nofuse=True)
                    for s in range(NS):
                        i = nc.vector.bn_aggr(lnmv[n][:, s, :], lnst[n][:, s, :])
                    i.then_inc(ln_st[n].sem, 1)
                    dve.wait_ge(ln_st[n].sem, ln_st[n].val(t, 2))
                    nc.vector.tensor_scalar(lnve[n][:], lnmv[n][:, :, 1], LN_EPS, None, ALU.add).then_inc(ln_ve[n].sem, 1)

                def normalise(n, t, src):
                    dve.wait_ge(ln_rs[n].sem, ln_rs[n].val(t))
                    for s in range(NS):
                        i = nc.vector.tensor_scalar(xn[n][:, s, :], src[:, s, :], lnmv[n][:, s, 0:1], lnrs[n][:, s:s + 1],
                                                    ALU.subtract, ALU.mult)
                    i.then_inc(ln_ok[n].sem, 1)

                def second(n, t, bank, bias=None):
                    p, r = parts[n], rest[n]
                    dve.wait_ge(part1[n].sem, part1[n].val(t))
                    src = wb[bank][0:p.shape[0], 0:p.shape[2]]
                    if bias is None:
                        i = nc.vector.tensor_tensor(out=r[:], in0=src, in1=p[:, 0, :], op=ALU.subtract)
                    else:
                        i = nc.vector.scalar_tensor_tensor(out=r[:], in0=src, scalar=bias[:, 0:1], in1=p[:, 0, :],
                                                           op0=ALU.add, op1=ALU.subtract)
                    i.then_inc(drained[n].sem, 1)
                    dve.wait_ge(drained[n].sem, drained[n].val(t))
                    nc.vector.tensor_copy(p[:, 1, :], r[:]).then_inc(part2[n].sem, 1)

                def maxima(n, t, cols):
                    for u in range(2 * NS):
                        s, half = u // 2, u % 2
                        dve.wait_ge(max_f[n].sem, max_f[n].val(t, u + 1))
                        nc.vector.tensor_reduce(out=negm[n][:, s, :, 4 * half:4 * half + 4], in_=heads_of(sc[u % 2], cols),
                                                op=ALU.max, axis=AX.X, negate=True).then_inc(max_ok[n].sem, 1)

                def finish(n, t, res, dst):
                    for s in range(NS):
                        k = f"oTT_{n}"
                        dve.wait_ge(filled[k].sem, filled[k].val(t, s + 1))
                        v = wb[s % 2][:].rearrange("p (h w) -> p h w", w=VW)
                        nc.vector.reciprocal(rden[n][:, s, :], v[:, :, DH]).then_inc(rden_ok[n].sem, 1)
                        dve.wait_ge(rden_ok[n].sem, rden_ok[n].val(t, s + 1))
                        nc.vector.tensor_tensor(out=on[n][:, s], in0=v[:, :, 0:DH],
                                                in1=rden[n][:, s, :].unsqueeze(2).broadcast_to([128, H, DH]),
                                                op=ALU.mult).then_inc(drained[k].sem, 1)
                    k = f"y_{n}"
                    dve.wait_ge(filled[k].sem, filled[k].val(t))
                    rsem = xres_ok if n == "s" else x2res_ok
                    dve.wait_ge(rsem.sem, rsem.val(t))
                    nc.vector.tensor_tensor(out=dst[:], in0=wb[1][:].rearrange("p (s d) -> p s d", s=NS), in1=res[:],
                                            op=ALU.add).then_inc(drained[k].sem, 1)
                    dve.wait_ge(drained[k].sem, drained[k].val(t))

                def gate(t):
                    dve.wait_ge(ss_ok.sem, ss_ok.val(t))
                    nc.vector.tensor_scalar(ssc[:], ss[:], L2_EPS2, None, ALU.max).then_inc(ssc_ok.sem, 1)
                    dve.wait_ge(rn_ok.sem, rn_ok.val(t))
                    for s in range(NS):
                        a = (D + E) * (s % 2) + D
                        i = nc.vector.tensor_scalar(gs[:, s, :], wb[s // 2][:, a:a + E], rn[:, s:s + 1], itemp[:, 0:1],
                                                    ALU.mult, ALU.mult)
                        if s % 2:
                            i.then_inc(drained[f"pj{s // 2}"].sem, 1)
                    dve.wait_ge(drained["pj1"].sem, drained["pj1"].val(t))
                    dve.nop(nofuse=True)
                    for s in range(NS):
                        i = nc.vector.max(top_v[:, s, :], gs[:, s, :])
                    i.then_inc(gate_step.sem, 1)
                    dve.wait_ge(gate_step.sem, gate_step.val(t, 1))
                    dve.nop(nofuse=True)
                    for s in range(NS):
                        i = nc.vector.max_index(top_i[:, s, :], top_v[:, s, :], gs[:, s, :])
                    i.then_inc(gate_step.sem, 1)
                    nc.vector.tensor_tensor(out=dv[:], in0=top_v[:, :, 1], in1=top_v[:, :, 0], op=ALU.subtract)\
                        .then_inc(dv_ok.sem, 1)
                    dve.wait_ge(gate_step.sem, gate_step.val(t, 2))
                    nc.vector.tensor_copy(top_f[:], top_i[:, :, 0:2]).then_inc(gate_step.sem, 1)
                    dve.wait_ge(gate_step.sem, gate_step.val(t, 3))
                    for eq, k in ((eq1, 0), (eq2, 1)):
                        i = nc.vector.tensor_tensor(out=eq[:], in0=iota8[:].unsqueeze(1).broadcast_to([128, NS, E]),
                                                    in1=top_f[:, :, k:k + 1].broadcast_to([128, NS, E]), op=ALU.is_equal)
                    i.then_inc(gate_step.sem, 1)
                    dve.wait_ge(ev_ok.sem, ev_ok.val(t))
                    nc.vector.tensor_scalar(den[:], ev[:], 1.0, None, ALU.add).then_inc(gate_step.sem, 1)
                    dve.wait_ge(gate_step.sem, gate_step.val(t, 5))
                    nc.vector.reciprocal(p1[:], den[:]).then_inc(gate_step.sem, 1)
                    dve.wait_ge(gate_step.sem, gate_step.val(t, 6))
                    nc.vector.tensor_tensor(out=p2[:], in0=ev[:], in1=p1[:], op=ALU.mult).then_inc(gate_step.sem, 1)
                    dve.wait_ge(gate_step.sem, gate_step.val(t, 7))
                    dve.wait_ge(gate_step.sem, gate_step.val(t, 4))
                    for eq, w, c in ((eq1, p1, c1), (eq2, p2, c2)):
                        i = nc.vector.tensor_tensor(out=c[:], in0=eq[:], in1=w[:].unsqueeze(2).broadcast_to([128, NS, E]),
                                                    op=ALU.mult)
                    i.then_inc(gate_step.sem, 1)
                    dve.wait_ge(gate_step.sem, gate_step.val(t, 8))
                    nc.vector.tensor_tensor(out=comb[:], in0=c1[:], in1=c2[:], op=ALU.add).then_inc(comb_ok.sem, 1)

                dve.wait_ge(x_in.sem, x_in.val(0))
                stats("1", 0, xin)
                normalise("1", 0, xin)
                second("q", 0, 1)
                second("k", 0, 0)
                nc.vector.tensor_tensor_reduce(out=sim_j[:], in0=sim_n[:], in1=sim_n[:], scale=1.0, scalar=0.0,
                                               op0=ALU.mult, op1=ALU.add, accum_out=sim_sq_sum[:]).then_inc(sim_sum.sem, 1)
                dve.wait_ge(sim_sum.sem, 1)
                nc.vector.tensor_scalar(sim_ss[:], sim_sq_sum[:], L2_EPS2, None, ALU.max).then_inc(sim_sq.sem, 1)
                dve.wait_ge(sim_pow.sem, 1)
                nc.vector.tensor_scalar(sim_u[:], sim_n[:], sim_rn[:, 0:1], None, ALU.mult).then_inc(sim_ok.sem, 1)

                def body(t, cross, own, nxt):
                    if cross:
                        second("cq", t - 1, 1, bq_c)
                    if own:
                        maxima("m", t, S)
                    if nxt:
                        dve.wait_ge(x_in.sem, x_in.val(t + 1))
                        stats("1", t + 1, xin)
                    if own:
                        second("m", t, 0)
                    if cross:
                        maxima("cm", t - 1, SC)
                        second("cm", t - 1, 1)
                    if nxt:
                        normalise("1", t + 1, xin)
                    if own:
                        finish("s", t, xres, x2)
                        stats("2", t, x2)
                    if nxt:
                        second("q", t + 1, 1)
                        second("k", t + 1, 0)
                    if own:
                        normalise("2", t, x2)
                    if cross:
                        if not isinstance(t, int) or t >= 2:
                            dve.wait_ge(x3_st.sem, x3_st.val(t - 2))
                        finish("c", t - 1, x2res, x3)
                        stats("3", t - 1, x3)
                    if own:
                        second("ck", t, 1, bk_c)
                        dve.wait_ge(filled["cv"].sem, filled["cv"].val(t))
                        nc.vector.tensor_tensor(
                            out=cvaug[:, :, :, 0:DH], in0=wb[0][0:SC, :].rearrange("p (s h i) -> p s h i", s=NS, h=H),
                            in1=bv_b[:].rearrange("p (h i) -> p h i", h=H).unsqueeze(1).broadcast_to([SC, NS, H, DH]),
                            op=ALU.add).then_inc(drained["cv"].sem, 1)
                    if cross:
                        normalise("3", t - 1, x3)
                        gate(t - 1)

                steps(Run(dve, body))

            @block.tensor
            def _(pe):
                pe.wait_ge(const_in.sem, 16 * len(CONSTS))
                pe.wait_ge(ident_ok.sem, 4)
                user = [None, None]

                def claim(bank, n, t, k=None):
                    if user[bank] is not None:
                        last, value = user[bank]
                        pe.wait_ge(drained[last].sem, value)
                    user[bank] = (n, drained[n].val(t, k))

                def transposes(n, t, bank, pieces, rows):
                    claim(bank, n, t)
                    for j, src in enumerate(pieces):
                        w = src.shape[0]
                        i = nc.tensor.transpose(wb[bank][0:rows, j * w:(j + 1) * w], src, ident[0:w, 0:w])
                    i.then_inc(filled[n].sem, 1)

                def product(n, t, bank, lhsT, rhs, cols):
                    claim(bank, n, t)
                    nc.tensor.matmul(wb[bank][:, 0:cols], lhsT, rhs, start=True, stop=True).then_inc(filled[n].sem, 1)

                def by_token(n, t, bank, lhs, w, width, rows):
                    claim(bank, n, t)
                    for s in range(NS):
                        i = nc.tensor.matmul(wb[bank][0:rows, s * width:(s + 1) * width], lhs[:, s * rows:(s + 1) * rows],
                                             w, start=True, stop=True)
                    i.then_inc(filled[n].sem, 1)

                def self_proj(t):
                    pe.wait_ge(ln_ok["1"].sem, ln_ok["1"].val(t))
                    transposes("x1T", t, 0, [xn["1"][:, s, :] for s in range(NS)], 128)
                    pe.wait_ge(drained["x1T"].sem, drained["x1T"].val(t))
                    product("q", t, 1, w_q[:], xnT["1"][:], T)
                    product("k", t, 0, w_k[:], xnT["1"][:], T)
                    by_token("v", t, 1, xnT["1"], w_v[:], D, S)

                def scores(n, t, qst, kst, cols, masked):
                    for u in range(2 * NS):
                        s, half = u // 2, u % 2
                        if u >= 2:
                            pe.wait_ge(max_ok[n].sem, max_ok[n].val(t, u - 1))
                        for j in range(4):
                            for g in range(2):
                                r = slice(64 * g, 64 * g + KS)
                                i = nc.tensor.matmul(sc[u % 2][:, g, j * cols:(j + 1) * cols],
                                                     qst[r, 4 * half + j, s * S:(s + 1) * S],
                                                     kst[r, 4 * half + j, s * cols:(s + 1) * cols],
                                                     start=(j == 0 or not masked), stop=not masked, skip_group_check=masked)
                        if masked:
                            for g in range(2):
                                i = nc.tensor.matmul(sc[u % 2][:, g, 0:4 * cols], identb[:],
                                                     mbias[:, s, :].unsqueeze(1).broadcast_to([128, 4, cols]),
                                                     start=False, stop=True, skip_group_check=True)
                        i.then_inc(max_f[n].sem, 1)

                def attend(n, t, qst, kst, va, cols, masked):
                    def shifted(u):
                        s, half = u // 2, u % 2
                        if u >= 2:
                            pe.wait_ge(exp_ok[n].sem, exp_ok[n].val(t, u - 1))
                        for j in range(4):
                            for g in range(2):
                                r = slice(64 * g, 64 * g + KM)
                                i = nc.tensor.matmul(sc[u % 2][0:cols, g, j * S:(j + 1) * S],
                                                     kst[r, 4 * half + j, s * cols:(s + 1) * cols],
                                                     qst[r, 4 * half + j, s * S:(s + 1) * S],
                                                     start=(j == 0 or not masked), stop=not masked, skip_group_check=masked)
                        if masked:
                            for g in range(2):
                                i = nc.tensor.matmul(sc[u % 2][0:cols, g, :], mbias[:, s, :],
                                                     identb[:].unsqueeze(1).broadcast_to([128, 4, S]),
                                                     start=False, stop=True, skip_group_check=True)
                        i.then_inc(st_f[n].sem, 1)

                    def values(u):
                        s, half = u // 2, u % 2
                        pe.wait_ge(exp_ok[n].sem, exp_ok[n].val(t, u + 1))
                        if s >= 2 and half == 0:
                            pe.wait_ge(oT_ok[n].sem, oT_ok[n].val(t, s - 1))
                        for g in range(2):
                            for c in range(4):
                                slot = 2 * half + g
                                i = nc.tensor.matmul(pv[s % 2][32 * c:32 * c + VW, slot * S:(slot + 1) * S],
                                                     va[:, s, HG * g + 4 * half + c, :],
                                                     probs[u % 2][0:cols, g, c * S:(c + 1) * S], start=True, stop=True)
                        i.then_inc(pv_ok[n].sem, 1)

                    shifted(0)
                    for u in range(1, 2 * NS):
                        shifted(u)
                        values(u - 1)
                    values(2 * NS - 1)

                def output(n, t, w):
                    for s in range(NS):
                        k = f"oTT_{n}"
                        claim(s % 2, k, t, s + 1)
                        pe.wait_ge(oT_ok[n].sem, oT_ok[n].val(t, s + 1))
                        for slot in range(4):
                            i = nc.tensor.transpose(wb[s % 2][:, slot * S:(slot + 1) * S],
                                                    oT[n][:, s, slot * S:(slot + 1) * S], ident[:])
                        i.then_inc(filled[k].sem, 1)
                    pe.wait_ge(drained[f"oTT_{n}"].sem, drained[f"oTT_{n}"].val(t))
                    transposes(f"onT_{n}", t, 0, [on[n][:, s].rearrange("p h i -> p (h i)") for s in range(NS)], 128)
                    pe.wait_ge(drained[f"onT_{n}"].sem, drained[f"onT_{n}"].val(t))
                    by_token(f"y_{n}", t, 1, onT[n], w[:], D, S)

                self_proj(0)
                pe.wait_ge(sim_ok.sem, 1)
                pe.wait_ge(drained["k"].sem, drained["k"].val(0))
                nc.tensor.transpose(wb[0][:, 0:E], sim_u[:], ident[0:E, 0:E]).then_inc(simT_f.sem, 1)
                pe.wait_ge(simT_ok.sem, 1)
                nc.tensor.matmul(wb[0][:, 0:E], wp_n[:], simT[:], start=True, stop=True).then_inc(wps_f.sem, 1)
                pe.wait_ge(wps_ok.sem, 1)
                pe.wait_ge(vones_ok.sem, 4)

                def body(t, cross, own, nxt):
                    if not isinstance(t, int) or t >= 2:
                        user[0], user[1] = ("combT", drained["combT"].val(t - 2)), ("pj1", drained["pj1"].val(t - 2))
                    if cross:
                        pe.wait_ge(ln_ok["2"].sem, ln_ok["2"].val(t - 1))
                        transposes("x2T", t - 1, 0, [xn["2"][:, s, :] for s in range(NS)], 128)
                        pe.wait_ge(drained["x2T"].sem, drained["x2T"].val(t - 1))
                        product("cq", t - 1, 1, cw_q[:], xnT["2"][:], T)
                    if own:
                        for n in ("q", "k"):
                            pe.wait_ge(stacked[n].sem, stacked[n].val(t))
                        scores("m", t, qs, ks, S, False)
                        pe.wait_ge(max_ok["m"].sem, max_ok["m"].val(t))
                        transposes("m", t, 0, [negm["m"][:, s].rearrange("p g j -> p (g j)") for s in range(NS)], H)
                    if cross:
                        for n in ("cq", "ck"):
                            pe.wait_ge(stacked[n].sem, stacked[n].val(t - 1))
                        pe.wait_ge(mb_ok.sem, mb_ok.val(t - 1))
                        scores("cm", t - 1, cqs, cks, SC, True)
                        pe.wait_ge(max_ok["cm"].sem, max_ok["cm"].val(t - 1))
                        transposes("cm", t - 1, 1, [negm["cm"][:, s].rearrange("p g j -> p (g j)") for s in range(NS)], H)
                    if own:
                        pe.wait_ge(drained["v"].sem, drained["v"].val(t))
                        pe.wait_ge(stacked["m"].sem, stacked["m"].val(t))
                        attend("s", t, qs, ks, vaug, S, False)
                        output("s", t, w_ff)
                    if nxt:
                        self_proj(t + 1)
                    if cross:
                        pe.wait_ge(drained["cv"].sem, drained["cv"].val(t - 1))
                        pe.wait_ge(stacked["cm"].sem, stacked["cm"].val(t - 1))
                        attend("c", t - 1, cqs, cks, cvaug, SC, True)
                        output("c", t - 1, cw_o)
                    if own:
                        pe.wait_ge(c_in.sem, c_in.val(t))
                        transposes("cT", t, 0, [cin[:, s, :] for s in range(NS)], 128)
                        pe.wait_ge(drained["cT"].sem, drained["cT"].val(t))
                        product("ck", t, 1, cw_k[:], cT[:], TC)
                        by_token("cv", t, 0, cT, cw_v[:], D, SC)
                    if cross:
                        pe.wait_ge(ln_ok["3"].sem, ln_ok["3"].val(t - 1))
                        transposes("x3T", t - 1, 1, [xn["3"][:, s, :] for s in range(NS)], 128)
                        pe.wait_ge(drained["x3T"].sem, drained["x3T"].val(t - 1))
                        for half in range(2):
                            n = f"pj{half}"
                            claim(half, n, t - 1)
                            for k in range(2):
                                s = 2 * half + k
                                i = nc.tensor.matmul(wb[half][:, (D + E) * k:(D + E) * (k + 1)], xnT["3"][:, s * S:(s + 1) * S],
                                                     wpx[:], start=True, stop=True)
                            i.then_inc(filled[n].sem, 1)
                        pe.wait_ge(comb_ok.sem, comb_ok.val(t - 1))
                        transposes("combT", t - 1, 0, [comb[:, s, :] for s in range(NS)], E)

                steps(Run(pe, body))

        phase_a.close()
        phase_b(nc, ctx, sb, sem, dict(x3_d=x3_d, xt_d=xt_d, comb_d=comb_d, W1=W1, W2=W2, out_v=out_v, b1_c=b1_c, b2_r=b2_r,
                                       ident=ident, h_banks=[sc[0][:, 0, :], sc[0][:, 1, :], sc[1][:, 0, :]], y_banks=pv,
                                       z_bank=wb[0], t_bank=wb[1]))


def phase_b(nc, ctx, sb, sem, a):
    ident, b1_c, b2_r = a["ident"], a["b1_c"], a["b2_r"]
    h_banks, y_banks, z_bank, t_bank = a["h_banks"], a["y_banks"], a["z_bank"], a["t_bank"]
    NU = E * FC
    LAG = 2
    NG = 3

    w1f, w2f = sb("w1f", [128, E, F]), sb("w2f", [128, E, FC, D])
    w1h, w1l = sb("w1h", [128, E, F], F32R), sb("w1l", [128, E, F], F32R)
    w2h, w2l = sb("w2h", [128, E, FC, D], F32R), sb("w2l", [128, E, FC, D], F32R)
    xf = sb("xf", [128, T])
    xh, xl = sb("xh", [128, T], F32R), sb("xl", [128, T], F32R)
    cb = sb("cb", [128, E, T])
    ct = sb("ct", [E, T])
    g = [sb(f"g{i}", [128, T]) for i in range(NG)]
    gh = [sb(f"gh{i}", [128, T], F32R) for i in range(NG)]
    gl = [sb(f"gl{i}", [128, T], F32R) for i in range(NG)]
    wy = [sb(f"wy{i}", [128, T]) for i in range(2)]
    acc = sb("acc", [128, T])
    xr, yo = sb("xr", [128, NS, D]), sb("yo", [128, NS, D])

    w_in, wh_ok, wl_ok = sem("w_in"), sem("wh_ok"), sem("wl_ok")
    xf_in, ct_in, xr_in = sem("xf_in", 16), sem("ct_in", 16), sem("xr_in", 16)
    cb_in = [sem(f"cb_in{e}", 16) for e in range(E)]
    xh_ok, xl_ok = sem("xh_ok"), sem("xl_ok")
    h_f = sem("h_f", NU)
    g_ok, gh_ok, gl_ok = sem("g_ok", NU), sem("gh_ok", NU), sem("gl_ok", NU)
    w2_done = sem("w2_done", NU)
    wy_ok, acc_ok = sem("wy_ok", E), sem("acc_ok", E + 1)
    z_f, t_f, yo_ok, out_st = sem("z_f"), sem("t_f"), sem("yo_ok"), sem("out_st", 16)

    def hi32(ap):
        return ap.bitcast(F32)

    def blocks(engine, body):
        body(0, False, True)
        body(1, True, True)
        with engine.Fori(2, NB - 1) as b:
            body(b, True, True)
        body(NB - 1, True, False)

    with nc.Block() as block:
        @block.sync
        def _(sp):
            sp.dma_start(w1f[:], a["W1"].rearrange("e d f -> d e f")).then_inc(w_in.sem, 16)
            sp.dma_start(w2f[:], a["W2"].rearrange("e (c f) d -> f e c d", f=128)).then_inc(w_in.sem, 16)
            sp.dma_start(xf[:], a["xt_d"][0]).then_inc(xf_in.sem, 16)
            sp.dma_start(ct[:], a["comb_d"][0]).then_inc(ct_in.sem, 16)
            for e in range(E):
                sp.dma_start(cb[:, e, :], a["comb_d"][0, e].unsqueeze(0).broadcast_to([128, T])).then_inc(cb_in[e].sem, 16)
            sp.dma_start(xr[:], a["x3_d"][0]).then_inc(xr_in.sem, 16)

            def store(b):
                sp.wait_ge(yo_ok.sem, yo_ok.val(b))
                sp.dma_start(a["out_v"][b], yo[:]).then_inc(out_st.sem, 16)

            def body(b, prev, nxt):
                if nxt:
                    sp.wait_ge(xl_ok.sem, xl_ok.val(b))
                    sp.dma_start(xf[:], a["xt_d"][b + 1]).then_inc(xf_in.sem, 16)
                if prev:
                    store(b - 1)
                    sp.dma_start(xr[:], a["x3_d"][b]).then_inc(xr_in.sem, 16)
                if nxt:
                    sp.wait_ge(z_f.sem, z_f.val(b))
                    sp.dma_start(ct[:], a["comb_d"][b + 1]).then_inc(ct_in.sem, 16)
                    for e in range(E):
                        sp.wait_ge(wy_ok.sem, wy_ok.val(b, e + 1))
                        sp.dma_start(cb[:, e, :], a["comb_d"][b + 1, e].unsqueeze(0).broadcast_to([128, T]))\
                            .then_inc(cb_in[e].sem, 16)

            blocks(sp, body)
            store(NB - 1)
            sp.wait_ge(out_st.sem, out_st.val(NB - 1))

        @block.scalar
        def _(act):
            act.wait_ge(w_in.sem, 32)
            for w, h in ((w1f, w1h), (w2f, w2h)):
                nc.scalar.activation(h[:], w[:], ACT.Copy).then_inc(wh_ok.sem, 1)

            def body(b, prev, nxt):
                for n in range(NU):
                    act.wait_ge(h_f.sem, h_f.val(b, n + 1))
                    if n >= NG:
                        act.wait_ge(gl_ok.sem, gl_ok.val(b, n - NG + 1))
                    elif prev:
                        act.wait_ge(gl_ok.sem, gl_ok.val(b - 1))
                    nc.scalar.activation(g[(n) % NG][:], h_banks[n % 3], ACT.Gelu,
                                         bias=b1_c[:, n // FC, n % FC:n % FC + 1]).then_inc(g_ok.sem, 1)
                    if n == 2:
                        act.wait_ge(z_f.sem, z_f.val(b))
                        if prev:
                            act.wait_ge(t_f.sem, t_f.val(b - 1))
                        nc.scalar.activation(acc[:], z_bank[:], ACT.Copy).then_inc(acc_ok.sem, 1)

            blocks(act, body)

        @block.gpsimd
        def _(pool):
            def body(b, prev, nxt):
                for e in range(E):
                    pool.wait_ge(wy_ok.sem, wy_ok.val(b, e + 1))
                    pool.wait_ge(acc_ok.sem, acc_ok.val(b, e + 1))
                    nc.gpsimd.tensor_tensor(out=acc[:], in0=acc[:], in1=wy[e % 2][:], op=ALU.add).then_inc(acc_ok.sem, 1)

            blocks(pool, body)

        @block.vector
        def _(dve):
            for k, (w, h, lo) in enumerate(((w1f, w1h, w1l), (w2f, w2h, w2l))):
                dve.wait_ge(wh_ok.sem, k + 1)
                nc.vector.tensor_tensor(out=lo[:], in0=w[:], in1=hi32(h[:]), op=ALU.subtract).then_inc(wl_ok.sem, 1)

            def split_x(b):
                dve.wait_ge(xf_in.sem, xf_in.val(b))
                nc.vector.tensor_copy(xh[:], xf[:]).then_inc(xh_ok.sem, 1)
                dve.wait_ge(xh_ok.sem, xh_ok.val(b))
                nc.vector.tensor_tensor(out=xl[:], in0=xf[:], in1=hi32(xh[:]), op=ALU.subtract).then_inc(xl_ok.sem, 1)

            def result(b):
                dve.wait_ge(t_f.sem, t_f.val(b))
                dve.wait_ge(xr_in.sem, xr_in.val(b))
                if not isinstance(b, int) or b > 0:
                    dve.wait_ge(out_st.sem, out_st.val(b - 1))
                nc.vector.tensor_tensor(out=yo[:], in0=t_bank[:].rearrange("p (s d) -> p s d", s=NS), in1=xr[:],
                                        op=ALU.add).then_inc(yo_ok.sem, 1)

            split_x(0)

            def weigh(b, e):
                dve.wait_ge(w2_done.sem, w2_done.val(b, FC * (e + 1)))
                dve.wait_ge(cb_in[e].sem, cb_in[e].val(b))
                if e >= 2:
                    dve.wait_ge(acc_ok.sem, acc_ok.val(b, e))
                nc.vector.tensor_tensor(out=wy[e % 2][:], in0=y_banks[e % 2][:], in1=cb[:, e, :], op=ALU.mult)\
                    .then_inc(wy_ok.sem, 1)

            def body(b, prev, nxt):
                for n in range(NU):
                    if n >= NG:
                        dve.wait_ge(w2_done.sem, w2_done.val(b, n - NG + 1))
                    elif prev:
                        dve.wait_ge(w2_done.sem, w2_done.val(b - 1))
                    dve.wait_ge(g_ok.sem, g_ok.val(b, n + 1))
                    nc.vector.tensor_copy(gh[n % NG][:], g[n % NG][:]).then_inc(gh_ok.sem, 1)
                    dve.wait_ge(gh_ok.sem, gh_ok.val(b, n + 1))
                    nc.vector.tensor_tensor(out=gl[n % NG][:], in0=g[n % NG][:], in1=hi32(gh[n % NG][:]), op=ALU.subtract)\
                        .then_inc(gl_ok.sem, 1)
                    if n == 2 and prev:
                        result(b - 1)
                    if n >= FC and n % FC == LAG:
                        weigh(b, n // FC - 1)
                if nxt:
                    dve.wait_ge(h_f.sem, h_f.val(b))
                    split_x(b + 1)
                weigh(b, E - 1)

            blocks(dve, body)
            result(NB - 1)

        @block.tensor
        def _(pe):
            pe.wait_ge(wl_ok.sem, 2)

            def up(b, n):
                e, c = n // FC, n % FC
                if n >= 3:
                    pe.wait_ge(g_ok.sem, g_ok.val(b, n - 2))
                elif not isinstance(b, int) or b > 0:
                    pe.wait_ge(g_ok.sem, g_ok.val(b - 1))
                w = slice(c * 128, (c + 1) * 128)
                o = h_banks[n % 3]
                nc.tensor.matmul(o, w1h[:, e, w], xh[:], start=True, stop=False)
                nc.tensor.matmul(o, w1h[:, e, w], xl[:], start=False, stop=False)
                nc.tensor.matmul(o, w1l[:, e, w], xh[:], start=False, stop=True).then_inc(h_f.sem, 1)

            def down(b, n):
                e, c = n // FC, n % FC
                o = y_banks[e % 2][:]
                if c == 0:
                    if e >= 2:
                        pe.wait_ge(wy_ok.sem, wy_ok.val(b, e - 1))
                    elif not isinstance(b, int) or b > 0:
                        pe.wait_ge(wy_ok.sem, wy_ok.val(b - 1))
                pe.wait_ge(gl_ok.sem, gl_ok.val(b, n + 1))
                nc.tensor.matmul(o, w2h[:, e, c, :], gh[n % NG][:], start=(c == 0), stop=False)
                nc.tensor.matmul(o, w2h[:, e, c, :], gl[n % NG][:], start=False, stop=False)
                i = nc.tensor.matmul(o, w2l[:, e, c, :], gh[n % NG][:], start=False, stop=(c == FC - 1))
                i.then_inc(w2_done.sem, 1)

            def back(b):
                pe.wait_ge(acc_ok.sem, acc_ok.val(b))
                if not isinstance(b, int) or b > 0:
                    pe.wait_ge(yo_ok.sem, yo_ok.val(b - 1))
                for s in range(NS):
                    i = nc.tensor.transpose(t_bank[:, s * S:(s + 1) * S], acc[:, s * S:(s + 1) * S], ident[:])
                i.then_inc(t_f.sem, 1)

            def body(b, prev, nxt):
                pe.wait_ge(ct_in.sem, ct_in.val(b))
                if prev:
                    pe.wait_ge(acc_ok.sem, acc_ok.val(b - 1, 1))
                nc.tensor.matmul(z_bank[:], b2_r[:], ct[:], start=True, stop=True).then_inc(z_f.sem, 1)
                pe.wait_ge(xl_ok.sem, xl_ok.val(b))
                for n in range(NU + LAG):
                    if n < NU:
                        up(b, n)
                    if n == 1 and prev:
                        back(b - 1)
                    if n >= LAG:
                        down(b, n - LAG)

            blocks(pe, body)
            back(NB - 1)


_OUT = ("out_dram", (B, S, D))


def kernel(x, ctx_1024, mask_BxSxS2_if1, L0_attn_Wq, L0_attn_Wk, L0_attn_Wv, L0_attn_Wff, L0_attn_bff, L0_xattn_Wq,
           L0_xattn_bq, L0_xattn_Wk, L0_xattn_bk, L0_xattn_Wv, L0_xattn_bv, L0_xattn_Wo, L0_xattn_bo, L0_ffn_Wp,
           L0_ffn_sim_matrix, L0_ffn_temperature, L0_ffn_W1, L0_ffn_b1, L0_ffn_W2, L0_ffn_b2):
    import numpy as np
    import concourse.bacc as bacc
    from concourse.bass_utils import run_bass_kernel_spmd

    by_place = np.array([h * DH + i for i in range(DH) for h in range(H)])
    by_slot = np.array([(HG * g + 4 * u + c) * DH + i for u in range(2) for g in range(2) for c in range(4)
                        for i in range(DH)])
    a = np.asarray
    arrays = {
        "x": a(x), "ctx": a(ctx_1024), "mask": a(mask_BxSxS2_if1),
        "Wq": a(L0_attn_Wq).T[:, by_place], "Wk": a(L0_attn_Wk).T[:, by_place], "Wv": a(L0_attn_Wv).T,
        "Wff": a(L0_attn_Wff).T[by_slot], "bff": a(L0_attn_bff),
        "xWq": a(L0_xattn_Wq).T[:, by_place], "xbq": a(L0_xattn_bq)[by_place],
        "xWk": a(L0_xattn_Wk).T[:, by_place], "xbk": a(L0_xattn_bk)[by_place],
        "xWv": a(L0_xattn_Wv).T, "xbv": a(L0_xattn_bv), "xWo": a(L0_xattn_Wo).T[by_slot], "xbo": a(L0_xattn_bo),
        "Wp": a(L0_ffn_Wp), "WpT": a(L0_ffn_Wp).T, "sim": a(L0_ffn_sim_matrix),
        "temp": a(L0_ffn_temperature).reshape(1),
        "W1": a(L0_ffn_W1), "b1": a(L0_ffn_b1).reshape(E, FC, 128).transpose(2, 0, 1), "W2": a(L0_ffn_W2), "b2": a(L0_ffn_b2),
    }
    nc = bacc.Bacc("TRN2", target_bir_lowering=False, num_devices=1)
    fed, args = {}, []
    for name, value in arrays.items():
        value = np.ascontiguousarray(value)
        fed[f"{name}_dram"] = value
        args.append(nc.dram_tensor(f"{name}_dram", value.shape, mybir.dt.from_np(value.dtype), kind="ExternalInput").ap())
    out = nc.dram_tensor(_OUT[0], _OUT[1], F32, kind="ExternalOutput").ap()
    program(nc, *args, out)
    result = run_bass_kernel_spmd(nc, [fed], core_ids=[0])
    return result.results[0][_OUT[0]]
```

```python
import concourse.bass as bass
from concourse import mybir
from contextlib import ExitStack

F32 = mybir.dt.float32
F32R = mybir.dt.float32r
BF16 = mybir.dt.bfloat16
I32 = mybir.dt.int32
U32 = mybir.dt.uint32
ALU = mybir.AluOpType
ACT = mybir.ActivationFunctionType
AX = mybir.AxisListType

B, S, D = 64, 128, 128
SC = 77
H, DH = 16, 8
E, F = 8, 512
NS = 4
NB = B // NS
T = NS * S
TC = NS * SC
FC = F // 128
NPAIR = 6
KS = NPAIR * DH
NG = 2
HG = H // NG
KR = NG * KS
KM = KR + NG * 3
MASKED = -(2.0 ** 100)
LN_EPS = 1e-5
TS = 512
TQ = TS // 128
REGION = B * S
NT = 2 * B * S // TS + E - 1
SLOTS = E * REGION + (NT + 1) * TS
ROUTE = 17
L2_EPS2 = 1e-24
UNITS = 4 * NS
LEAD = 1
STEPS = UNITS + LEAD + 2
BANK = {"q": 0, "k": 0, "cq": 1, "ck": 1, "m": 0, "cm": 0}
VW = 32


class Steps:

    def __init__(self, sem, per, base=0):
        self.sem, self.per, self.base = sem, per, base

    def val(self, block, k=None):
        return block * self.per + (self.base + (self.per if k is None else k))


def program(nc, x, ctx_in, mask, Wq, Wk, Wv, Wff, bff, xWq, xbq, xWk, xbk, xWv, xbv, xWo, xbo,
            Wp, WpT, sim, temp, W1, b1, W2, b2, out):
    ctx = ExitStack()
    with ctx:
        def sb(name, shape, dt=F32):
            return ctx.enter_context(nc.sbuf_tensor(name, shape, dt))

        def pb(name, shape):
            return ctx.enter_context(nc.psum_tensor(name, shape, F32))

        def sem(name, per=1):
            return Steps(ctx.enter_context(nc.semaphore(name)), per)

        def dram(name, shape, dt=F32):
            return nc.dram_tensor(name, shape, dt, kind="Internal").ap()

        x_v = x.rearrange("(n s) p d -> n p s d", s=NS)
        ctx_v = ctx_in.rearrange("(n s) p d -> n p s d", s=NS)
        mask_v = mask.rearrange("(n s) p k -> n p s k", s=NS)
        out_v = out.rearrange("(n s) p d -> n p s d", s=NS)
        stk = {"q": dram("stk_q", [NPAIR, D, T], BF16), "k": dram("stk_k", [NPAIR, D, T], BF16),
               "cq": dram("stk_cq", [NPAIR, D, T], BF16), "ck": dram("stk_ck", [NPAIR, D, TC], BF16)}
        mscr = {"m": dram("mscr", [3, H, T], BF16), "cm": dram("cmscr", [3, H, T], BF16)}
        x3_d = dram("x3_d", [NB, 128, NS, D])
        xn_d = dram("xn_d", [B * S, D])
        xn_v = xn_d.rearrange("(n s p) d -> n p s d", s=NS, p=S)
        slot_d = dram("slot_d", [SLOTS, 1], I32)
        y_d = dram("y_d", [NT, 128, TQ, D])

        ident = sb("ident", [128, 128])
        identb = sb("identb", [128, 128], BF16)
        mhalf = sb("mhalf", [128, NS])
        iota8 = sb("iota8", [128, E])
        w_q, w_k, w_v, w_ff = (sb(n, [128, 128]) for n in ("w_q", "w_k", "w_v", "w_ff"))
        cw_q, cw_k, cw_v, cw_o = (sb(n, [128, 128]) for n in ("cw_q", "cw_k", "cw_v", "cw_o"))
        bff_b, bo_b = sb("bff_b", [128, D]), sb("bo_b", [128, D])
        bv_b = sb("bv_b", [SC, D])
        bq_c, bk_c = sb("bq_c", [128, 1]), sb("bk_c", [128, 1])
        wp_n = sb("wp_n", [128, 128])
        wpx = sb("wpx", [128, D + E])
        sim_n, sim_u, sim_j = sb("sim_n", [E, D]), sb("sim_u", [E, D]), sb("sim_j", [E, D])
        sim_sq_sum, sim_ss, sim_rn = sb("sim_sq_sum", [E, 1]), sb("sim_ss", [E, 1]), sb("sim_rn", [E, 1])
        simT = sb("simT", [128, E])
        temp_b, itemp = sb("temp_b", [128, 1]), sb("itemp", [128, 1])
        tri, ones = sb("tri", [128, 128], BF16), sb("ones", [128, 128], BF16)
        base = sb("base", [128, E])
        slot_all = sb("slot_all", [128, NB, NS, 2])
        prob_all = sb("prob_all", [128, NB, 2, NS])
        row_all = sb("row_all", [128, NB * NS * 2], I32)
        tab = sb("tab", [128, 2, NT], I32)

        phase_a = ctx.enter_context(ExitStack())

        def sa(name, shape, dt=F32):
            return phase_a.enter_context(nc.sbuf_tensor(name, shape, dt))

        def pair(name, shape, dt=F32):
            return [sa(f"{name}{i}", shape, dt) for i in range(2)]

        xin, xagain = sa("xin", [128, NS, D]), sa("xagain", [128, NS, D])
        cin = sa("cin", [SC, NS, D])
        mk = sa("mk", [128, NS, SC], I32)
        mbias = pair("mbias", [128, NS, SC], BF16)
        xres, x2, x3 = (sa(n, [128, NS, D]) for n in ("xres", "x2", "x3"))
        x2res = pair("x2res", [128, NS, D])
        xn = {n: sa(f"xn_{n}", [128, NS, D]) for n in ("1", "2", "3")}
        xnT = {n: sa(f"xnT_{n}", [128, T]) for n in ("1", "2", "3")}
        cT = sa("cT", [128, TC])
        lnst = {n: sa(f"lnst_{n}", [128, NS, 6]) for n in ("1", "2", "3")}
        lnmv = {n: sa(f"lnmv_{n}", [128, NS, 2]) for n in ("1", "2", "3")}
        lnve = {n: sa(f"lnve_{n}", [128, NS]) for n in ("1", "2", "3")}
        lnrs = {n: sa(f"lnrs_{n}", [128, NS]) for n in ("1", "2", "3")}
        lnnm = {n: sa(f"lnnm_{n}", [128, NS]) for n in ("1", "2", "3")}
        parts = {n: sa(f"parts_{n}", [128, 3, T], BF16) for n in ("q", "k", "cq")}
        parts["ck"] = sa("parts_ck", [128, 3, TC], BF16)
        parts["m"] = parts["cm"] = sa("parts_m", [H, 3, T], BF16)
        rest = {n: sa(f"rest_{n}", [128, T]) for n in ("q", "k", "cq")}
        rest["ck"] = sa("rest_ck", [128, TC])
        rest["m"] = rest["cm"] = sa("rest_m", [H, T])
        qs, cqs = pair("qs", [KM, HG, T], BF16), pair("cqs", [KM, HG, T], BF16)
        ks, cks = pair("ks", [KM, H, T], BF16), pair("cks", [KM, H, TC], BF16)
        vaug = pair("vaug", [128, NS, H, VW])
        cvaug = pair("cvaug", [128, NS, H, VW])
        negm = {n: sa(f"negm_{n}", [128, NS, 2, HG]) for n in ("m", "cm")}
        probs = [sa(f"probs{i}", [128, T]) for i in range(3)]
        oT = dict.fromkeys("sc", sa("oT", [128, NS, T]))
        rden = {n: sa(f"rden_{n}", [128, NS, H]) for n in ("s", "c")}
        on = dict.fromkeys("sc", sa("on", [128, NS, H, DH]))
        onT = dict.fromkeys("sc", sa("onT", [128, T]))
        sq_junk = sa("sq_junk", [128, NS, D])
        ss, ssc, rn = sa("ss", [128, NS]), sa("ssc", [128, NS]), sa("rn", [128, NS])
        graw, gs = sa("graw", [128, NS, E]), sa("gs", [128, NS, E])
        top_v = sa("top_v", [128, NS, 8])
        top_i = sa("top_i", [128, NS, 8], U32)
        top_f = sa("top_f", [128, NS, 2])
        dv, ev, den = (sa(n, [128, NS]) for n in ("dv", "ev", "den"))
        eq1, eq2, pos = (sa(n, [128, NS, E]) for n in ("eq1", "eq2", "pos"))
        here = [sa(f"here{k}", [128, NS, E]) for k in range(2)]
        chosen = sa("chosen", [128, NS, E], BF16)
        before = sa("before", [128, NS + 1, E], BF16)
        slot_f, slot_i = sa("slot_f", [128, NS, 2]), sa("slot_i", [128, NS * 2], I32)
        tok = sa("tok", [128, NS], I32)
        pr = sa("pr", [128, 2, NS])

        sc_m = [pb(f"sc_m{i}", [128, 512]) for i in range(2)]
        sc_a = [pb(f"sc_a{i}", [128, 512]) for i in range(2)]
        pv = [pb(f"pv{i}", [128, 512]) for i in range(2)]
        wb = [pb(f"wb{i}", [128, 512]) for i in range(2)]

        const_in = sem("const_in")
        ident_ok = sem("ident_ok")
        preset = [sem(f"preset{i}") for i in range(2)]
        gate_set, gate_mm, gate_ev = sem("gate_set"), sem("gate_mm"), sem("gate_ev")
        xa_in = sem("xa_in", 16)
        x_in, c_in, mk_in = sem("x_in", 16), sem("c_in", 16), sem("mk_in", 16)
        mb_ok = sem("mb_ok")
        xres_ok, x2res_ok = sem("xres_ok"), sem("x2res_ok")
        ln_st = {n: sem(f"ln{n}_st", 3) for n in "123"}
        ln_ve = {n: sem(f"ln{n}_ve") for n in "123"}
        ln_rs = {n: sem(f"ln{n}_rs") for n in "123"}
        ln_ok = {n: sem(f"ln{n}_ok", NS) for n in "123"}
        ONE = ("x1T", "x2T", "x3T", "cT", "q", "k", "v", "cq", "ck", "cv", "m", "cm", "onT_s", "onT_c",
               "y_s", "y_c", "pj0", "pj1", "rank")
        filled = {n: sem(f"{n}_filled") for n in ONE}
        drained = {n: sem(f"{n}_drained") for n in ONE}
        for n in ("s", "c"):
            filled[f"oTT_{n}"] = sem(f"oTT_{n}_filled", NS)
            drained[f"oTT_{n}"] = sem(f"oTT_{n}_drained", NS)
        part1 = {n: sem(f"{n}_part1") for n in ("q", "k", "cq", "ck", "m", "cm")}
        part2 = {n: sem(f"{n}_part2") for n in part1}
        part3 = {n: sem(f"{n}_part3") for n in part1}
        dumped = {n: sem(f"{n}_dumped", 48) for n in ("q", "k", "cq", "ck")}
        dumped["m"], dumped["cm"] = sem("m_dumped", 16), sem("cm_dumped", 16)
        stacked = {n: sem(f"{n}_stacked", 16 if n in ("q", "cq") else 32) for n in part1}
        max_f = {n: sem(f"{n}_sc_filled", UNITS) for n in ("m", "cm")}
        max_ok = {n: sem(f"{n}_max_ok", UNITS) for n in ("m", "cm")}
        st_f = {n: sem(f"st_{n}_filled", UNITS) for n in ("s", "c")}
        exp_ok = {n: sem(f"exp_{n}_ok", UNITS) for n in ("s", "c")}
        pv_ok = {n: sem(f"pv_{n}_ok", UNITS) for n in ("s", "c")}
        oT_ok = {n: sem(f"oT_{n}_ok", NS) for n in ("s", "c")}
        rden_ok = {n: sem(f"rden_{n}_ok", NS) for n in ("s", "c")}
        ss_ok = sem("ss_ok", 2)
        ssc_ok, rn_ok, gs_ok, dv_ok, ev_ok, slot_ok, tok_ok = (
            sem(n) for n in ("ssc_ok", "rn_ok", "gs_ok", "dv_ok", "ev_ok", "slot_ok", "tok_ok"))
        gate_step = sem("gate_step", ROUTE)
        listed = Steps(sem("listed").sem, 16 * 2 * NS, 16 * 2 * NS)
        x3_st, xn_st = sem("x3_st", 16), sem("xn_st", 16)
        tab_ok, table_step, iotas = sem("tab_ok"), sem("table_step"), sem("iotas")

        CONSTS = [(w_q, Wq), (w_k, Wk), (w_v, Wv), (w_ff, Wff), (cw_q, xWq), (cw_k, xWk), (cw_v, xWv), (cw_o, xWo),
                  (bff_b, bff.unsqueeze(0).broadcast_to([128, D])), (bo_b, xbo.unsqueeze(0).broadcast_to([128, D])),
                  (bv_b, xbv.unsqueeze(0).broadcast_to([SC, D])),
                  (bq_c, xbq.unsqueeze(1)), (bk_c, xbk.unsqueeze(1)), (wp_n, Wp), (wpx[:, 0:D], WpT), (sim_n, sim),
                  (temp_b, temp.unsqueeze(0).broadcast_to([128, 1]))]

        def on_(b):
            return not isinstance(b, int) or 0 <= b < NB

        def steps(engine, body):
            for t in range(-3, 4):
                body(t, t % 2)
            with engine.Fori(4, NB - 4, 2) as t:
                body(t, 0)
                body(again(engine, t, 1), 1)
            for t in range(NB - 4, NB + 4):
                body(t, t % 2)

        def again(engine, t, ahead=0):
            if isinstance(t, int):
                return t + ahead
            copy = engine.alloc_register()
            engine.reg_add(copy, t, ahead)
            return engine.snap(copy, min_val=t.min_val + ahead, max_val=t.max_val + ahead)

        def wait_block(engine, s, b, k=None):
            if on_(b):
                engine.wait_ge(s.sem, s.val(b, k))

        def zero_stacks(engine, op, i):
            done = preset[i].sem
            for tile in (ks[i], cks[i]):
                op.memset(tile[:].bitcast(F32), 0.0).then_inc(done, 1)
            engine.wait_ge(done, 2)
            for tile in (ks[i], cks[i]):
                op.memset(tile[KR:KR + 3, 0:HG, :], 1.0).then_inc(done, 1)
                op.memset(tile[KR:KM, HG:H, :], 1.0).then_inc(done, 1)
            engine.wait_ge(done, 6)
            for tile in (ks[i], cks[i]):
                op.memset(tile[KR:KR + 3, HG:H, :], 0.0).then_inc(done, 1)
            engine.wait_ge(done, 8)

        with nc.Block() as block:
            @block.sync
            def _(sp):
                for dst, src in CONSTS:
                    sp.dma_start(dst[:, :, :] if len(dst.shape) == 3 else dst[:, :], src).then_inc(const_in.sem, 16)
                for s_ in preset:
                    sp.wait_ge(s_.sem, 8)

                def dump(n, b):
                    sp.wait_ge(part3[n].sem, part3[n].val(b))
                    scr, p = stk[n], parts[n]
                    cols = p.shape[2]
                    if n in ("q", "cq"):
                        runs = [(0, 3, p[:, 0:1, :].broadcast_to([128, 3, cols])),
                                (3, 5, p[:, 1:2, :].broadcast_to([128, 2, cols])), (5, 6, p[:, 2:3, :])]
                    else:
                        runs = [(0, 3, p[:, 0:3, :]), (3, 5, p[:, 0:2, :]), (5, 6, p[:, 0:1, :])]
                    for lo, hi, src in runs:
                        sp.dma_start(scr[lo:hi].rearrange("c r t -> r c t"), src).then_inc(dumped[n].sem, 16)

                def stack(n, b, dst):
                    sp.wait_ge(dumped[n].sem, dumped[n].val(b))
                    if n in ("q", "cq"):
                        view = stk[n].rearrange("c (i g j) t -> (c i g) j t", i=DH, g=NG)
                        sp.dma_start(dst[0:KR, :, :], view).then_inc(stacked[n].sem, 16)
                    else:
                        view = stk[n].rearrange("c (i g j) t -> g (c i) j t", i=DH, g=NG)
                        for g in range(NG):
                            sp.dma_start(dst[g:KR:NG, g * HG:(g + 1) * HG, :], view[g]).then_inc(stacked[n].sem, 16)

                def fold(n, b, dst):
                    sp.wait_ge(part3[n].sem, part3[n].val(b))
                    sp.dma_start(mscr[n].rearrange("c h t -> h c t"), parts[n][:]).then_inc(dumped[n].sem, 16)
                    sp.wait_ge(dumped[n].sem, dumped[n].val(b))
                    view = mscr[n].rearrange("c (g j) t -> g c j t", g=NG)
                    for g in range(NG):
                        sp.dma_start(dst[KR + 3 * g:KR + 3 * g + 3, :, :], view[g]).then_inc(stacked[n].sem, 16)

                def body(t, par):
                    if on_(t):
                        wait_block(sp, filled["cT"], t - 1)
                        sp.dma_start(cin[:], ctx_v[t]).then_inc(c_in.sem, 16)
                        wait_block(sp, mb_ok, t - 1)
                        sp.dma_start(mk[:], mask_v[t]).then_inc(mk_in.sem, 16)
                        wait_block(sp, xres_ok, t - 1)
                        sp.dma_start(xagain[:], x_v[t]).then_inc(xa_in.sem, 16)
                    if on_(t - 1):
                        for n, dst in (("cq", cqs), ("ck", cks)):
                            wait_block(sp, st_f["c"], t - 3)
                            stack(n, t - 1, dst[1 - par])
                    if on_(t - 2):
                        fold("cm", t - 2, cqs[par])
                    if on_(t - 3):
                        sp.wait_ge(drained["y_c"].sem, drained["y_c"].val(t - 3))
                        sp.dma_start(x3_d[t - 3], x3[:]).then_inc(x3_st.sem, 16)
                    if on_(t + 2):
                        dump("q", t + 2)
                        dump("k", t + 2)
                    if on_(t):
                        wait_block(sp, stacked["ck"], t - 1)
                        sp.nop(nofuse=True)
                        dump("ck", t)
                    if on_(t - 3):
                        sp.wait_ge(ln_ok["3"].sem, ln_ok["3"].val(t - 3))
                        sp.dma_start(xn_v[t - 3], xn["3"][:]).then_inc(xn_st.sem, 16)
                    if on_(t + 3):
                        wait_block(sp, ln_ok["1"], t + 2)
                        sp.dma_start(xin[:], x_v[t + 3]).then_inc(x_in.sem, 16)
                    if on_(t + 2):
                        for n, dst in (("q", qs), ("k", ks)):
                            wait_block(sp, st_f["s"], t)
                            stack(n, t + 2, dst[par])
                    if on_(t + 1):
                        fold("m", t + 1, qs[1 - par])
                    if on_(t):
                        dump("cq", t)

                steps(sp, body)
                for s_ in (x3_st, xn_st):
                    sp.wait_ge(s_.sem, s_.val(NB - 1))

            @block.gpsimd
            def _(pool):
                nc.gpsimd.memset(ident[:], 0.0).then_inc(ident_ok.sem, 1)
                nc.gpsimd.memset(identb[:], 0.0).then_inc(ident_ok.sem, 1)
                nc.gpsimd.memset(ones[:], 1.0).then_inc(ident_ok.sem, 1)
                nc.gpsimd.memset(sq_junk[:], 0.0).then_inc(ident_ok.sem, 1)
                nc.gpsimd.memset(mhalf[:], -0.5).then_inc(ident_ok.sem, 1)
                pool.wait_ge(ident_ok.sem, 5)
                for m in (ident, identb):
                    nc.gpsimd.affine_select(out=m[:], in_=m[:], compare_op=ALU.not_equal, fill=1.0, base=0,
                                            pattern=[[-1, 128]], channel_multiplier=1).then_inc(ident_ok.sem, 1)
                nc.gpsimd.affine_select(out=tri[:], in_=ones[:], compare_op=ALU.is_gt, fill=0.0, base=0,
                                        pattern=[[1, 128]], channel_multiplier=-1).then_inc(ident_ok.sem, 1)
                nc.gpsimd.iota(base[:], pattern=[[REGION, E]], base=0, channel_multiplier=0,
                               allow_small_or_imprecise_dtypes=True).then_inc(iotas.sem, 1)
                nc.gpsimd.iota(tok[:], pattern=[[S, NS]], base=-T, channel_multiplier=1).then_inc(iotas.sem, 1)
                piece = SLOTS // (2 * NS)
                for k in range(2 * NS):
                    pool.dma_start(slot_d[k * piece:(k + 1) * piece].rearrange("(p c) o -> p (c o)", p=128),
                                   sq_junk[:, 0, 0:piece // 128].bitcast(I32)).then_inc(listed.sem, 16)
                zero_stacks(pool, nc.gpsimd, 1)
                for tile in vaug:
                    nc.gpsimd.memset(tile[:], 0.0).then_inc(preset[1].sem, 1)
                pool.wait_ge(preset[1].sem, 10)
                for tile in vaug:
                    nc.gpsimd.memset(tile[:, :, :, DH:DH + 1], 1.0).then_inc(preset[1].sem, 1)
                pool.wait_ge(const_in.sem, 16 * len(CONSTS))

                def power(n, b):
                    pool.wait_ge(ln_ve[n].sem, ln_ve[n].val(b))
                    nc.gpsimd.tensor_tensor(out=lnrs[n][:], in0=lnve[n][:], in1=mhalf[:], op=ALU.pow)\
                        .then_inc(ln_rs[n].sem, 1)

                def residual(dst, src, bias, done):
                    nc.gpsimd.tensor_tensor(out=dst[:], in0=src[:], in1=bias[:].unsqueeze(1).broadcast_to([128, NS, D]),
                                            op=ALU.add).then_inc(done.sem, 1)

                def third(n, b):
                    pool.wait_ge(part2[n].sem, part2[n].val(b))
                    nc.gpsimd.tensor_tensor(out=parts[n][:, 2, :], in0=rest[n][:], in1=parts[n][:, 1, :],
                                            op=ALU.subtract).then_inc(part3[n].sem, 1)

                pool.wait_ge(gate_set.sem, 5)
                nc.gpsimd.tensor_tensor(out=sim_rn[:], in0=sim_ss[:], in1=mhalf[0:E, 0:1], op=ALU.pow)\
                    .then_inc(iotas.sem, 1)

                def enlist(b):
                    pool.wait_ge(listed.sem, listed.val(b - 1))
                    pool.nop(nofuse=True)
                    nc.gpsimd.tensor_scalar(out=tok[:], in0=tok[:], scalar1=float(T), scalar2=None, op0=ALU.add)\
                        .then_inc(tok_ok.sem, 1)
                    pool.wait_ge(slot_ok.sem, slot_ok.val(b))
                    pool.wait_ge(tok_ok.sem, tok_ok.val(b))
                    pool.nop(nofuse=True)
                    for c in range(2 * NS):
                        nc.gpsimd.indirect_dma_start(out=slot_d, in_=tok[:, c // 2:c // 2 + 1], in_offset=None,
                                                     out_offset=bass.IndirectOffsetOnAxis(ap=slot_i[:, c:c + 1], axis=0))\
                            .then_inc(listed.sem, 16)

                def body(t, par):
                    if on_(t):
                        wait_block(pool, drained["y_s"], t - 1)
                        pool.wait_ge(xa_in.sem, xa_in.val(t))
                        residual(xres, xagain, bff_b, xres_ok)
                    if on_(t - 2):
                        third("cm", t - 2)
                    if on_(t - 1):
                        wait_block(pool, drained["y_c"], t - 3)
                        pool.wait_ge(drained["y_s"].sem, drained["y_s"].val(t - 1))
                        residual(x2res[1 - par], x2, bo_b, x2res_ok)
                    if on_(t + 2):
                        third("q", t + 2)
                    if on_(t - 3):
                        power("3", t - 3)
                    if on_(t + 2):
                        third("k", t + 2)
                    if on_(t):
                        third("ck", t)
                    if on_(t - 4):
                        enlist(t - 4)
                    if on_(t + 1):
                        third("m", t + 1)
                    if on_(t):
                        power("2", t)
                    if on_(t + 3):
                        power("1", t + 3)
                    if on_(t - 3):
                        pool.wait_ge(ssc_ok.sem, ssc_ok.val(t - 3))
                        nc.gpsimd.tensor_tensor(out=rn[:], in0=ssc[:], in1=mhalf[:], op=ALU.pow).then_inc(rn_ok.sem, 1)
                    if on_(t):
                        third("cq", t)
                        wait_block(pool, st_f["c"], t - 2)
                        pool.wait_ge(mk_in.sem, mk_in.val(t))
                        pool.nop(nofuse=True)
                        nc.gpsimd.tensor_scalar(out=mbias[par][:], in0=mk[:], scalar1=0.0, scalar2=MASKED,
                                                op0=ALU.is_equal, op1=ALU.mult).then_inc(mb_ok.sem, 1)

                steps(pool, body)
                pool.wait_ge(listed.sem, listed.val(NB - 1))

            @block.scalar
            def _(act):
                act.wait_ge(const_in.sem, 16 * len(CONSTS))
                act.wait_ge(listed.sem, listed.val(-1))

                def evac(dst, n, b, bank, cols=T, rows=128):
                    act.wait_ge(filled[n].sem, filled[n].val(b))
                    nc.scalar.activation(dst, wb[bank][0:rows, 0:cols], ACT.Copy).then_inc(drained[n].sem, 1)

                def first(n, b, bias=None):
                    p = parts[n]
                    act.wait_ge(filled[n].sem, filled[n].val(b))
                    src = wb[BANK[n]][0:p.shape[0], 0:p.shape[2]]
                    if bias is None:
                        i = nc.scalar.activation(p[:, 0, :], src, ACT.Copy)
                    else:
                        i = nc.scalar.activation(p[:, 0, :], src, ACT.Identity, bias=bias[:, 0:1])
                    i.then_inc(part1[n].sem, 1)

                def second(n, b):
                    act.wait_ge(drained[n].sem, drained[n].val(b))
                    nc.scalar.activation(parts[n][:, 1, :], rest[n][:], ACT.Copy).then_inc(part2[n].sem, 1)

                def normalise(n, b, src, s):
                    if s == 0:
                        act.wait_ge(ln_st[n].sem, ln_st[n].val(b))
                    nc.scalar.activation(xn[n][:, s, :], src[:, s, :], ACT.Identity, bias=lnnm[n][:, s:s + 1],
                                         scale=lnrs[n][:, s:s + 1]).then_inc(ln_ok[n].sem, 1)

                def attend(n, b, rows, scale, between):
                    for u in range(STEPS):
                        e = u - LEAD
                        if on_(b) and 0 <= e < UNITS:
                            act.wait_ge(st_f[n].sem, st_f[n].val(b, e + 1))
                            if e >= 3:
                                act.wait_ge(pv_ok[n].sem, pv_ok[n].val(b, e - 2))
                            nc.scalar.activation(probs[e % 3][0:rows], sc_a[e % 2][0:rows], ACT.Exp, scale=scale)\
                                .then_inc(exp_ok[n].sem, 1)
                            if e % 4 == 2 and e > 4:
                                out_T(n, b, e // 4 - 1)
                        between(u)
                    if on_(b):
                        out_T(n, b, NS - 1)

                def out_T(n, b, s):
                    act.wait_ge(pv_ok[n].sem, pv_ok[n].val(b, 4 * s + 4))
                    nc.scalar.activation(oT[n][:, s, :], pv[s % 2][:], ACT.Copy).then_inc(oT_ok[n].sem, 1)

                act.wait_ge(gate_mm.sem, 1)
                nc.scalar.activation(simT[:], wb[0][:, 0:E], ACT.Copy).then_inc(gate_ev.sem, 1)
                act.wait_ge(gate_mm.sem, 2)
                nc.scalar.activation(wpx[:, D:D + E], wb[0][:, 0:E], ACT.Copy).then_inc(gate_ev.sem, 1)

                def body(t, par):
                    def in_x(u):
                        if 2 <= u < 2 + NS and on_(t + 2):
                            normalise("1", t + 2, xin, u - 2)
                        if u == 5 and on_(t - 3):
                            evac(onT["c"][:], "onT_c", t - 3, 1)
                        if u == 6 and on_(t - 2):
                            first("cm", t - 2)
                        if u == 8 and on_(t - 2):
                            second("cm", t - 2)
                        if u == 8 and on_(t + 2):
                            evac(xnT["1"][:], "x1T", t + 2, 0)
                        if u == 9 and on_(t):
                            evac(cT[:], "cT", t, 1, TC)
                        if u == 10 and on_(t + 2):
                            first("q", t + 2)
                        if u == 11 and on_(t):
                            wait_block(act, dumped["ck"], t - 1)
                            first("ck", t, bk_c)
                        if u == 12 and on_(t + 2):
                            second("q", t + 2)
                        if u == 13 and on_(t + 2):
                            first("k", t + 2)
                        if u == 13 and on_(t):
                            second("ck", t)
                        if 14 <= u < 14 + NS and on_(t - 3):
                            if u == 14:
                                wait_block(act, xn_st, t - 4)
                            normalise("3", t - 3, x3, u - 14)
                        if u == 15 and on_(t + 2):
                            second("k", t + 2)

                    def in_y(u):
                        if u == 4 and on_(t + 2):
                            act.wait_ge(filled["v"].sem, filled["v"].val(t + 2))
                            nc.scalar.activation(vaug[par][:, :, :, 0:DH], wb[0][:].rearrange("p (s h i) -> p s h i", s=NS, h=H),
                                                 ACT.Copy).then_inc(drained["v"].sem, 1)
                        if u == 5 and on_(t):
                            evac(onT["s"][:], "onT_s", t, 1)
                        if u == 6 and on_(t + 1):
                            first("m", t + 1)
                        if u == 8 and on_(t + 1):
                            second("m", t + 1)
                        if u == 8 and on_(t - 3):
                            evac(xnT["3"][:], "x3T", t - 3, 0)
                        if u in (10, 11) and on_(t - 3):
                            half = u - 10
                            n = f"pj{half}"
                            act.wait_ge(filled[n].sem, filled[n].val(t - 3))
                            for k in range(2):
                                s, a = 2 * half + k, (D + E) * k
                                i = nc.scalar.activation(sq_junk[:, s, :], wb[half][:, a:a + D], ACT.Square,
                                                         accum_out=ss[:, s:s + 1])
                            i.then_inc(ss_ok.sem, 1)
                            raw = wb[half][:, 0:2 * (D + E)].rearrange("p (k c) -> p k c", k=2)[:, :, D:D + E]
                            nc.scalar.activation(graw[:, 2 * half:2 * half + 2, :], raw, ACT.Copy)\
                                .then_inc(drained[n].sem, 1)
                        if 11 <= u < 11 + NS and on_(t):
                            normalise("2", t, x2, u - 11)
                        if u == 15 and on_(t):
                            evac(xnT["2"][:], "x2T", t, 0)
                        if u == 17 and on_(t):
                            first("cq", t, bq_c)

                    attend("s", t, 128, float(D) ** -0.5, in_x)
                    t = again(act, t)
                    attend("c", t - 2, SC, float(DH) ** -0.5, in_y)
                    if on_(t):
                        second("cq", t)
                    if on_(t - 3):
                        act.wait_ge(dv_ok.sem, dv_ok.val(t - 3))
                        nc.scalar.activation(ev[:], dv[:], ACT.Exp).then_inc(ev_ok.sem, 1)

                steps(act, body)

            @block.vector
            def _(dve):
                zero_stacks(dve, nc.vector, 0)
                for tile in cvaug:
                    nc.vector.memset(tile[:], 0.0).then_inc(preset[0].sem, 1)
                dve.wait_ge(preset[0].sem, 10)
                for tile in cvaug:
                    nc.vector.memset(tile[0:SC, :, :, DH:DH + 1], 1.0).then_inc(preset[0].sem, 1)
                nc.vector.memset(before[:, 0, :], 0.0).then_inc(gate_set.sem, 1)
                for e in range(E):
                    i = nc.vector.memset(iota8[:, e:e + 1], float(e))
                i.then_inc(gate_set.sem, 1)
                dve.wait_ge(const_in.sem, 16 * len(CONSTS))
                nc.vector.reciprocal(itemp[:], temp_b[:]).then_inc(gate_set.sem, 1)
                dve.wait_ge(gate_set.sem, 3)

                def stats(n, b, src):
                    for s in range(NS):
                        i = nc.vector.bn_stats(lnst[n][:, s, :], src[:, s, :])
                    i.then_inc(ln_st[n].sem, 1)
                    dve.wait_ge(ln_st[n].sem, ln_st[n].val(b, 1))
                    dve.nop(nofuse=True)
                    for s in range(NS):
                        i = nc.vector.bn_aggr(lnmv[n][:, s, :], lnst[n][:, s, :])
                    i.then_inc(ln_st[n].sem, 1)
                    dve.wait_ge(ln_st[n].sem, ln_st[n].val(b, 2))
                    nc.vector.tensor_scalar(lnve[n][:], lnmv[n][:, :, 1], LN_EPS, None, ALU.add).then_inc(ln_ve[n].sem, 1)

                def shift(n, b):
                    dve.wait_ge(ln_rs[n].sem, ln_rs[n].val(b))
                    nc.vector.scalar_tensor_tensor(out=lnnm[n][:], in0=lnmv[n][:, :, 0], scalar=-1.0, in1=lnrs[n][:],
                                                   op0=ALU.mult, op1=ALU.mult).then_inc(ln_st[n].sem, 1)

                def remainder(n, b, bias=None):
                    p, r = parts[n], rest[n]
                    dve.wait_ge(part1[n].sem, part1[n].val(b))
                    src = wb[BANK[n]][0:p.shape[0], 0:p.shape[2]]
                    if bias is None:
                        i = nc.vector.tensor_tensor(out=r[:], in0=src, in1=p[:, 0, :], op=ALU.subtract)
                    else:
                        i = nc.vector.scalar_tensor_tensor(out=r[:], in0=src, scalar=bias[:, 0:1], in1=p[:, 0, :],
                                                           op0=ALU.add, op1=ALU.subtract)
                    i.then_inc(drained[n].sem, 1)

                def maxima(n, b, cols, between):
                    for u in range(STEPS):
                        if on_(b) and u < UNITS:
                            s, half, g = u // 4, u // 2 % 2, u % 2
                            dve.wait_ge(max_f[n].sem, max_f[n].val(b, u + 1))
                            nc.vector.tensor_reduce(out=negm[n][:, s, g, 4 * half:4 * half + 4],
                                                    in_=sc_m[u % 2][:, 0:4 * cols].rearrange("p (j k) -> p j k", j=4),
                                                    op=ALU.max, axis=AX.X, negate=True).then_inc(max_ok[n].sem, 1)
                        between(u)

                def divide(n, b, s):
                    k = f"oTT_{n}"
                    dve.wait_ge(filled[k].sem, filled[k].val(b, s + 1))
                    v = wb[s % 2][:].rearrange("p (h w) -> p h w", w=VW)
                    nc.vector.reciprocal(rden[n][:, s, :], v[:, :, DH]).then_inc(rden_ok[n].sem, 1)
                    dve.wait_ge(rden_ok[n].sem, rden_ok[n].val(b, s + 1))
                    nc.vector.tensor_tensor(out=on[n][:, s], in0=v[:, :, 0:DH],
                                            in1=rden[n][:, s, :].unsqueeze(2).broadcast_to([128, H, DH]),
                                            op=ALU.mult).then_inc(drained[k].sem, 1)

                def add_residual(n, b, res, dst):
                    k = f"y_{n}"
                    dve.wait_ge(filled[k].sem, filled[k].val(b))
                    rsem = xres_ok if n == "s" else x2res_ok
                    dve.wait_ge(rsem.sem, rsem.val(b))
                    nc.vector.tensor_tensor(out=dst[:], in0=wb[1][:].rearrange("p (s d) -> p s d", s=NS), in1=res[:],
                                            op=ALU.add).then_inc(drained[k].sem, 1)
                    dve.wait_ge(drained[k].sem, drained[k].val(b))

                def choose(b):
                    dve.wait_ge(drained["pj1"].sem, drained["pj1"].val(b))
                    dve.wait_ge(rn_ok.sem, rn_ok.val(b))
                    for s in range(NS):
                        i = nc.vector.tensor_scalar(gs[:, s, :], graw[:, s, :], rn[:, s:s + 1], itemp[:, 0:1],
                                                    ALU.mult, ALU.mult)
                    i.then_inc(gs_ok.sem, 1)
                    dve.wait_ge(gs_ok.sem, gs_ok.val(b))
                    dve.nop(nofuse=True)
                    for s in range(NS):
                        i = nc.vector.max(top_v[:, s, :], gs[:, s, :])
                    i.then_inc(gate_step.sem, 1)
                    dve.wait_ge(gate_step.sem, gate_step.val(b, 1))
                    dve.nop(nofuse=True)
                    for s in range(NS):
                        i = nc.vector.max_index(top_i[:, s, :], top_v[:, s, :], gs[:, s, :])
                    i.then_inc(gate_step.sem, 1)
                    nc.vector.tensor_tensor(out=dv[:], in0=top_v[:, :, 1], in1=top_v[:, :, 0], op=ALU.subtract)\
                        .then_inc(dv_ok.sem, 1)
                    dve.wait_ge(gate_step.sem, gate_step.val(b, 2))
                    nc.vector.tensor_copy(top_f[:], top_i[:, :, 0:2]).then_inc(gate_step.sem, 1)
                    dve.wait_ge(gate_step.sem, gate_step.val(b, 3))
                    for eq, k in ((eq1, 0), (eq2, 1)):
                        i = nc.vector.tensor_tensor(out=eq[:], in0=iota8[:].unsqueeze(1).broadcast_to([128, NS, E]),
                                                    in1=top_f[:, :, k:k + 1].broadcast_to([128, NS, E]), op=ALU.is_equal)
                    i.then_inc(gate_step.sem, 1)
                    dve.wait_ge(gate_step.sem, gate_step.val(b, 4))
                    nc.vector.tensor_tensor(out=chosen[:], in0=eq1[:], in1=eq2[:], op=ALU.add).then_inc(gate_step.sem, 1)
                    for s in range(NS):
                        dve.wait_ge(gate_step.sem, gate_step.val(b, 5 + s))
                        nc.vector.tensor_tensor(out=before[:, s + 1, :], in0=before[:, s, :], in1=chosen[:, s, :],
                                                op=ALU.add).then_inc(gate_step.sem, 1)

                def weigh(b):
                    dve.wait_ge(ev_ok.sem, ev_ok.val(b))
                    nc.vector.tensor_scalar(den[:], ev[:], 1.0, None, ALU.add).then_inc(gate_step.sem, 1)
                    dve.wait_ge(gate_step.sem, gate_step.val(b, 10))
                    nc.vector.reciprocal(pr[:, 0, :], den[:]).then_inc(gate_step.sem, 1)
                    dve.wait_ge(gate_step.sem, gate_step.val(b, 11))
                    nc.vector.tensor_tensor(out=pr[:, 1, :], in0=ev[:], in1=pr[:, 0, :], op=ALU.mult)\
                        .then_inc(gate_step.sem, 1)
                    dve.wait_ge(gate_step.sem, gate_step.val(b, 12))
                    nc.vector.tensor_scalar(prob_all[:, b], pr[:], 1.0, None, ALU.mult).then_inc(gate_step.sem, 1)

                def route(b):
                    dve.wait_ge(filled["rank"].sem, filled["rank"].val(b))
                    rank = wb[0][:, 0:NS * E].rearrange("p (s e) -> p s e", s=NS)
                    nc.vector.tensor_tensor(out=pos[:], in0=rank, in1=base[:].unsqueeze(1).broadcast_to([128, NS, E]),
                                            op=ALU.add).then_inc(gate_step.sem, 1)
                    dve.wait_ge(gate_step.sem, gate_step.val(b, 14))
                    nc.vector.tensor_tensor(out=base[:], in0=base[:], in1=wb[0][:, NS * E:(NS + 1) * E], op=ALU.add)\
                        .then_inc(drained["rank"].sem, 1)
                    for eq, h in ((eq1, here[0]), (eq2, here[1])):
                        i = nc.vector.tensor_tensor(out=h[:], in0=eq[:], in1=pos[:], op=ALU.mult)
                    i.then_inc(gate_step.sem, 1)
                    dve.wait_ge(gate_step.sem, gate_step.val(b, 15))
                    for k in range(2):
                        i = nc.vector.tensor_reduce(out=slot_f[:, :, k], in_=here[k][:], op=ALU.add, axis=AX.X)
                    i.then_inc(gate_step.sem, 1)
                    dve.wait_ge(gate_step.sem, gate_step.val(b, 16))
                    nc.vector.tensor_scalar(slot_all[:, b], slot_f[:], 1.0, None, ALU.mult).then_inc(gate_step.sem, 1)
                    dve.wait_ge(listed.sem, listed.val(b - 1))
                    nc.vector.tensor_copy(slot_i[:], slot_f[:].rearrange("p s k -> p (s k)")).then_inc(slot_ok.sem, 1)

                nc.vector.tensor_tensor_reduce(out=sim_j[:], in0=sim_n[:], in1=sim_n[:], scale=1.0, scalar=0.0,
                                               op0=ALU.mult, op1=ALU.add, accum_out=sim_sq_sum[:]).then_inc(gate_set.sem, 1)
                dve.wait_ge(gate_set.sem, 4)
                nc.vector.tensor_scalar(sim_ss[:], sim_sq_sum[:], L2_EPS2, None, ALU.max).then_inc(gate_set.sem, 1)
                dve.wait_ge(iotas.sem, 3)
                nc.vector.tensor_scalar(sim_u[:], sim_n[:], sim_rn[:, 0:1], None, ALU.mult).then_inc(gate_set.sem, 1)

                def body(t, par):
                    def in_x(u):
                        if u == 0 and on_(t + 2):
                            shift("1", t + 2)
                        if 1 <= u < 1 + NS and on_(t - 3):
                            divide("c", t - 3, u - 1)
                        if u == 5 and on_(t - 1):
                            dve.wait_ge(filled["cv"].sem, filled["cv"].val(t - 1))
                            nc.vector.tensor_tensor(
                                out=cvaug[1 - par][0:SC, :, :, 0:DH],
                                in0=wb[0][0:SC, :].rearrange("p (s h i) -> p s h i", s=NS, h=H),
                                in1=bv_b[:].rearrange("p (h i) -> p h i", h=H).unsqueeze(1).broadcast_to([SC, NS, H, DH]),
                                op=ALU.add).then_inc(drained["cv"].sem, 1)
                        if u == 7 and on_(t - 2):
                            remainder("cm", t - 2)
                        if u == 8 and on_(t - 3):
                            wait_block(dve, x3_st, t - 4)
                            add_residual("c", t - 3, x2res[1 - par], x3)
                        if u == 9 and on_(t - 3):
                            stats("3", t - 3, x3)
                        if u == 10 and on_(t - 4):
                            weigh(t - 4)
                        if u == 11 and on_(t + 2):
                            remainder("q", t + 2)
                        if u == 12 and on_(t):
                            remainder("ck", t, bk_c)
                        if u == 13 and on_(t - 3):
                            shift("3", t - 3)
                        if u == 14 and on_(t + 2):
                            remainder("k", t + 2)
                        if u == 16 and on_(t - 4):
                            route(t - 4)

                    def in_y(u):
                        if 1 <= u < 1 + NS and on_(t):
                            divide("s", t, u - 1)
                        if u == 7 and on_(t + 1):
                            remainder("m", t + 1)
                        if u == 8 and on_(t):
                            wait_block(dve, x2res_ok, t - 1)
                            add_residual("s", t, xres, x2)
                            stats("2", t, x2)
                        if u == 10 and on_(t):
                            shift("2", t)
                        if u == 11 and on_(t + 3):
                            dve.wait_ge(x_in.sem, x_in.val(t + 3))
                            stats("1", t + 3, xin)
                        if u == 13 and on_(t - 3):
                            dve.wait_ge(ss_ok.sem, ss_ok.val(t - 3))
                            nc.vector.tensor_scalar(ssc[:], ss[:], L2_EPS2, None, ALU.max).then_inc(ssc_ok.sem, 1)
                        if u == 16 and on_(t - 3):
                            choose(t - 3)
                        if u == 18 and on_(t):
                            remainder("cq", t, bq_c)

                    maxima("m", t + 1, S, in_x)
                    t = again(dve, t)
                    maxima("cm", t - 1, SC, in_y)

                dve.wait_ge(iotas.sem, 2)
                steps(dve, body)

            @block.tensor
            def _(pe):
                pe.wait_ge(const_in.sem, 16 * len(CONSTS))
                pe.wait_ge(ident_ok.sem, 8)
                user = [None, None]

                def claim(bank, n, b, k=None):
                    if user[bank] is not None:
                        last, value = user[bank]
                        pe.wait_ge(drained[last].sem, value)
                    user[bank] = (n, drained[n].val(b, k))

                def transposes(n, b, bank, pieces, rows):
                    claim(bank, n, b)
                    for j, src in enumerate(pieces):
                        w = src.shape[0]
                        i = nc.tensor.transpose(wb[bank][0:rows, j * w:(j + 1) * w], src, ident[0:w, 0:w])
                    i.then_inc(filled[n].sem, 1)

                def product(n, b, lhsT, rhs, cols):
                    claim(BANK[n], n, b)
                    nc.tensor.matmul(wb[BANK[n]][:, 0:cols], lhsT, rhs, start=True, stop=True).then_inc(filled[n].sem, 1)

                def by_token(n, b, bank, lhs, w, width, rows):
                    claim(bank, n, b)
                    for s in range(NS):
                        i = nc.tensor.matmul(wb[bank][0:rows, s * width:(s + 1) * width], lhs[:, s * rows:(s + 1) * rows],
                                             w, start=True, stop=True)
                    i.then_inc(filled[n].sem, 1)

                def scores(n, b, u, qst, kst, cols, bias):
                    s, half, g = u // 4, u // 2 % 2, u % 2
                    if u >= 2:
                        pe.wait_ge(max_ok[n].sem, max_ok[n].val(b, u - 1))
                    for j in range(4):
                        i = nc.tensor.matmul(sc_m[u % 2][:, j * cols:(j + 1) * cols],
                                             qst[0:KR, 4 * half + j, s * S:(s + 1) * S],
                                             kst[0:KR, HG * g + 4 * half + j, s * cols:(s + 1) * cols],
                                             start=(j == 0 or not bias), stop=not bias, skip_group_check=bool(bias))
                    if bias:
                        i = nc.tensor.matmul(sc_m[u % 2][:, 0:4 * cols], identb[:],
                                             bias[:, s, :].unsqueeze(1).broadcast_to([128, 4, cols]),
                                             start=False, stop=True, skip_group_check=True)
                    i.then_inc(max_f[n].sem, 1)

                def shifted(n, b, u, qst, kst, cols, bias):
                    s, half, g = u // 4, u // 2 % 2, u % 2
                    if u >= 2:
                        pe.wait_ge(exp_ok[n].sem, exp_ok[n].val(b, u - 1))
                    for j in range(4):
                        i = nc.tensor.matmul(sc_a[u % 2][0:cols, j * S:(j + 1) * S],
                                             kst[:, HG * g + 4 * half + j, s * cols:(s + 1) * cols],
                                             qst[:, 4 * half + j, s * S:(s + 1) * S],
                                             start=(j == 0 or not bias), stop=not bias, skip_group_check=bool(bias))
                    if bias:
                        i = nc.tensor.matmul(sc_a[u % 2][0:cols, :], bias[:, s, :],
                                             identb[:].unsqueeze(1).broadcast_to([128, 4, S]),
                                             start=False, stop=True, skip_group_check=True)
                    i.then_inc(st_f[n].sem, 1)

                def values(n, b, u, va, last):
                    s, half, g = u // 4, u // 2 % 2, u % 2
                    pe.wait_ge(exp_ok[n].sem, exp_ok[n].val(b, u + 1))
                    if u % 4 == 0 and s >= 2:
                        pe.wait_ge(oT_ok[n].sem, oT_ok[n].val(b, s - 1))
                    elif u % 4 == 0:
                        wait_block(pe, oT_ok[last[0]], last[1], s + 3)
                    for c in range(4):
                        i = nc.tensor.matmul(pv[s % 2][32 * c:32 * c + VW, (u % 4) * S:(u % 4 + 1) * S],
                                             va[:, s, HG * g + 4 * half + c, :],
                                             probs[u % 3][:, c * S:(c + 1) * S], start=True, stop=True)
                    i.then_inc(pv_ok[n].sem, 1)

                def beside(attn, maxi, between):
                    for u in range(STEPS):
                        if maxi and u < UNITS:
                            scores(maxi[0], maxi[1], u, *maxi[2:])
                        if attn:
                            n, b, qst, kst, va, cols, bias, last = attn
                            if LEAD <= u < UNITS + LEAD:
                                shifted(n, b, u - LEAD, qst, kst, cols, bias)
                            if u >= LEAD + 2:
                                values(n, b, u - LEAD - 2, va, last)
                        between(u)

                def maxima_T(n, b):
                    pe.wait_ge(max_ok[n].sem, max_ok[n].val(b))
                    transposes(n, b, BANK[n], [negm[n][:, s].rearrange("p g j -> p (g j)") for s in range(NS)], H)

                def outputs_T(n, b, s):
                    k = f"oTT_{n}"
                    claim(s % 2, k, b, s + 1)
                    pe.wait_ge(oT_ok[n].sem, oT_ok[n].val(b, s + 1))
                    for slot in range(4):
                        i = nc.tensor.transpose(wb[s % 2][:, slot * S:(slot + 1) * S],
                                                oT[n][:, s, slot * S:(slot + 1) * S], ident[:])
                    i.then_inc(filled[k].sem, 1)

                def divided_T(n, b):
                    pe.wait_ge(drained[f"oTT_{n}"].sem, drained[f"oTT_{n}"].val(b))
                    transposes(f"onT_{n}", b, 1, [on[n][:, s].rearrange("p h i -> p (h i)") for s in range(NS)], 128)

                def project(n, b, w):
                    pe.wait_ge(drained[f"onT_{n}"].sem, drained[f"onT_{n}"].val(b))
                    by_token(f"y_{n}", b, 1, onT[n], w[:], D, S)

                pe.wait_ge(gate_set.sem, 6)
                nc.tensor.transpose(wb[0][:, 0:E], sim_u[:], ident[0:E, 0:E]).then_inc(gate_mm.sem, 1)
                pe.wait_ge(gate_ev.sem, 1)
                nc.tensor.matmul(wb[0][:, 0:E], wp_n[:], simT[:], start=True, stop=True).then_inc(gate_mm.sem, 1)
                pe.wait_ge(gate_ev.sem, 2)
                for s_ in preset:
                    pe.wait_ge(s_.sem, 12)

                def body(t, par):
                    if on_(t - 1):
                        user[0], user[1] = ("x2T", drained["x2T"].val(t - 1)), ("cq", drained["cq"].val(t - 1))

                    def in_x(u):
                        if u == 4 and on_(t - 1):
                            by_token("cv", t - 1, 0, cT, cw_v[:], D, SC)
                        if u == 6 and on_(t - 2):
                            maxima_T("cm", t - 2)
                        if u < NS and on_(t - 3):
                            outputs_T("c", t - 3, u)
                        if u == 5 and on_(t - 3):
                            divided_T("c", t - 3)
                        if u == 8 and on_(t + 2):
                            pe.wait_ge(ln_ok["1"].sem, ln_ok["1"].val(t + 2))
                            transposes("x1T", t + 2, 0, [xn["1"][:, s, :] for s in range(NS)], 128)
                        if u == 7 and on_(t - 3):
                            project("c", t - 3, cw_o)
                        if u == 10 and on_(t + 2):
                            pe.wait_ge(drained["x1T"].sem, drained["x1T"].val(t + 2))
                            product("q", t + 2, w_q[:], xnT["1"][:], T)
                        if u == 9 and on_(t):
                            pe.wait_ge(c_in.sem, c_in.val(t))
                            transposes("cT", t, 1, [cin[:, s, :] for s in range(NS)], 128)
                        if u == 13 and on_(t + 2):
                            product("k", t + 2, w_k[:], xnT["1"][:], T)
                        if u == 11 and on_(t):
                            pe.wait_ge(drained["cT"].sem, drained["cT"].val(t))
                            product("ck", t, cw_k[:], cT[:], TC)
                        if u == 15 and on_(t - 4):
                            claim(0, "rank", t - 4)
                            pe.wait_ge(gate_step.sem, gate_step.val(t - 4, 9))
                            nc.tensor.matmul(wb[0][:, 0:NS * E], tri[:], chosen[:].rearrange("p s e -> p (s e)"),
                                             start=True, stop=False, skip_group_check=True)
                            nc.tensor.matmul(wb[0][:, 0:NS * E], ones[:], before[:, 0:NS, :].rearrange("p s e -> p (s e)"),
                                             start=False, stop=True, skip_group_check=True)
                            nc.tensor.matmul(wb[0][:, NS * E:(NS + 1) * E], ones[:], before[:, NS, :], start=True, stop=True,
                                             skip_group_check=True).then_inc(filled["rank"].sem, 1)

                    def in_y(u):
                        if u == 6 and on_(t + 1):
                            maxima_T("m", t + 1)
                        if u < NS and on_(t):
                            outputs_T("s", t, u)
                        if u == 4 and on_(t + 2):
                            by_token("v", t + 2, 0, xnT["1"], w_v[:], D, S)
                        if u == 5 and on_(t):
                            divided_T("s", t)
                        if u == 8 and on_(t - 3):
                            pe.wait_ge(ln_ok["3"].sem, ln_ok["3"].val(t - 3))
                            transposes("x3T", t - 3, 0, [xn["3"][:, s, :] for s in range(NS)], 128)
                        if u == 7 and on_(t):
                            project("s", t, w_ff)
                        if u in (10, 11) and on_(t - 3):
                            half = u - 10
                            n = f"pj{half}"
                            pe.wait_ge(drained["x3T"].sem, drained["x3T"].val(t - 3))
                            claim(half, n, t - 3)
                            for k in range(2):
                                s = 2 * half + k
                                i = nc.tensor.matmul(wb[half][:, (D + E) * k:(D + E) * (k + 1)], xnT["3"][:, s * S:(s + 1) * S],
                                                     wpx[:], start=True, stop=True)
                            i.then_inc(filled[n].sem, 1)
                        if u == 15 and on_(t):
                            pe.wait_ge(ln_ok["2"].sem, ln_ok["2"].val(t))
                            transposes("x2T", t, 0, [xn["2"][:, s, :] for s in range(NS)], 128)
                        if u == 17 and on_(t):
                            pe.wait_ge(drained["x2T"].sem, drained["x2T"].val(t))
                            product("cq", t, cw_q[:], xnT["2"][:], T)

                    attn = maxi = None
                    wait_block(pe, max_ok["cm"], t - 2)
                    if on_(t):
                        pe.wait_ge(drained["v"].sem, drained["v"].val(t))
                        pe.wait_ge(stacked["m"].sem, stacked["m"].val(t))
                        attn = ("s", t, qs[par], ks[par], vaug[par], S, None, ("c", t - 3))
                    if on_(t + 1):
                        for n in ("q", "k"):
                            pe.wait_ge(stacked[n].sem, stacked[n].val(t + 1))
                        maxi = ("m", t + 1, qs[1 - par], ks[1 - par], S, None)
                    beside(attn, maxi, in_x)
                    t = again(pe, t)
                    attn = maxi = None
                    wait_block(pe, max_ok["m"], t + 1)
                    if on_(t - 2):
                        pe.wait_ge(drained["cv"].sem, drained["cv"].val(t - 2))
                        pe.wait_ge(stacked["cm"].sem, stacked["cm"].val(t - 2))
                        attn = ("c", t - 2, cqs[par], cks[par], cvaug[par], SC, mbias[par], ("s", t))
                    if on_(t - 1):
                        for n in ("cq", "ck"):
                            pe.wait_ge(stacked[n].sem, stacked[n].val(t - 1))
                        pe.wait_ge(mb_ok.sem, mb_ok.val(t - 1))
                        maxi = ("cm", t - 1, cqs[1 - par], cks[1 - par], SC, mbias[1 - par])
                    beside(attn, maxi, in_y)

                steps(pe, body)

        phase_a.close()
        counts = phase_b(nc, ctx, sb, sem, dict(ident=ident, tab=tab, tab_ok=tab_ok, base=base, table_step=table_step, iotas=iotas,
                                       iotas_before=3, slot_all=slot_all, row_all=row_all, slot_d=slot_d, x_d=xn_d, y_d=y_d,
                                       W1=W1, W2=W2, b1=b1, b2=b2, h_banks=[sc_m[0][:], sc_m[1][:], sc_a[0][:], sc_a[1][:]],
                                       y_banks=pv, x_bank=wb[0], t_bank=wb[1]))
        phase_c(nc, ctx, sb, sem, dict(counts, x3_d=x3_d, out_v=out_v, prob_all=prob_all, row_all=row_all,
                                       y_rows=y_d.rearrange("n p c d -> (n p c) d")))


def phase_b(nc, ctx, sb, sem, a):
    ident, tab, tab_ok, base = a["ident"], a["tab"], a["tab_ok"], a["base"]
    h_banks, y_banks, x_bank, t_bank = a["h_banks"], a["y_banks"], a["x_bank"], a["t_bank"]
    slot_d, x_d, y_d, b1, b2 = a["slot_d"], a["x_d"], a["y_d"], a["b1"], a["b2"]
    phase = ctx.enter_context(ExitStack())

    def sa(name, shape, dt=F32):
        return phase.enter_context(nc.sbuf_tensor(name, shape, dt))

    wf = sa("wf", [128, E, 2, F])
    wh, wl = ([sa(f"{n}{i}", [128, F], F32R) for i in range(2)] for n in ("wh", "wl"))
    w2 = [sa(f"w2_{i}", [128, F]) for i in range(2)]
    ids = [sa(f"ids{i}", [128, TQ], I32) for i in range(2)]
    xg = [sa(f"xg{i}", [128, TQ, D]) for i in range(2)]
    bias = [sa(f"bias{i}", [128, FC + 1]) for i in range(2)]
    xh, xl = ([sa(f"{n}{i}", [128, TS], F32R) for i in range(2)] for n in ("xh", "xl"))
    g = [sa(f"g{c}", [128, TS]) for c in range(FC)]
    yT = sa("yT", [128, TS])
    yo = [sa(f"yo{i}", [128, TQ, D]) for i in range(2)]
    cnt, tls, ends, rest_rows = (sa(n, [128, E]) for n in ("cnt", "tls", "ends", "rest_rows"))
    iota_r, iota_k, iota_t = sa("iota_r", [128, E]), sa("iota_k", [128, S * B // TS]), sa("iota_t", [128, NT])
    more = sa("more", [128, E, S * B // TS])
    past, skip = sa("past", [128, NT]), sa("skip", [128, NT])
    tab_f = sa("tab_f", [128, 2, NT])
    past_r, row_f = sa("past_r", [128, NB * NS * 2]), sa("row_f", [128, NB * NS * 2])

    w_in, wh_ok, wl_ok = sem("w_in", 16), sem("wh_ok"), sem("wl_ok", 2)
    ids_in, xg_in, y_st = ([sem(f"{n}{i}", per) for i in range(2)] for n, per in (("ids_in", 16), ("xg_in", 64), ("y_st", 16)))
    bias_in = [sem(f"bias_in{i}", 32) for i in range(2)]
    xT_f, xh_ok, xl_ok = sem("xT_f"), sem("xh_ok"), sem("xl_ok")
    h_f, g_ok, w2_done = (sem(n, FC) for n in ("h_f", "g_ok", "w2_done"))
    yT_ok, back_f, yo_ok = sem("yT_ok"), sem("back_f"), sem("yo_ok")

    def hi32(ap):
        return ap.bitcast(F32)

    def tiles(engine, body):
        body(0, 0)
        body(0, 1)
        with engine.Fori(1, NT // 2) as j:
            body(j, 0)
            body(j, 1)
        body(NT // 2, 0)

    def ago(j, par, n):
        back = n // 2 + (1 if par < n % 2 else 0)
        return None if isinstance(j, int) and 2 * j + par < n else (j - back, (par - n) % 2)

    with nc.Block() as block:
        @block.sync
        def _(sp):
            sp.dma_start(wf[:, :, 0, :], a["W1"].rearrange("e d f -> d e f")).then_inc(w_in.sem, 16)
            for e in range(E):
                sp.dma_start(wf[:, e, 1, :].rearrange("p (c d) -> p c d", c=FC), a["W2"][e].rearrange("(c f) d -> f c d", f=128))\
                    .then_inc(w_in.sem, 16)
            sp.wait_ge(tab_ok.sem, 1)

            def body(j, par):
                i = 2 * j + par
                two = ago(j, par, 2)
                if two:
                    sp.wait_ge(xg_in[par].sem, xg_in[par].val(two[0]))
                start = sp.value_load(tab[0:1, 1, bass.ds(i, 1)], min_val=0, max_val=SLOTS - TS)
                sp.dma_start(ids[par][:], slot_d[bass.ds(start, TS)].rearrange("(p c) o -> p (c o)", c=TQ))\
                    .then_inc(ids_in[par].sem, 16)
                if not isinstance(i, int) or i >= 1:
                    biases(*ago(j, par, 1))

            def biases(j, par):
                i = 2 * j + par
                if ago(j, par, 2):
                    sp.wait_ge(yT_ok.sem, yT_ok.val(i - 2))
                e = sp.value_load(tab[0:1, 0, bass.ds(i, 1)], min_val=0, max_val=E - 1)
                sp.dma_start(bias[par][:, 0:FC], b1[e]).then_inc(bias_in[par].sem, 16)
                sp.dma_start(bias[par][:, FC:FC + 1], b2[e].unsqueeze(1)).then_inc(bias_in[par].sem, 16)

            tiles(sp, body)
            biases(NT // 2, 0)

        @block.gpsimd
        def _(pool):
            nc.gpsimd.iota(iota_r[:], pattern=[[REGION, E]], base=0, channel_multiplier=0,
                           allow_small_or_imprecise_dtypes=True).then_inc(a["iotas"].sem, 1)
            nc.gpsimd.iota(iota_k[:], pattern=[[TS, S * B // TS]], base=0, channel_multiplier=0,
                           allow_small_or_imprecise_dtypes=True).then_inc(a["iotas"].sem, 1)
            nc.gpsimd.iota(iota_t[:], pattern=[[1, NT]], base=0, channel_multiplier=0,
                           allow_small_or_imprecise_dtypes=True).then_inc(a["iotas"].sem, 1)

            def body(j, par):
                two = ago(j, par, 2)
                if two:
                    pool.wait_ge(xT_f.sem, xT_f.val(2 * j + par - 2))
                pool.wait_ge(ids_in[par].sem, ids_in[par].val(j))
                pool.nop(nofuse=True)
                for c in range(TQ):
                    nc.gpsimd.indirect_dma_start(out=xg[par][:, c, :], out_offset=None, in_=x_d,
                                                 in_offset=bass.IndirectOffsetOnAxis(ap=ids[par][:, c:c + 1], axis=0))\
                        .then_inc(xg_in[par].sem, 16)

            tiles(pool, body)

        @block.scalar
        def _(act):
            def split_w(j, par):
                e = act.value_load(tab[0:1, 0, bass.ds(2 * j + par, 1)], min_val=0, max_val=E - 1)
                two = ago(j, par, 2)
                if two:
                    act.wait_ge(h_f.sem, h_f.val(2 * j + par - 2))
                    act.nop(nofuse=True)
                nc.scalar.activation(wh[par][:], wf[:, e, 0, :], ACT.Copy).then_inc(wh_ok.sem, 1)

            def high(j, par):
                act.wait_ge(xT_f.sem, xT_f.val(2 * j + par))
                two = ago(j, par, 2)
                if two:
                    act.wait_ge(h_f.sem, h_f.val(2 * j + par - 2))
                nc.scalar.activation(xh[par][:], x_bank[:], ACT.Copy).then_inc(xh_ok.sem, 1)

            def add_b2(j, par):
                i = 2 * j + par
                act.wait_ge(w2_done.sem, w2_done.val(i))
                if not isinstance(i, int) or i >= 1:
                    act.wait_ge(back_f.sem, back_f.val(i - 1))
                nc.scalar.activation(yT[:], y_banks[par][:], ACT.Identity, bias=bias[par][:, FC:FC + 1]).then_inc(yT_ok.sem, 1)

            def result(j, par):
                i = 2 * j + par
                act.wait_ge(back_f.sem, back_f.val(i))
                two = ago(j, par, 2)
                if two:
                    act.wait_ge(y_st[par].sem, y_st[par].val(two[0]))
                nc.scalar.activation(yo[par][:], t_bank[:].rearrange("p (c d) -> p c d", c=TQ), ACT.Copy).then_inc(yo_ok.sem, 1)
                act.wait_ge(yo_ok.sem, yo_ok.val(i))
                act.dma_start(y_d[i], yo[par][:]).then_inc(y_st[par].sem, 16)

            def body(j, par):
                i, one = 2 * j + par, ago(j, par, 1)
                nxt = (j, 1) if par == 0 else (j + 1, 0)
                more_tiles = not isinstance(i, int) or i < NT - 1
                act.wait_ge(bias_in[par].sem, bias_in[par].val(j))
                for c in range(FC):
                    act.wait_ge(h_f.sem, h_f.val(i, c + 1))
                    if one:
                        act.wait_ge(w2_done.sem, w2_done.val(i - 1, c + 1))
                    nc.scalar.activation(g[c][:], h_banks[c], ACT.Gelu, bias=bias[par][:, c:c + 1]).then_inc(g_ok.sem, 1)
                    if c == 0 and one:
                        add_b2(*one)
                    if c == 1 and more_tiles:
                        high(*nxt)
                if more_tiles:
                    split_w(*nxt)
                if one:
                    result(*one)

            act.wait_ge(w_in.sem, 16 * (E + 1))
            act.wait_ge(tab_ok.sem, 1)
            split_w(0, 0)
            high(0, 0)
            tiles(act, body)
            add_b2(NT // 2, 0)
            result(NT // 2, 0)
            for par, last in ((0, NT // 2), (1, NT // 2 - 1)):
                act.wait_ge(y_st[par].sem, y_st[par].val(last))

        @block.vector
        def _(dve):
            steps = [0]

            def step(i):
                steps[0] += 1
                i.then_inc(a["table_step"].sem, 1)
                dve.wait_ge(a["table_step"].sem, steps[0])

            dve.wait_ge(a["iotas"].sem, a["iotas_before"] + 3)
            step(nc.vector.tensor_tensor(out=cnt[:], in0=base[:], in1=iota_r[:], op=ALU.subtract))
            step(nc.vector.tensor_tensor(out=more[:], in0=cnt[:].unsqueeze(2).broadcast_to([128, E, S * B // TS]),
                                         in1=iota_k[:].unsqueeze(1).broadcast_to([128, E, S * B // TS]), op=ALU.is_gt))
            step(nc.vector.tensor_reduce(out=tls[:], in_=more[:], op=ALU.add, axis=AX.X))
            step(nc.vector.tensor_copy(ends[:, 0:1], tls[:, 0:1]))
            for e in range(1, E):
                step(nc.vector.tensor_tensor(out=ends[:, e:e + 1], in0=ends[:, e - 1:e], in1=tls[:, e:e + 1], op=ALU.add))
            step(nc.vector.tensor_scalar(rest_rows[:], tls[:], -float(TS), float(REGION), ALU.mult, ALU.add))
            step(nc.vector.memset(tab_f[:, 0, :], 0.0))
            step(nc.vector.tensor_scalar(tab_f[:, 1, :], iota_t[:], float(TS), None, ALU.mult))
            for e in range(E - 1):
                step(nc.vector.tensor_scalar(past[:], iota_t[:], ends[:, e:e + 1], None, ALU.is_ge))
                step(nc.vector.tensor_tensor(out=tab_f[:, 0, :], in0=tab_f[:, 0, :], in1=past[:], op=ALU.add))
                step(nc.vector.tensor_scalar(skip[:], past[:], rest_rows[:, e:e + 1], None, ALU.mult))
                step(nc.vector.tensor_tensor(out=tab_f[:, 1, :], in0=tab_f[:, 1, :], in1=skip[:], op=ALU.add))
            nc.vector.tensor_copy(tab[:], tab_f[:]).then_inc(tab_ok.sem, 1)

            def low(j, par):
                i = 2 * j + par
                dve.wait_ge(xh_ok.sem, xh_ok.val(i))
                nc.vector.tensor_tensor(out=xl[par][:], in0=x_bank[:], in1=hi32(xh[par][:]), op=ALU.subtract)\
                    .then_inc(xl_ok.sem, 1)

            def split_w(j, par):
                e = dve.value_load(tab[0:1, 0, bass.ds(2 * j + par, 1)], min_val=0, max_val=E - 1)
                if ago(j, par, 2):
                    dve.wait_ge(w2_done.sem, w2_done.val(2 * j + par - 2))
                dve.wait_ge(wh_ok.sem, wh_ok.val(2 * j + par))
                nc.vector.tensor_tensor(out=wl[par][:], in0=wf[:, e, 0, :], in1=hi32(wh[par][:]), op=ALU.subtract)\
                    .then_inc(wl_ok.sem, 1)
                nc.vector.tensor_copy(w2[par][:], wf[:, e, 1, :]).then_inc(wl_ok.sem, 1)

            dve.wait_ge(tab_ok.sem, 1)
            split_w(0, 0)
            low(0, 0)

            def body(j, par):
                nxt = (j, 1) if par == 0 else (j + 1, 0)
                if not isinstance(j, int) or 2 * j + par < NT - 1:
                    low(*nxt)
                    split_w(*nxt)

            tiles(dve, body)
            slots = a["slot_all"][:].rearrange("p n s k -> p (n s k)")
            step(nc.vector.tensor_scalar(row_f[:], slots, 1.0, None, ALU.mult))
            for e in range(E - 1):
                step(nc.vector.tensor_scalar(past_r[:], slots, float((e + 1) * REGION), rest_rows[:, e:e + 1],
                                             ALU.is_ge, ALU.mult))
                step(nc.vector.tensor_tensor(out=row_f[:], in0=row_f[:], in1=past_r[:], op=ALU.subtract))
            step(nc.vector.tensor_copy(a["row_all"][:], row_f[:]))

        @block.tensor
        def _(pe):
            def front(j, par):
                pe.wait_ge(xg_in[par].sem, xg_in[par].val(j))
                for c in range(TQ):
                    i = nc.tensor.transpose(x_bank[:, c * 128:(c + 1) * 128], xg[par][:, c, :], ident[:])
                i.then_inc(xT_f.sem, 1)

            def back(j, par):
                i = 2 * j + par
                pe.wait_ge(yT_ok.sem, yT_ok.val(i))
                if not isinstance(i, int) or i >= 1:
                    pe.wait_ge(yo_ok.sem, yo_ok.val(i - 1))
                for c in range(TQ):
                    last = nc.tensor.transpose(t_bank[:, c * 128:(c + 1) * 128], yT[:, c * 128:(c + 1) * 128], ident[:])
                last.then_inc(back_f.sem, 1)

            def body(j, par):
                i, one = 2 * j + par, ago(j, par, 1)
                pe.wait_ge(wl_ok.sem, wl_ok.val(i))
                pe.wait_ge(xl_ok.sem, xl_ok.val(i))

                def up(c):
                    if one:
                        pe.wait_ge(g_ok.sem, g_ok.val(i - 1, c + 1))
                    w = slice(c * 128, (c + 1) * 128)
                    nc.tensor.matmul(h_banks[c], wh[par][:, w], xh[par][:], start=True, stop=False)
                    nc.tensor.matmul(h_banks[c], wh[par][:, w], xl[par][:], start=False, stop=False)
                    nc.tensor.matmul(h_banks[c], wl[par][:, w], xh[par][:], start=False, stop=True).then_inc(h_f.sem, 1)

                def down(c):
                    o, w = y_banks[par][:], slice(c * 128, (c + 1) * 128)
                    if c == 0 and ago(j, par, 2):
                        pe.wait_ge(yT_ok.sem, yT_ok.val(i - 2))
                    pe.wait_ge(g_ok.sem, g_ok.val(i, c + 1))
                    nc.tensor.matmul(o, w2[par][:, w], g[c][:], start=(c == 0), stop=(c == FC - 1)).then_inc(w2_done.sem, 1)

                up(0)
                up(1)
                if not isinstance(i, int) or i < NT - 1:
                    front(*((j, 1) if par == 0 else (j + 1, 0)))
                up(2)
                down(0)
                up(3)
                down(1)
                if one:
                    back(*one)
                down(2)
                down(3)

            front(0, 0)
            tiles(pe, body)
            back(NT // 2, 0)

    phase.close()
    return dict(ids_in=ids_in, xg_in=xg_in, y_st=y_st)


def phase_c(nc, ctx, sb, sem, a):
    phase = ctx.enter_context(ExitStack())

    def pair(name, shape, dt=F32):
        return [phase.enter_context(nc.sbuf_tensor(f"{name}{i}", shape, dt)) for i in range(2)]

    xr, yo = pair("xr", [128, NS, D]), pair("out", [128, NS, D])
    y2 = pair("y2", [128, NS, 2, D])
    acc = pair("acc", [128, NS, D])
    rows, pr = pair("rows", [128, NS * 2], I32), pair("pr", [128, 2, NS])
    xr_in, y2_in, out_st = ([Steps(s.sem, per, s.val((NT + 1 - i) // 2 - 1)) for i, s in enumerate(a[n])]
                            for n, per in (("ids_in", 16), ("xg_in", 16 * NS * 2), ("y_st", 16)))
    rows_ok, acc_ok, out_ok = sem("rows_ok"), sem("acc_ok"), sem("out_ok")

    def blocks(engine, body):
        body(0, 0)
        body(0, 1)
        with engine.Fori(1, NB // 2) as j:
            body(j, 0)
            body(j, 1)

    def later(j):
        return not isinstance(j, int) or j > 0

    with nc.Block() as block:
        @block.sync
        def _(sp):
            def body(j, par):
                if later(j):
                    sp.wait_ge(out_ok.sem, out_ok.val(2 * j + par - 2))
                sp.dma_start(xr[par][:], a["x3_d"][2 * j + par]).then_inc(xr_in[par].sem, 16)

            blocks(sp, body)

        @block.scalar
        def _(act):
            def body(j, par):
                act.wait_ge(out_ok.sem, out_ok.val(2 * j + par))
                act.dma_start(a["out_v"][2 * j + par], yo[par][:]).then_inc(out_st[par].sem, 16)

            blocks(act, body)
            for par in range(2):
                act.wait_ge(out_st[par].sem, out_st[par].val(NB // 2 - 1))

        @block.gpsimd
        def _(pool):
            def body(j, par):
                pool.wait_ge(rows_ok.sem, rows_ok.val(2 * j + par))
                if later(j):
                    pool.wait_ge(out_ok.sem, out_ok.val(2 * j + par - 2))
                pool.nop(nofuse=True)
                for s in range(NS):
                    for k in range(2):
                        nc.gpsimd.indirect_dma_start(
                            out=y2[par][:, s, k, :], out_offset=None, in_=a["y_rows"],
                            in_offset=bass.IndirectOffsetOnAxis(ap=rows[par][:, 2 * s + k:2 * s + k + 1], axis=0))\
                            .then_inc(y2_in[par].sem, 16)

            blocks(pool, body)

        @block.vector
        def _(dve):
            def fetch(j, par):
                if later(j):
                    dve.wait_ge(y2_in[par].sem, y2_in[par].val(j - 1))
                i = 2 * j + par
                nc.vector.tensor_tensor(out=rows[par][:], in0=a["row_all"][:, bass.ds(i * NS * 2, NS * 2)],
                                        in1=a["row_all"][:, bass.ds(i * NS * 2, NS * 2)], op=ALU.max).then_inc(rows_ok.sem, 1)

            def body(j, par):
                i = 2 * j + par
                nc.vector.tensor_tensor(out=pr[par][:], in0=a["prob_all"][:, i], in1=a["prob_all"][:, i], op=ALU.max)\
                    .then_inc(acc_ok.sem, 1)
                dve.wait_ge(xr_in[par].sem, xr_in[par].val(j))
                dve.wait_ge(y2_in[par].sem, y2_in[par].val(j))
                dve.wait_ge(acc_ok.sem, 2 * i + 1)
                for s in range(NS):
                    last = nc.vector.scalar_tensor_tensor(out=acc[par][:, s, :], in0=y2[par][:, s, 0, :],
                                                          scalar=pr[par][:, 0, s:s + 1], in1=xr[par][:, s, :],
                                                          op0=ALU.mult, op1=ALU.add)
                last.then_inc(acc_ok.sem, 1)
                if later(j):
                    dve.wait_ge(out_st[par].sem, out_st[par].val(j - 1))
                dve.wait_ge(acc_ok.sem, 2 * i + 2)
                for s in range(NS):
                    last = nc.vector.scalar_tensor_tensor(out=yo[par][:, s, :], in0=y2[par][:, s, 1, :],
                                                          scalar=pr[par][:, 1, s:s + 1], in1=acc[par][:, s, :],
                                                          op0=ALU.mult, op1=ALU.add)
                last.then_inc(out_ok.sem, 1)

            fetch(0, 0)
            fetch(0, 1)
            for par in range(2):
                body(0, par)
                fetch(1, par)
            with dve.Fori(1, NB // 2 - 1) as j:
                for par in range(2):
                    body(j, par)
                    fetch(j + 1, par)
            body(NB // 2 - 1, 0)
            body(NB // 2 - 1, 1)

    phase.close()


_OUT = ("out_dram", (B, S, D))


def kernel(x, ctx_1024, mask_BxSxS2_if1, L0_attn_Wq, L0_attn_Wk, L0_attn_Wv, L0_attn_Wff, L0_attn_bff, L0_xattn_Wq,
           L0_xattn_bq, L0_xattn_Wk, L0_xattn_bk, L0_xattn_Wv, L0_xattn_bv, L0_xattn_Wo, L0_xattn_bo, L0_ffn_Wp,
           L0_ffn_sim_matrix, L0_ffn_temperature, L0_ffn_W1, L0_ffn_b1, L0_ffn_W2, L0_ffn_b2):
    import numpy as np
    import concourse.bacc as bacc
    from concourse.bass_utils import run_bass_kernel_spmd

    by_place = np.array([h * DH + i for i in range(DH) for h in range(H)])
    by_slot = np.array([(HG * g + 4 * u + c) * DH + i for u in range(2) for g in range(2) for c in range(4)
                        for i in range(DH)])
    a = np.asarray
    arrays = {
        "x": a(x), "ctx": a(ctx_1024), "mask": a(mask_BxSxS2_if1),
        "Wq": a(L0_attn_Wq).T[:, by_place], "Wk": a(L0_attn_Wk).T[:, by_place], "Wv": a(L0_attn_Wv).T,
        "Wff": a(L0_attn_Wff).T[by_slot], "bff": a(L0_attn_bff),
        "xWq": a(L0_xattn_Wq).T[:, by_place], "xbq": a(L0_xattn_bq)[by_place],
        "xWk": a(L0_xattn_Wk).T[:, by_place], "xbk": a(L0_xattn_bk)[by_place],
        "xWv": a(L0_xattn_Wv).T, "xbv": a(L0_xattn_bv), "xWo": a(L0_xattn_Wo).T[by_slot], "xbo": a(L0_xattn_bo),
        "Wp": a(L0_ffn_Wp), "WpT": a(L0_ffn_Wp).T, "sim": a(L0_ffn_sim_matrix),
        "temp": a(L0_ffn_temperature).reshape(1),
        "W1": a(L0_ffn_W1), "b1": a(L0_ffn_b1).reshape(E, FC, 128).transpose(0, 2, 1), "W2": a(L0_ffn_W2), "b2": a(L0_ffn_b2),
    }
    nc = bacc.Bacc("TRN2", target_bir_lowering=False, num_devices=1)
    fed, args = {}, []
    for name, value in arrays.items():
        value = np.ascontiguousarray(value)
        fed[f"{name}_dram"] = value
        args.append(nc.dram_tensor(f"{name}_dram", value.shape, mybir.dt.from_np(value.dtype), kind="ExternalInput").ap())
    out = nc.dram_tensor(_OUT[0], _OUT[1], F32, kind="ExternalOutput").ap()
    program(nc, *args, out)
    result = run_bass_kernel_spmd(nc, [fed], core_ids=[0])
    return result.results[0][_OUT[0]]
```

```python
import concourse.bass as bass
from concourse import mybir
from contextlib import ExitStack

F32 = mybir.dt.float32
F32R = mybir.dt.float32r
BF16 = mybir.dt.bfloat16
I32 = mybir.dt.int32
U32 = mybir.dt.uint32
ALU = mybir.AluOpType
ACT = mybir.ActivationFunctionType
AX = mybir.AxisListType

B, S, D = 64, 128, 128
SC = 77
H, DH = 16, 8
E, F = 8, 512
NS = 4
NB = B // NS
T = NS * S
TC = NS * SC
FC = F // 128
NPAIR = 6
KS = NPAIR * DH
NG = 2
HG = H // NG
KR = NG * KS
KM = KR + NG * 3
MASKED = -(2.0 ** 100)
LN_EPS = 1e-5
TS = 512
TQ = TS // 128
DW = D + 2
REGION = B * S + TS
NT = 2 * B * S // TS + E - 1
SPARE = E - 1
SLOTS = E * REGION + SPARE * TS
ROUTE = 17
L2_EPS2 = 1e-24
UNITS = 4 * NS
LEAD = 1
STEPS = UNITS + LEAD + 2
BANK = {"q": 0, "k": 0, "cq": 1, "ck": 1, "m": 0, "cm": 0}
VW = 32


class Steps:

    def __init__(self, sem, per, base=0):
        self.sem, self.per, self.base = sem, per, base

    def val(self, block, k=None):
        return block * self.per + (self.base + (self.per if k is None else k))


def program(nc, x, ctx_in, mask, Wq, Wk, Wv, Wff, bff, xWq, xbq, xWk, xbk, xWv, xbv, xWo, xbo,
            Wp, WpT, sim, temp, W1, b1, W2, b2, out):
    ctx = ExitStack()
    with ctx:
        def sb(name, shape, dt=F32):
            return ctx.enter_context(nc.sbuf_tensor(name, shape, dt))

        def pb(name, shape):
            return ctx.enter_context(nc.psum_tensor(name, shape, F32))

        def sem(name, per=1):
            return Steps(ctx.enter_context(nc.semaphore(name)), per)

        def dram(name, shape, dt=F32):
            return nc.dram_tensor(name, shape, dt, kind="Internal").ap()

        x_v = x.rearrange("(n s) p d -> n p s d", s=NS)
        ctx_v = ctx_in.rearrange("(n s) p d -> n p s d", s=NS)
        mask_v = mask.rearrange("(n s) p k -> n p s k", s=NS)
        out_v = out[0:B * S].rearrange("(n s p) d -> n p s d", s=NS, p=S)
        stk = {"q": dram("stk_q", [NPAIR, D, T], BF16), "k": dram("stk_k", [NPAIR, D, T], BF16),
               "cq": dram("stk_cq", [NPAIR, D, T], BF16), "ck": dram("stk_ck", [NPAIR, D, TC], BF16)}
        mscr = {"m": dram("mscr", [3, H, T], BF16), "cm": dram("cmscr", [3, H, T], BF16)}
        xs_d = dram("xs_d", [SLOTS, DW])

        ident = sb("ident", [128, 128])
        identb = sb("identb", [128, 128], BF16)
        mhalf = sb("mhalf", [128, NS])
        iota8 = sb("iota8", [128, E])
        w_q, w_k, w_v, w_ff = (sb(n, [128, 128]) for n in ("w_q", "w_k", "w_v", "w_ff"))
        cw_q, cw_k, cw_v, cw_o = (sb(n, [128, 128]) for n in ("cw_q", "cw_k", "cw_v", "cw_o"))
        bff_b, bo_b = sb("bff_b", [128, D]), sb("bo_b", [128, D])
        bv_b = sb("bv_b", [SC, D])
        bq_c, bk_c = sb("bq_c", [128, 1]), sb("bk_c", [128, 1])
        wp_n = sb("wp_n", [128, 128])
        wpx = sb("wpx", [128, D + E])
        sim_n, sim_u, sim_j = sb("sim_n", [E, D]), sb("sim_u", [E, D]), sb("sim_j", [E, D])
        sim_sq_sum, sim_ss, sim_rn = sb("sim_sq_sum", [E, 1]), sb("sim_ss", [E, 1]), sb("sim_rn", [E, 1])
        simT = sb("simT", [128, E])
        temp_b, itemp = sb("temp_b", [128, 1]), sb("itemp", [128, 1])
        tri, ones = sb("tri", [128, 128], BF16), sb("ones", [128, 128], BF16)
        base = sb("base", [128, E])
        big = sb("big", [128, 4, NS * H * VW])
        vaug, cvaug = ([big[:, g + i].rearrange("p (s h w) -> p s h w", s=NS, h=H) for i in range(2)] for g in (0, 2))
        wf = big[:].rearrange("p a (e j f) -> p (a e) j f", e=E // 4, j=2)
        tab = sb("tab", [128, 2, NT], I32)

        phase_a = ctx.enter_context(ExitStack())

        def sa(name, shape, dt=F32):
            return phase_a.enter_context(nc.sbuf_tensor(name, shape, dt))

        def pair(name, shape, dt=F32):
            return [sa(f"{name}{i}", shape, dt) for i in range(2)]

        xin, xagain = sa("xin", [128, NS, D]), sa("xagain", [128, NS, D])
        cin = sa("cin", [SC, NS, D])
        mk = sa("mk", [128, NS, SC], I32)
        mbias = pair("mbias", [128, NS, SC], BF16)
        xres, x2, x3 = (sa(n, [128, NS, D]) for n in ("xres", "x2", "x3"))
        x2res = pair("x2res", [128, NS, D])
        xn = {n: sa(f"xn_{n}", [128, NS, D]) for n in ("1", "2", "3")}
        xnT = {n: sa(f"xnT_{n}", [128, T]) for n in ("1", "2", "3")}
        cT = sa("cT", [128, TC])
        lnst = {n: sa(f"lnst_{n}", [128, NS, 6]) for n in ("1", "2", "3")}
        lnmv = {n: sa(f"lnmv_{n}", [128, NS, 2]) for n in ("1", "2", "3")}
        lnve = {n: sa(f"lnve_{n}", [128, NS]) for n in ("1", "2", "3")}
        lnrs = {n: sa(f"lnrs_{n}", [128, NS]) for n in ("1", "2", "3")}
        lnnm = {n: sa(f"lnnm_{n}", [128, NS]) for n in ("1", "2", "3")}
        parts = {n: sa(f"parts_{n}", [128, 3, T], BF16) for n in ("q", "k", "cq")}
        parts["ck"] = sa("parts_ck", [128, 3, TC], BF16)
        parts["m"] = parts["cm"] = sa("parts_m", [H, 3, T], BF16)
        rest = {n: sa(f"rest_{n}", [128, T]) for n in ("q", "k", "cq")}
        rest["ck"] = sa("rest_ck", [128, TC])
        rest["m"] = rest["cm"] = sa("rest_m", [H, T])
        qs, cqs = pair("qs", [KM, HG, T], BF16), pair("cqs", [KM, HG, T], BF16)
        ks, cks = pair("ks", [KM, H, T], BF16), pair("cks", [KM, H, TC], BF16)
        negm = {n: sa(f"negm_{n}", [128, NS, 2, HG]) for n in ("m", "cm")}
        probs = [sa(f"probs{i}", [128, T]) for i in range(3)]
        oT = dict.fromkeys("sc", sa("oT", [128, NS, T]))
        rden = {n: sa(f"rden_{n}", [128, NS, H]) for n in ("s", "c")}
        on = dict.fromkeys("sc", sa("on", [128, NS, H, DH]))
        onT = dict.fromkeys("sc", sa("onT", [128, T]))
        sq_junk = sa("sq_junk", [128, NS, D])
        ss, ssc, rn = sa("ss", [128, NS]), sa("ssc", [128, NS]), sa("rn", [128, NS])
        graw, gs = sa("graw", [128, NS, E]), sa("gs", [128, NS, E])
        top_v = sa("top_v", [128, NS, 8])
        top_i = sa("top_i", [128, NS, 8], U32)
        top_f = sa("top_f", [128, NS, 2])
        dv, ev, den = (sa(n, [128, NS]) for n in ("dv", "ev", "den"))
        eq1, eq2, pos = (sa(n, [128, NS, E]) for n in ("eq1", "eq2", "pos"))
        here = [sa(f"here{k}", [128, NS, E]) for k in range(2)]
        chosen = sa("chosen", [128, NS, E], BF16)
        before = sa("before", [128, NS + 1, E], BF16)
        slot_f, slot_i = sa("slot_f", [128, NS, 2]), sa("slot_i", [128, NS * 2], I32)
        iota_r, iota_k, iota_t = sa("iota_r", [128, E]), sa("iota_k", [128, S * B // TS]), sa("iota_t", [128, NT])
        tok = sa("tok", [128, NS])
        xrow = sa("xrow", [128, NS, 2, DW])
        pr = sa("pr", [128, 2, NS])

        sc_m = [pb(f"sc_m{i}", [128, 512]) for i in range(2)]
        sc_a = [pb(f"sc_a{i}", [128, 512]) for i in range(2)]
        pv = [pb(f"pv{i}", [128, 512]) for i in range(2)]
        wb = [pb(f"wb{i}", [128, 512]) for i in range(2)]

        const_in = sem("const_in")
        ident_ok = sem("ident_ok")
        preset = {n: sem(f"preset_{n}") for n in ("k", "ck", "v", "cv")}
        ones_in = sem("ones_in", 32)
        gate_set, gate_mm, gate_ev = sem("gate_set"), sem("gate_mm"), sem("gate_ev")
        xa_in = sem("xa_in", 16)
        x_in, c_in, mk_in = sem("x_in", 16), sem("c_in", 16), sem("mk_in", 16)
        mb_ok = sem("mb_ok")
        xres_ok, x2res_ok = sem("xres_ok"), sem("x2res_ok")
        ln_st = {n: sem(f"ln{n}_st", 3) for n in "123"}
        ln_ve = {n: sem(f"ln{n}_ve") for n in "123"}
        ln_rs = {n: sem(f"ln{n}_rs") for n in "123"}
        ln_ok = {n: sem(f"ln{n}_ok", NS) for n in "123"}
        ONE = ("x1T", "x2T", "x3T", "cT", "q", "k", "v", "cq", "ck", "cv", "m", "cm", "onT_s", "onT_c",
               "y_s", "y_c", "pj0", "pj1", "rank")
        filled = {n: sem(f"{n}_filled") for n in ONE}
        drained = {n: sem(f"{n}_drained") for n in ONE}
        for n in ("s", "c"):
            filled[f"oTT_{n}"] = sem(f"oTT_{n}_filled", NS)
            drained[f"oTT_{n}"] = sem(f"oTT_{n}_drained", NS)
        part1 = {n: sem(f"{n}_part1") for n in ("q", "k", "cq", "ck", "m", "cm")}
        part2 = {n: sem(f"{n}_part2") for n in part1}
        part3 = {n: sem(f"{n}_part3") for n in part1}
        dumped = {n: sem(f"{n}_dumped", 48) for n in ("q", "k", "cq", "ck")}
        dumped["m"], dumped["cm"] = sem("m_dumped", 16), sem("cm_dumped", 16)
        stacked = {n: sem(f"{n}_stacked", 16 if n in ("q", "cq") else 32) for n in part1}
        max_f = {n: sem(f"{n}_sc_filled", UNITS) for n in ("m", "cm")}
        max_ok = {n: sem(f"{n}_max_ok", UNITS) for n in ("m", "cm")}
        st_f = {n: sem(f"st_{n}_filled", UNITS) for n in ("s", "c")}
        exp_ok = {n: sem(f"exp_{n}_ok", UNITS) for n in ("s", "c")}
        pv_ok = {n: sem(f"pv_{n}_ok", UNITS) for n in ("s", "c")}
        oT_ok = {n: sem(f"oT_{n}_ok", NS) for n in ("s", "c")}
        rden_ok = {n: sem(f"rden_{n}_ok", NS) for n in ("s", "c")}
        ss_ok = sem("ss_ok", 2)
        ssc_ok, rn_ok, gs_ok, dv_ok, ev_ok, slot_ok, fill_ok = (
            sem(n) for n in ("ssc_ok", "rn_ok", "gs_ok", "dv_ok", "ev_ok", "slot_ok", "fill_ok"))
        gate_step = sem("gate_step", ROUTE)
        listed = Steps(sem("listed").sem, 16 * 2 * NS, 16 * 2 * NS)
        x3_st, rows_ok = sem("x3_st", 16), sem("rows_ok", 2)
        tab_ok, table_step, iotas = sem("tab_ok"), sem("table_step"), sem("iotas")
        w_in, fill_st = sem("w_in", 16), sem("fill_st", 16)

        CONSTS = [(w_q, Wq), (w_k, Wk), (w_v, Wv), (w_ff, Wff), (cw_q, xWq), (cw_k, xWk), (cw_v, xWv), (cw_o, xWo),
                  (bff_b, bff.unsqueeze(0).broadcast_to([128, D])), (bo_b, xbo.unsqueeze(0).broadcast_to([128, D])),
                  (bv_b, xbv.unsqueeze(0).broadcast_to([SC, D])),
                  (bq_c, xbq.unsqueeze(1)), (bk_c, xbk.unsqueeze(1)), (wp_n, Wp), (wpx[:, 0:D], WpT), (sim_n, sim),
                  (temp_b, temp.unsqueeze(0).broadcast_to([128, 1]))]

        empty = oT["c"][:].rearrange("p s q -> p (s q)")[:, 0:TQ * DW].rearrange("p (c w) -> p c w", c=TQ)
        scrap = xn["1"][:].rearrange("p s d -> p (s d)")
        widths = dict(cnt=E, tls=E, ends=E, rest_rows=E, base_i=E, past=NT, skip=NT, tab_f=2 * NT, more=E * (B * S // TS))
        at = {n: sum(list(widths.values())[:k]) for k, n in enumerate(widths)}
        cnt, tls, ends, rest_rows, base_i, past, skip, tab_f, more = (scrap[:, at[n]:at[n] + w] for n, w in widths.items())
        base_i, tab_f = base_i.bitcast(I32), tab_f.rearrange("p (k i) -> p k i", k=2)
        more = more.rearrange("p (e k) -> p e k", e=E)

        def on_(b):
            return not isinstance(b, int) or 0 <= b < NB

        def steps(engine, body, after={}):
            for t in range(-3, 4):
                body(t, t % 2)
                if t in after:
                    after[t]()
            with engine.Fori(4, NB - 4, 2) as t:
                body(t, 0)
                body(again(engine, t, 1), 1)
            for t in range(NB - 4, NB + 4):
                body(t, t % 2)
                if t in after:
                    after[t]()

        def again(engine, t, ahead=0):
            if isinstance(t, int):
                return t + ahead
            copy = engine.alloc_register()
            engine.reg_add(copy, t, ahead)
            return engine.snap(copy, min_val=t.min_val + ahead, max_val=t.max_val + ahead)

        def wait_block(engine, s, b, k=None):
            if on_(b):
                engine.wait_ge(s.sem, s.val(b, k))

        with nc.Block() as block:
            @block.sync
            def _(sp):
                def constants():
                    for dst, src in CONSTS[::2]:
                        sp.dma_start(dst[:], src).then_inc(const_in.sem, 16)

                def dump(n, b):
                    sp.wait_ge(part3[n].sem, part3[n].val(b))
                    scr, p = stk[n], parts[n]
                    cols = p.shape[2]
                    if n in ("q", "cq"):
                        runs = [(0, 3, p[:, 0:1, :].broadcast_to([128, 3, cols])),
                                (3, 5, p[:, 1:2, :].broadcast_to([128, 2, cols])), (5, 6, p[:, 2:3, :])]
                    else:
                        runs = [(0, 3, p[:, 0:3, :]), (3, 5, p[:, 0:2, :]), (5, 6, p[:, 0:1, :])]
                    for lo, hi, src in runs:
                        sp.dma_start(scr[lo:hi].rearrange("c r t -> r c t"), src).then_inc(dumped[n].sem, 16)

                def stack(n, b, dst):
                    sp.wait_ge(dumped[n].sem, dumped[n].val(b))
                    if n in ("k", "ck") and isinstance(b, int) and b < 2:
                        sp.wait_ge(preset[n].sem, b + 1)
                        cols = dst.shape[2] // NS
                        for g in range(NG):
                            sp.dma_start(dst[KR + 3 * g:KR + 3 * (g + 1), g * HG:(g + 1) * HG, :]
                                         .rearrange("c j (s k) -> c (j s) k", k=cols),
                                         ones[0:3, 0:cols].unsqueeze(1).broadcast_to([3, HG * NS, cols])).then_inc(ones_in.sem, 16)
                    if n in ("q", "cq"):
                        view = stk[n].rearrange("c (i g j) t -> (c i g) j t", i=DH, g=NG)
                        sp.dma_start(dst[0:KR, :, :], view).then_inc(stacked[n].sem, 16)
                    else:
                        view = stk[n].rearrange("c (i g j) t -> g (c i) j t", i=DH, g=NG)
                        for g in range(NG):
                            sp.dma_start(dst[g:KR:NG, g * HG:(g + 1) * HG, :], view[g]).then_inc(stacked[n].sem, 16)

                def fold(n, b, dst):
                    sp.wait_ge(part3[n].sem, part3[n].val(b))
                    sp.dma_start(mscr[n].rearrange("c h t -> h c t"), parts[n][:]).then_inc(dumped[n].sem, 16)
                    sp.wait_ge(dumped[n].sem, dumped[n].val(b))
                    view = mscr[n].rearrange("c (g j) t -> g c j t", g=NG)
                    for g in range(NG):
                        sp.dma_start(dst[KR + 3 * g:KR + 3 * g + 3, :, :], view[g]).then_inc(stacked[n].sem, 16)

                def body(t, par):
                    if on_(t):
                        wait_block(sp, filled["cT"], t - 1)
                        sp.dma_start(cin[:], ctx_v[t]).then_inc(c_in.sem, 16)
                        wait_block(sp, mb_ok, t - 1)
                        sp.dma_start(mk[:], mask_v[t]).then_inc(mk_in.sem, 16)
                        wait_block(sp, xres_ok, t - 1)
                        sp.dma_start(xagain[:], x_v[t]).then_inc(xa_in.sem, 16)
                    if on_(t - 1):
                        for n, dst in (("cq", cqs), ("ck", cks)):
                            wait_block(sp, st_f["c"], t - 3)
                            stack(n, t - 1, dst[1 - par])
                    if on_(t - 2):
                        fold("cm", t - 2, cqs[par])
                    if on_(t - 3):
                        sp.wait_ge(drained["y_c"].sem, drained["y_c"].val(t - 3))
                        sp.dma_start(out_v[t - 3], x3[:]).then_inc(x3_st.sem, 16)
                    if on_(t + 2):
                        dump("q", t + 2)
                        dump("k", t + 2)
                    if on_(t):
                        wait_block(sp, stacked["ck"], t - 1)
                        sp.nop(nofuse=True)
                        dump("ck", t)
                    if on_(t + 3):
                        wait_block(sp, ln_ok["1"], t + 2)
                        sp.dma_start(xin[:], x_v[t + 3]).then_inc(x_in.sem, 16)
                    if on_(t + 2):
                        for n, dst in (("q", qs), ("k", ks)):
                            wait_block(sp, st_f["s"], t)
                            stack(n, t + 2, dst[par])
                    if on_(t + 1):
                        fold("m", t + 1, qs[1 - par])
                    if on_(t):
                        dump("cq", t)

                steps(sp, body, {-3: constants})
                sp.wait_ge(pv_ok["s"].sem, pv_ok["s"].val(NB - 1))
                sp.wait_ge(pv_ok["c"].sem, pv_ok["c"].val(NB - 1))
                sp.dma_start(wf[:, :, 0, :], W1.rearrange("e d f -> d e f")).then_inc(w_in.sem, 16)
                for e in range(E):
                    sp.dma_start(wf[:, e, 1, :].rearrange("p (c d) -> p c d", c=FC), W2[e].rearrange("(c f) d -> f c d", f=128))\
                        .then_inc(w_in.sem, 16)
                sp.wait_ge(fill_ok.sem, 3)
                sp.wait_ge(table_step.sem, 1)
                for e in range(E):
                    end = sp.value_load(base_i[0:1, e:e + 1], min_val=0, max_val=E * REGION - TS)
                    sp.dma_start(xs_d[bass.ds(end, TS)].rearrange("(p c) w -> p c w", c=TQ), empty).then_inc(fill_st.sem, 16)
                sp.wait_ge(fill_st.sem, 16 * E)
                sp.wait_ge(w_in.sem, 16 * (E + 1))
                sp.wait_ge(tab_ok.sem, 1)
                sp.wait_ge(x3_st.sem, x3_st.val(NB - 1))

            @block.gpsimd
            def _(pool):
                fill = xrow[:, :, 0, :]
                nc.gpsimd.memset(ident[:], 0.0).then_inc(ident_ok.sem, 1)
                nc.gpsimd.memset(identb[:], 0.0).then_inc(ident_ok.sem, 1)
                nc.gpsimd.memset(ones[:], 1.0).then_inc(ident_ok.sem, 1)
                nc.gpsimd.memset(fill, 0.0).then_inc(ident_ok.sem, 1)
                nc.gpsimd.memset(mhalf[:], -0.5).then_inc(ident_ok.sem, 1)
                pool.wait_ge(ident_ok.sem, 5)
                for m in (ident, identb):
                    nc.gpsimd.affine_select(out=m[:], in_=m[:], compare_op=ALU.not_equal, fill=1.0, base=0,
                                            pattern=[[-1, 128]], channel_multiplier=1).then_inc(ident_ok.sem, 1)
                nc.gpsimd.affine_select(out=tri[:], in_=ones[:], compare_op=ALU.is_gt, fill=0.0, base=0,
                                        pattern=[[1, 128]], channel_multiplier=-1).then_inc(ident_ok.sem, 1)
                nc.gpsimd.iota(base[:], pattern=[[REGION, E]], base=0, channel_multiplier=0,
                               allow_small_or_imprecise_dtypes=True).then_inc(iotas.sem, 1)
                nc.gpsimd.iota(tok[:], pattern=[[S, NS]], base=-T, channel_multiplier=1,
                               allow_small_or_imprecise_dtypes=True).then_inc(iotas.sem, 1)
                nc.gpsimd.iota(xrow[:, :, 0, D].bitcast(I32), pattern=[[1, TQ]], base=B * S, channel_multiplier=TQ)\
                    .then_inc(fill_ok.sem, 1)
                pool.wait_ge(fill_ok.sem, 1)
                def power(n, b):
                    pool.wait_ge(ln_ve[n].sem, ln_ve[n].val(b))
                    nc.gpsimd.tensor_tensor(out=lnrs[n][:], in0=lnve[n][:], in1=mhalf[:], op=ALU.pow)\
                        .then_inc(ln_rs[n].sem, 1)

                def residual(dst, src, bias, done):
                    nc.gpsimd.tensor_tensor(out=dst[:], in0=src[:], in1=bias[:].unsqueeze(1).broadcast_to([128, NS, D]),
                                            op=ALU.add).then_inc(done.sem, 1)

                def third(n, b):
                    pool.wait_ge(part2[n].sem, part2[n].val(b))
                    nc.gpsimd.tensor_tensor(out=parts[n][:, 2, :], in0=rest[n][:], in1=parts[n][:, 1, :],
                                            op=ALU.subtract).then_inc(part3[n].sem, 1)

                def enlist(b):
                    pool.wait_ge(slot_ok.sem, slot_ok.val(b))
                    pool.wait_ge(gate_step.sem, gate_step.val(b))
                    pool.nop(nofuse=True)
                    for c in range(2 * NS):
                        nc.gpsimd.indirect_dma_start(out=xs_d, in_=xrow[:, c // 2, c % 2, :], in_offset=None,
                                                     out_offset=bass.IndirectOffsetOnAxis(ap=slot_i[:, c:c + 1], axis=0))\
                            .then_inc(listed.sem, 16)

                def body(t, par):
                    if on_(t):
                        wait_block(pool, drained["y_s"], t - 1)
                        pool.wait_ge(xa_in.sem, xa_in.val(t))
                        residual(xres, xagain, bff_b, xres_ok)
                    if on_(t - 2):
                        third("cm", t - 2)
                    if on_(t - 1):
                        wait_block(pool, drained["y_c"], t - 3)
                        pool.wait_ge(drained["y_s"].sem, drained["y_s"].val(t - 1))
                        residual(x2res[1 - par], x2, bo_b, x2res_ok)
                    if on_(t - 3):
                        power("3", t - 3)
                    if on_(t + 2):
                        third("q", t + 2)
                    if on_(t + 2):
                        third("k", t + 2)
                    if on_(t):
                        third("ck", t)
                    if on_(t - 4):
                        enlist(t - 4)
                    if on_(t + 1):
                        third("m", t + 1)
                    if on_(t):
                        power("2", t)
                    if on_(t + 3):
                        power("1", t + 3)
                    if on_(t - 3):
                        pool.wait_ge(ssc_ok.sem, ssc_ok.val(t - 3))
                        nc.gpsimd.tensor_tensor(out=rn[:], in0=ssc[:], in1=mhalf[:], op=ALU.pow).then_inc(rn_ok.sem, 1)
                    if on_(t):
                        third("cq", t)
                        wait_block(pool, st_f["c"], t - 2)
                        pool.wait_ge(mk_in.sem, mk_in.val(t))
                        pool.nop(nofuse=True)
                        nc.gpsimd.tensor_scalar(out=mbias[par][:], in0=mk[:], scalar1=0.0, scalar2=MASKED,
                                                op0=ALU.is_equal, op1=ALU.mult).then_inc(mb_ok.sem, 1)

                def zeros(stacks, n):
                    for tile in stacks:
                        nc.gpsimd.memset(tile[:].bitcast(F32), 0.0).then_inc(preset[n].sem, 1)
                    pool.wait_ge(preset[n].sem, 2)

                def numbers():
                    pool.wait_ge(const_in.sem, 16 * len(CONSTS))
                    pool.wait_ge(gate_set.sem, 5)
                    nc.gpsimd.tensor_tensor(out=sim_rn[:], in0=sim_ss[:], in1=mhalf[0:E, 0:1], op=ALU.pow)\
                        .then_inc(iotas.sem, 1)
                    nc.gpsimd.iota(iota_r[:], pattern=[[REGION, E]], base=0, channel_multiplier=0,
                                   allow_small_or_imprecise_dtypes=True).then_inc(iotas.sem, 1)
                    nc.gpsimd.iota(iota_k[:], pattern=[[TS, S * B // TS]], base=0, channel_multiplier=0,
                                   allow_small_or_imprecise_dtypes=True).then_inc(iotas.sem, 1)
                    nc.gpsimd.iota(iota_t[:], pattern=[[1, NT]], base=0, channel_multiplier=0,
                                   allow_small_or_imprecise_dtypes=True).then_inc(iotas.sem, 1)
                    zeros(cks, "ck")

                def spare_tiles():
                    for k in range(SPARE):
                        lo = E * REGION + k * TS
                        pool.dma_start(xs_d[lo:lo + TS].rearrange("(p c) w -> p c w", c=TQ), fill).then_inc(listed.sem, 16)
                    pool.dma_start(out[B * S:B * S + TS].rearrange("(p c) d -> p c d", c=TQ), xrow[:, :, 0, 0:D])\
                        .then_inc(listed.sem, 16)

                def empty_tile():
                    pool.wait_ge(drained["oTT_c"].sem, drained["oTT_c"].val(NB - 1))
                    nc.gpsimd.memset(empty, 0.0).then_inc(fill_ok.sem, 1)
                    pool.wait_ge(fill_ok.sem, 2)
                    nc.gpsimd.iota(empty[:, :, D].bitcast(I32), pattern=[[1, TQ]], base=B * S, channel_multiplier=TQ)\
                        .then_inc(fill_ok.sem, 1)

                steps(pool, body, {-3: lambda: zeros(ks, "k"), -2: numbers, -1: spare_tiles, NB + 2: empty_tile})
                pool.wait_ge(listed.sem, listed.val(NB - 1))

            @block.scalar
            def _(act):
                for dst, src in CONSTS[1::2]:
                    act.dma_start(dst[:], src).then_inc(const_in.sem, 16)
                act.wait_ge(const_in.sem, 16 * len(CONSTS))

                def evac(dst, n, b, bank, cols=T, rows=128):
                    act.wait_ge(filled[n].sem, filled[n].val(b))
                    nc.scalar.activation(dst, wb[bank][0:rows, 0:cols], ACT.Copy).then_inc(drained[n].sem, 1)

                def first(n, b, bias=None):
                    p = parts[n]
                    act.wait_ge(filled[n].sem, filled[n].val(b))
                    src = wb[BANK[n]][0:p.shape[0], 0:p.shape[2]]
                    if bias is None:
                        i = nc.scalar.activation(p[:, 0, :], src, ACT.Copy)
                    else:
                        i = nc.scalar.activation(p[:, 0, :], src, ACT.Identity, bias=bias[:, 0:1])
                    i.then_inc(part1[n].sem, 1)

                def second(n, b):
                    act.wait_ge(drained[n].sem, drained[n].val(b))
                    nc.scalar.activation(parts[n][:, 1, :], rest[n][:], ACT.Copy).then_inc(part2[n].sem, 1)

                def normalise(n, b, src, s):
                    if s == 0:
                        act.wait_ge(ln_st[n].sem, ln_st[n].val(b))
                    nc.scalar.activation(xn[n][:, s, :], src[:, s, :], ACT.Identity, bias=lnnm[n][:, s:s + 1],
                                         scale=lnrs[n][:, s:s + 1]).then_inc(ln_ok[n].sem, 1)

                def attend(n, b, rows, scale, between):
                    for u in range(STEPS):
                        e = u - LEAD
                        if on_(b) and 0 <= e < UNITS:
                            act.wait_ge(st_f[n].sem, st_f[n].val(b, e + 1))
                            if e >= 3:
                                act.wait_ge(pv_ok[n].sem, pv_ok[n].val(b, e - 2))
                            nc.scalar.activation(probs[e % 3][0:rows], sc_a[e % 2][0:rows], ACT.Exp, scale=scale)\
                                .then_inc(exp_ok[n].sem, 1)
                            if e % 4 == 3 and e > 4:
                                out_T(n, b, e // 4 - 1)
                        between(u)
                    if on_(b):
                        out_T(n, b, NS - 1)

                def out_T(n, b, s):
                    act.wait_ge(pv_ok[n].sem, pv_ok[n].val(b, 4 * s + 4))
                    nc.scalar.activation(oT[n][:, s, :], pv[s % 2][:], ACT.Copy).then_inc(oT_ok[n].sem, 1)

                def body(t, par):
                    def in_x(u):
                        if 2 <= u < 2 + NS and on_(t + 2):
                            normalise("1", t + 2, xin, u - 2)
                        if u == 5 and on_(t - 3):
                            evac(onT["c"][:], "onT_c", t - 3, 1)
                        if u == 6 and on_(t - 2):
                            first("cm", t - 2)
                        if u == 8 and on_(t - 2):
                            second("cm", t - 2)
                        if u == 8 and on_(t + 2):
                            evac(xnT["1"][:], "x1T", t + 2, 0)
                        if u == 9 and on_(t):
                            evac(cT[:], "cT", t, 1, TC)
                        if u == 10 and on_(t + 2):
                            first("q", t + 2)
                        if u == 11 and on_(t):
                            wait_block(act, dumped["ck"], t - 1)
                            first("ck", t, bk_c)
                        if u == 12 and on_(t + 2):
                            second("q", t + 2)
                        if u == 13 and on_(t + 2):
                            first("k", t + 2)
                        if u == 13 and on_(t):
                            second("ck", t)

                    def in_y(u):
                        if 0 <= u < 0 + NS and on_(t - 3):
                            if u == 0:
                                wait_block(act, rows_ok, t - 4)
                            normalise("3", t - 3, x3, u - 0)
                        if u == 4 and on_(t + 2):
                            if isinstance(t, int) and t + 2 == 0:
                                act.wait_ge(preset["v"].sem, 4)
                            act.wait_ge(filled["v"].sem, filled["v"].val(t + 2))
                            nc.scalar.activation(vaug[par][:, :, :, 0:DH], wb[0][:].rearrange("p (s h i) -> p s h i", s=NS, h=H),
                                                 ACT.Copy).then_inc(drained["v"].sem, 1)
                        if u == 5 and on_(t):
                            evac(onT["s"][:], "onT_s", t, 1)
                        if u == 6 and on_(t + 1):
                            first("m", t + 1)
                        if u == 8 and on_(t + 1):
                            second("m", t + 1)
                        if u == 8 and on_(t - 3):
                            evac(xnT["3"][:], "x3T", t - 3, 0)
                        if u in (10, 11) and on_(t - 3):
                            half = u - 10
                            n = f"pj{half}"
                            act.wait_ge(filled[n].sem, filled[n].val(t - 3))
                            for k in range(2):
                                s, a = 2 * half + k, (D + E) * k
                                i = nc.scalar.activation(sq_junk[:, s, :], wb[half][:, a:a + D], ACT.Square,
                                                         accum_out=ss[:, s:s + 1])
                            i.then_inc(ss_ok.sem, 1)
                            raw = wb[half][:, 0:2 * (D + E)].rearrange("p (k c) -> p k c", k=2)[:, :, D:D + E]
                            nc.scalar.activation(graw[:, 2 * half:2 * half + 2, :], raw, ACT.Copy)\
                                .then_inc(drained[n].sem, 1)
                        if 11 <= u < 11 + NS and on_(t):
                            normalise("2", t, x2, u - 11)
                        if u == 15 and on_(t):
                            evac(xnT["2"][:], "x2T", t, 0)
                        if u == 17 and on_(t):
                            first("cq", t, bq_c)

                    attend("s", t, 128, float(D) ** -0.5, in_x)
                    t = again(act, t)
                    attend("c", t - 2, SC, float(DH) ** -0.5, in_y)
                    if on_(t):
                        second("cq", t)
                    if on_(t - 3):
                        act.wait_ge(dv_ok.sem, dv_ok.val(t - 3))
                        nc.scalar.activation(ev[:], dv[:], ACT.Exp).then_inc(ev_ok.sem, 1)

                def gate():
                    act.wait_ge(gate_mm.sem, 1)
                    nc.scalar.activation(simT[:], wb[0][:, 0:E], ACT.Copy).then_inc(gate_ev.sem, 1)
                    act.wait_ge(gate_mm.sem, 2)
                    nc.scalar.activation(wpx[:, D:D + E], wb[0][:, 0:E], ACT.Copy).then_inc(gate_ev.sem, 1)

                steps(act, body, {-1: gate})

            @block.vector
            def _(dve):
                def ones_beside(tiles, n, rows):
                    for tile in tiles:
                        nc.vector.memset(tile, 0.0).then_inc(preset[n].sem, 1)
                    dve.wait_ge(preset[n].sem, 2)
                    for tile in tiles:
                        nc.vector.memset(tile[0:rows, :, :, DH:DH + 1], 1.0).then_inc(preset[n].sem, 1)

                ones_beside(vaug, "v", 128)
                nc.vector.memset(before[:, 0, :], 0.0).then_inc(gate_set.sem, 1)
                for e in range(E):
                    i = nc.vector.memset(iota8[:, e:e + 1], float(e))
                i.then_inc(gate_set.sem, 1)
                def stats(n, b, src):
                    for s in range(NS):
                        i = nc.vector.bn_stats(lnst[n][:, s, :], src[:, s, :])
                    i.then_inc(ln_st[n].sem, 1)
                    dve.wait_ge(ln_st[n].sem, ln_st[n].val(b, 1))
                    dve.nop(nofuse=True)
                    for s in range(NS):
                        i = nc.vector.bn_aggr(lnmv[n][:, s, :], lnst[n][:, s, :])
                    i.then_inc(ln_st[n].sem, 1)
                    dve.wait_ge(ln_st[n].sem, ln_st[n].val(b, 2))
                    nc.vector.tensor_scalar(lnve[n][:], lnmv[n][:, :, 1], LN_EPS, None, ALU.add).then_inc(ln_ve[n].sem, 1)

                def shift(n, b):
                    dve.wait_ge(ln_rs[n].sem, ln_rs[n].val(b))
                    nc.vector.scalar_tensor_tensor(out=lnnm[n][:], in0=lnmv[n][:, :, 0], scalar=-1.0, in1=lnrs[n][:],
                                                   op0=ALU.mult, op1=ALU.mult).then_inc(ln_st[n].sem, 1)

                def remainder(n, b, bias=None):
                    p, r = parts[n], rest[n]
                    dve.wait_ge(part1[n].sem, part1[n].val(b))
                    src = wb[BANK[n]][0:p.shape[0], 0:p.shape[2]]
                    if bias is None:
                        i = nc.vector.tensor_tensor(out=r[:], in0=src, in1=p[:, 0, :], op=ALU.subtract)
                    else:
                        i = nc.vector.scalar_tensor_tensor(out=r[:], in0=src, scalar=bias[:, 0:1], in1=p[:, 0, :],
                                                           op0=ALU.add, op1=ALU.subtract)
                    i.then_inc(drained[n].sem, 1)

                def second(n, b):
                    dve.wait_ge(drained[n].sem, drained[n].val(b))
                    nc.vector.tensor_copy(parts[n][:, 1, :], rest[n][:]).then_inc(part2[n].sem, 1)

                def maxima(n, b, cols, between):
                    for u in range(STEPS):
                        if on_(b) and u < UNITS:
                            s, half, g = u // 4, u // 2 % 2, u % 2
                            dve.wait_ge(max_f[n].sem, max_f[n].val(b, u + 1))
                            nc.vector.tensor_reduce(out=negm[n][:, s, g, 4 * half:4 * half + 4],
                                                    in_=sc_m[u % 2][:, 0:4 * cols].rearrange("p (j k) -> p j k", j=4),
                                                    op=ALU.max, axis=AX.X, negate=True).then_inc(max_ok[n].sem, 1)
                        between(u)

                def divide(n, b, s):
                    k = f"oTT_{n}"
                    dve.wait_ge(filled[k].sem, filled[k].val(b, s + 1))
                    v = wb[s % 2][:].rearrange("p (h w) -> p h w", w=VW)
                    nc.vector.reciprocal(rden[n][:, s, :], v[:, :, DH]).then_inc(rden_ok[n].sem, 1)
                    dve.wait_ge(rden_ok[n].sem, rden_ok[n].val(b, s + 1))
                    nc.vector.tensor_tensor(out=on[n][:, s], in0=v[:, :, 0:DH],
                                            in1=rden[n][:, s, :].unsqueeze(2).broadcast_to([128, H, DH]),
                                            op=ALU.mult).then_inc(drained[k].sem, 1)

                def add_residual(n, b, res, dst):
                    k = f"y_{n}"
                    dve.wait_ge(filled[k].sem, filled[k].val(b))
                    rsem = xres_ok if n == "s" else x2res_ok
                    dve.wait_ge(rsem.sem, rsem.val(b))
                    nc.vector.tensor_tensor(out=dst[:], in0=wb[1][:].rearrange("p (s d) -> p s d", s=NS), in1=res[:],
                                            op=ALU.add).then_inc(drained[k].sem, 1)
                    dve.wait_ge(drained[k].sem, drained[k].val(b))

                def choose(b):
                    dve.wait_ge(drained["pj1"].sem, drained["pj1"].val(b))
                    dve.wait_ge(rn_ok.sem, rn_ok.val(b))
                    for s in range(NS):
                        i = nc.vector.tensor_scalar(gs[:, s, :], graw[:, s, :], rn[:, s:s + 1], itemp[:, 0:1],
                                                    ALU.mult, ALU.mult)
                    i.then_inc(gs_ok.sem, 1)
                    dve.wait_ge(gs_ok.sem, gs_ok.val(b))
                    dve.nop(nofuse=True)
                    for s in range(NS):
                        i = nc.vector.max(top_v[:, s, :], gs[:, s, :])
                    i.then_inc(gate_step.sem, 1)
                    dve.wait_ge(gate_step.sem, gate_step.val(b, 1))
                    dve.nop(nofuse=True)
                    for s in range(NS):
                        i = nc.vector.max_index(top_i[:, s, :], top_v[:, s, :], gs[:, s, :])
                    i.then_inc(gate_step.sem, 1)
                    nc.vector.tensor_tensor(out=dv[:], in0=top_v[:, :, 1], in1=top_v[:, :, 0], op=ALU.subtract)\
                        .then_inc(dv_ok.sem, 1)
                    dve.wait_ge(gate_step.sem, gate_step.val(b, 2))
                    nc.vector.tensor_copy(top_f[:], top_i[:, :, 0:2]).then_inc(gate_step.sem, 1)
                    dve.wait_ge(gate_step.sem, gate_step.val(b, 3))
                    for eq, k in ((eq1, 0), (eq2, 1)):
                        i = nc.vector.tensor_tensor(out=eq[:], in0=iota8[:].unsqueeze(1).broadcast_to([128, NS, E]),
                                                    in1=top_f[:, :, k:k + 1].broadcast_to([128, NS, E]), op=ALU.is_equal)
                    i.then_inc(gate_step.sem, 1)
                    dve.wait_ge(gate_step.sem, gate_step.val(b, 4))
                    nc.vector.tensor_tensor(out=chosen[:], in0=eq1[:], in1=eq2[:], op=ALU.add).then_inc(gate_step.sem, 1)
                    for s in range(NS):
                        dve.wait_ge(gate_step.sem, gate_step.val(b, 5 + s))
                        nc.vector.tensor_tensor(out=before[:, s + 1, :], in0=before[:, s, :], in1=chosen[:, s, :],
                                                op=ALU.add).then_inc(gate_step.sem, 1)

                def rows(b):
                    nc.vector.tensor_scalar(tok[:], tok[:], float(T), None, ALU.add).then_inc(rows_ok.sem, 1)
                    dve.wait_ge(listed.sem, listed.val(b - 1))
                    dve.wait_ge(ln_ok["3"].sem, ln_ok["3"].val(b))
                    for k in range(2):
                        i = nc.vector.tensor_copy(xrow[:, :, k, 0:D], xn["3"][:])
                    i.then_inc(rows_ok.sem, 1)

                def weigh(b):
                    dve.wait_ge(ev_ok.sem, ev_ok.val(b))
                    nc.vector.tensor_scalar(den[:], ev[:], 1.0, None, ALU.add).then_inc(gate_step.sem, 1)
                    dve.wait_ge(gate_step.sem, gate_step.val(b, 10))
                    nc.vector.reciprocal(pr[:, 0, :], den[:]).then_inc(gate_step.sem, 1)
                    dve.wait_ge(gate_step.sem, gate_step.val(b, 11))
                    nc.vector.tensor_tensor(out=pr[:, 1, :], in0=ev[:], in1=pr[:, 0, :], op=ALU.mult)\
                        .then_inc(gate_step.sem, 1)
                    dve.wait_ge(gate_step.sem, gate_step.val(b, 12))
                    nc.vector.tensor_copy(xrow[:, :, :, D + 1], pr[:].rearrange("p k s -> p s k")).then_inc(gate_step.sem, 1)

                def route(b):
                    dve.wait_ge(filled["rank"].sem, filled["rank"].val(b))
                    rank = wb[0][:, 0:NS * E].rearrange("p (s e) -> p s e", s=NS)
                    nc.vector.tensor_tensor(out=pos[:], in0=rank, in1=base[:].unsqueeze(1).broadcast_to([128, NS, E]),
                                            op=ALU.add).then_inc(gate_step.sem, 1)
                    dve.wait_ge(gate_step.sem, gate_step.val(b, 14))
                    nc.vector.tensor_tensor(out=base[:], in0=base[:], in1=wb[0][:, NS * E:(NS + 1) * E], op=ALU.add)\
                        .then_inc(drained["rank"].sem, 1)
                    for eq, h in ((eq1, here[0]), (eq2, here[1])):
                        i = nc.vector.tensor_tensor(out=h[:], in0=eq[:], in1=pos[:], op=ALU.mult)
                    i.then_inc(gate_step.sem, 1)
                    dve.wait_ge(gate_step.sem, gate_step.val(b, 15))
                    for k in range(2):
                        i = nc.vector.tensor_reduce(out=slot_f[:, :, k], in_=here[k][:], op=ALU.add, axis=AX.X)
                    i.then_inc(gate_step.sem, 1)
                    dve.wait_ge(gate_step.sem, gate_step.val(b, 16))
                    dve.wait_ge(rows_ok.sem, rows_ok.val(b, 1))
                    nc.vector.tensor_copy(xrow[:, :, :, D].bitcast(I32), tok[:].unsqueeze(2).broadcast_to([128, NS, 2]))\
                        .then_inc(gate_step.sem, 1)
                    dve.wait_ge(listed.sem, listed.val(b - 1))
                    nc.vector.tensor_copy(slot_i[:], slot_f[:].rearrange("p s k -> p (s k)")).then_inc(slot_ok.sem, 1)

                def body(t, par):
                    def in_x(u):
                        if u == 0 and on_(t + 2):
                            shift("1", t + 2)
                        if u < NS and on_(t - 3):
                            divide("c", t - 3, u)
                        if u == 5 and on_(t - 1):
                            if isinstance(t, int) and t - 1 == 0:
                                dve.wait_ge(preset["cv"].sem, 4)
                            dve.wait_ge(filled["cv"].sem, filled["cv"].val(t - 1))
                            nc.vector.tensor_tensor(
                                out=cvaug[1 - par][0:SC, :, :, 0:DH],
                                in0=wb[0][0:SC, :].rearrange("p (s h i) -> p s h i", s=NS, h=H),
                                in1=bv_b[:].rearrange("p (h i) -> p h i", h=H).unsqueeze(1).broadcast_to([SC, NS, H, DH]),
                                op=ALU.add).then_inc(drained["cv"].sem, 1)
                        if u == 6 and on_(t - 4):
                            rows(t - 4)
                        if u == 7 and on_(t - 2):
                            remainder("cm", t - 2)
                        if u == 8 and on_(t - 3):
                            wait_block(dve, x3_st, t - 4)
                            add_residual("c", t - 3, x2res[1 - par], x3)
                        if u == 9 and on_(t - 3):
                            stats("3", t - 3, x3)
                        if u == 10 and on_(t - 4):
                            weigh(t - 4)
                        if u == 11 and on_(t + 2):
                            remainder("q", t + 2)
                        if u == 12 and on_(t):
                            remainder("ck", t, bk_c)
                        if u == 13 and on_(t - 3):
                            shift("3", t - 3)
                        if u == 14 and on_(t + 2):
                            remainder("k", t + 2)
                            second("k", t + 2)
                        if u == 16 and on_(t - 4):
                            route(t - 4)

                    def in_y(u):
                        if u < NS and on_(t):
                            divide("s", t, u)
                        if u == 7 and on_(t + 1):
                            remainder("m", t + 1)
                        if u == 8 and on_(t):
                            wait_block(dve, x2res_ok, t - 1)
                            add_residual("s", t, xres, x2)
                            stats("2", t, x2)
                        if u == 10 and on_(t):
                            shift("2", t)
                        if u == 11 and on_(t + 3):
                            dve.wait_ge(x_in.sem, x_in.val(t + 3))
                            stats("1", t + 3, xin)
                        if u == 13 and on_(t - 3):
                            dve.wait_ge(ss_ok.sem, ss_ok.val(t - 3))
                            nc.vector.tensor_scalar(ssc[:], ss[:], L2_EPS2, None, ALU.max).then_inc(ssc_ok.sem, 1)
                        if u == 16 and on_(t - 3):
                            choose(t - 3)
                        if u == 18 and on_(t):
                            remainder("cq", t, bq_c)

                    maxima("m", t + 1, S, in_x)
                    t = again(dve, t)
                    maxima("cm", t - 1, SC, in_y)

                dve.wait_ge(iotas.sem, 2)
                def gate():
                    dve.wait_ge(const_in.sem, 16 * len(CONSTS))
                    nc.vector.reciprocal(itemp[:], temp_b[:]).then_inc(gate_set.sem, 1)
                    dve.wait_ge(gate_set.sem, 3)
                    nc.vector.tensor_tensor_reduce(out=sim_j[:], in0=sim_n[:], in1=sim_n[:], scale=1.0, scalar=0.0,
                                                   op0=ALU.mult, op1=ALU.add, accum_out=sim_sq_sum[:]).then_inc(gate_set.sem, 1)
                    dve.wait_ge(gate_set.sem, 4)
                    nc.vector.tensor_scalar(sim_ss[:], sim_sq_sum[:], L2_EPS2, None, ALU.max).then_inc(gate_set.sem, 1)
                    dve.wait_ge(iotas.sem, 3)
                    nc.vector.tensor_scalar(sim_u[:], sim_n[:], sim_rn[:, 0:1], None, ALU.mult).then_inc(gate_set.sem, 1)

                steps(dve, body, {-2: gate, -1: lambda: ones_beside(cvaug, "cv", SC)})

                count = [0]

                def step(i):
                    count[0] += 1
                    i.then_inc(table_step.sem, 1)
                    dve.wait_ge(table_step.sem, count[0])

                dve.wait_ge(iotas.sem, 6)
                step(nc.vector.tensor_copy(base_i, base[:]))
                step(nc.vector.tensor_tensor(out=cnt, in0=base[:], in1=iota_r[:], op=ALU.subtract))
                step(nc.vector.tensor_tensor(out=more, in0=cnt.unsqueeze(2).broadcast_to([128, E, S * B // TS]),
                                             in1=iota_k[:].unsqueeze(1).broadcast_to([128, E, S * B // TS]), op=ALU.is_gt))
                step(nc.vector.tensor_reduce(out=tls, in_=more, op=ALU.add, axis=AX.X))
                step(nc.vector.tensor_copy(ends[:, 0:1], tls[:, 0:1]))
                for e in range(1, E):
                    step(nc.vector.tensor_tensor(out=ends[:, e:e + 1], in0=ends[:, e - 1:e], in1=tls[:, e:e + 1], op=ALU.add))
                step(nc.vector.tensor_scalar(rest_rows, tls, -float(TS), float(REGION), ALU.mult, ALU.add))
                step(nc.vector.memset(tab_f[:, 0, :], 0.0))
                step(nc.vector.tensor_scalar(tab_f[:, 1, :], iota_t[:], float(TS), None, ALU.mult))
                for e in range(E):
                    step(nc.vector.tensor_scalar(past, iota_t[:], ends[:, e:e + 1], None, ALU.is_ge))
                    if e < E - 1:
                        step(nc.vector.tensor_tensor(out=tab_f[:, 0, :], in0=tab_f[:, 0, :], in1=past, op=ALU.add))
                    step(nc.vector.tensor_scalar(skip, past, rest_rows[:, e:e + 1], None, ALU.mult))
                    step(nc.vector.tensor_tensor(out=tab_f[:, 1, :], in0=tab_f[:, 1, :], in1=skip, op=ALU.add))
                nc.vector.tensor_copy(tab[:], tab_f[:]).then_inc(tab_ok.sem, 1)

            @block.tensor
            def _(pe):
                pe.wait_ge(const_in.sem, 16 * len(CONSTS))
                pe.wait_ge(ident_ok.sem, 8)
                user = [None, None]

                def claim(bank, n, b, k=None):
                    if user[bank] is not None:
                        last, value = user[bank]
                        pe.wait_ge(drained[last].sem, value)
                    user[bank] = (n, drained[n].val(b, k))

                def transposes(n, b, bank, pieces, rows):
                    claim(bank, n, b)
                    for j, src in enumerate(pieces):
                        w = src.shape[0]
                        i = nc.tensor.transpose(wb[bank][0:rows, j * w:(j + 1) * w], src, ident[0:w, 0:w])
                    i.then_inc(filled[n].sem, 1)

                def product(n, b, lhsT, rhs, cols):
                    claim(BANK[n], n, b)
                    nc.tensor.matmul(wb[BANK[n]][:, 0:cols], lhsT, rhs, start=True, stop=True).then_inc(filled[n].sem, 1)

                def by_token(n, b, bank, lhs, w, width, rows):
                    claim(bank, n, b)
                    for s in range(NS):
                        i = nc.tensor.matmul(wb[bank][0:rows, s * width:(s + 1) * width], lhs[:, s * rows:(s + 1) * rows],
                                             w, start=True, stop=True)
                    i.then_inc(filled[n].sem, 1)

                def scores(n, b, u, qst, kst, cols, bias):
                    s, half, g = u // 4, u // 2 % 2, u % 2
                    if u >= 2:
                        pe.wait_ge(max_ok[n].sem, max_ok[n].val(b, u - 1))
                    for j in range(4):
                        i = nc.tensor.matmul(sc_m[u % 2][:, j * cols:(j + 1) * cols],
                                             qst[0:KR, 4 * half + j, s * S:(s + 1) * S],
                                             kst[0:KR, HG * g + 4 * half + j, s * cols:(s + 1) * cols],
                                             start=(j == 0 or not bias), stop=not bias, skip_group_check=bool(bias))
                    if bias:
                        i = nc.tensor.matmul(sc_m[u % 2][:, 0:4 * cols], identb[:],
                                             bias[:, s, :].unsqueeze(1).broadcast_to([128, 4, cols]),
                                             start=False, stop=True, skip_group_check=True)
                    i.then_inc(max_f[n].sem, 1)

                def shifted(n, b, u, qst, kst, cols, bias):
                    s, half, g = u // 4, u // 2 % 2, u % 2
                    if u >= 2:
                        pe.wait_ge(exp_ok[n].sem, exp_ok[n].val(b, u - 1))
                    for j in range(4):
                        i = nc.tensor.matmul(sc_a[u % 2][0:cols, j * S:(j + 1) * S],
                                             kst[:, HG * g + 4 * half + j, s * cols:(s + 1) * cols],
                                             qst[:, 4 * half + j, s * S:(s + 1) * S],
                                             start=(j == 0 or not bias), stop=not bias, skip_group_check=bool(bias))
                    if bias:
                        i = nc.tensor.matmul(sc_a[u % 2][0:cols, :], bias[:, s, :],
                                             identb[:].unsqueeze(1).broadcast_to([128, 4, S]),
                                             start=False, stop=True, skip_group_check=True)
                    i.then_inc(st_f[n].sem, 1)

                def values(n, b, u, va, last):
                    s, half, g = u // 4, u // 2 % 2, u % 2
                    pe.wait_ge(exp_ok[n].sem, exp_ok[n].val(b, u + 1))
                    if u % 4 == 0 and s >= 2:
                        pe.wait_ge(oT_ok[n].sem, oT_ok[n].val(b, s - 1))
                    elif u % 4 == 0:
                        wait_block(pe, oT_ok[last[0]], last[1], s + 3)
                    for c in range(4):
                        i = nc.tensor.matmul(pv[s % 2][32 * c:32 * c + VW, (u % 4) * S:(u % 4 + 1) * S],
                                             va[:, s, HG * g + 4 * half + c, :],
                                             probs[u % 3][:, c * S:(c + 1) * S], start=True, stop=True)
                    i.then_inc(pv_ok[n].sem, 1)

                def beside(attn, maxi, between):
                    for u in range(STEPS):
                        if maxi and u < UNITS:
                            scores(maxi[0], maxi[1], u, *maxi[2:])
                        if attn:
                            n, b, qst, kst, va, cols, bias, last = attn
                            if LEAD <= u < UNITS + LEAD:
                                shifted(n, b, u - LEAD, qst, kst, cols, bias)
                            if u >= LEAD + 2:
                                values(n, b, u - LEAD - 2, va, last)
                        between(u)

                def maxima_T(n, b):
                    pe.wait_ge(max_ok[n].sem, max_ok[n].val(b))
                    transposes(n, b, BANK[n], [negm[n][:, s].rearrange("p g j -> p (g j)") for s in range(NS)], H)

                def outputs_T(n, b, s):
                    k = f"oTT_{n}"
                    claim(s % 2, k, b, s + 1)
                    pe.wait_ge(oT_ok[n].sem, oT_ok[n].val(b, s + 1))
                    for slot in range(4):
                        i = nc.tensor.transpose(wb[s % 2][:, slot * S:(slot + 1) * S],
                                                oT[n][:, s, slot * S:(slot + 1) * S], ident[:])
                    i.then_inc(filled[k].sem, 1)

                def divided_T(n, b):
                    pe.wait_ge(drained[f"oTT_{n}"].sem, drained[f"oTT_{n}"].val(b))
                    transposes(f"onT_{n}", b, 1, [on[n][:, s].rearrange("p h i -> p (h i)") for s in range(NS)], 128)

                def project(n, b, w):
                    pe.wait_ge(drained[f"onT_{n}"].sem, drained[f"onT_{n}"].val(b))
                    by_token(f"y_{n}", b, 1, onT[n], w[:], D, S)

                def body(t, par):
                    if on_(t - 1):
                        user[0], user[1] = ("x2T", drained["x2T"].val(t - 1)), ("cq", drained["cq"].val(t - 1))

                    def in_x(u):
                        if u == 4 and on_(t - 1):
                            by_token("cv", t - 1, 0, cT, cw_v[:], D, SC)
                        if u == 6 and on_(t - 2):
                            maxima_T("cm", t - 2)
                        if u < NS and on_(t - 3):
                            outputs_T("c", t - 3, u)
                        if u == 5 and on_(t - 3):
                            divided_T("c", t - 3)
                        if u == 8 and on_(t + 2):
                            pe.wait_ge(ln_ok["1"].sem, ln_ok["1"].val(t + 2))
                            transposes("x1T", t + 2, 0, [xn["1"][:, s, :] for s in range(NS)], 128)
                        if u == 7 and on_(t - 3):
                            project("c", t - 3, cw_o)
                        if u == 10 and on_(t + 2):
                            pe.wait_ge(drained["x1T"].sem, drained["x1T"].val(t + 2))
                            product("q", t + 2, w_q[:], xnT["1"][:], T)
                        if u == 9 and on_(t):
                            pe.wait_ge(c_in.sem, c_in.val(t))
                            transposes("cT", t, 1, [cin[:, s, :] for s in range(NS)], 128)
                        if u == 13 and on_(t + 2):
                            product("k", t + 2, w_k[:], xnT["1"][:], T)
                        if u == 11 and on_(t):
                            pe.wait_ge(drained["cT"].sem, drained["cT"].val(t))
                            product("ck", t, cw_k[:], cT[:], TC)
                        if u == 15 and on_(t - 4):
                            claim(0, "rank", t - 4)
                            pe.wait_ge(gate_step.sem, gate_step.val(t - 4, 9))
                            nc.tensor.matmul(wb[0][:, 0:NS * E], tri[:], chosen[:].rearrange("p s e -> p (s e)"),
                                             start=True, stop=False, skip_group_check=True)
                            nc.tensor.matmul(wb[0][:, 0:NS * E], ones[:], before[:, 0:NS, :].rearrange("p s e -> p (s e)"),
                                             start=False, stop=True, skip_group_check=True)
                            nc.tensor.matmul(wb[0][:, NS * E:(NS + 1) * E], ones[:], before[:, NS, :], start=True, stop=True,
                                             skip_group_check=True).then_inc(filled["rank"].sem, 1)

                    def in_y(u):
                        if u == 6 and on_(t + 1):
                            maxima_T("m", t + 1)
                        if u < NS and on_(t):
                            outputs_T("s", t, u)
                        if u == 4 and on_(t + 2):
                            by_token("v", t + 2, 0, xnT["1"], w_v[:], D, S)
                        if u == 5 and on_(t):
                            divided_T("s", t)
                        if u == 8 and on_(t - 3):
                            pe.wait_ge(ln_ok["3"].sem, ln_ok["3"].val(t - 3))
                            transposes("x3T", t - 3, 0, [xn["3"][:, s, :] for s in range(NS)], 128)
                        if u == 7 and on_(t):
                            project("s", t, w_ff)
                        if u in (10, 11) and on_(t - 3):
                            half = u - 10
                            n = f"pj{half}"
                            pe.wait_ge(drained["x3T"].sem, drained["x3T"].val(t - 3))
                            claim(half, n, t - 3)
                            for k in range(2):
                                s = 2 * half + k
                                i = nc.tensor.matmul(wb[half][:, (D + E) * k:(D + E) * (k + 1)], xnT["3"][:, s * S:(s + 1) * S],
                                                     wpx[:], start=True, stop=True)
                            i.then_inc(filled[n].sem, 1)
                        if u == 15 and on_(t):
                            pe.wait_ge(ln_ok["2"].sem, ln_ok["2"].val(t))
                            transposes("x2T", t, 0, [xn["2"][:, s, :] for s in range(NS)], 128)
                        if u == 17 and on_(t):
                            pe.wait_ge(drained["x2T"].sem, drained["x2T"].val(t))
                            product("cq", t, cw_q[:], xnT["2"][:], T)

                    attn = maxi = None
                    wait_block(pe, max_ok["cm"], t - 2)
                    if on_(t):
                        pe.wait_ge(drained["v"].sem, drained["v"].val(t))
                        pe.wait_ge(stacked["m"].sem, stacked["m"].val(t))
                        attn = ("s", t, qs[par], ks[par], vaug[par], S, None, ("c", t - 3))
                    if on_(t + 1):
                        for n in ("q", "k"):
                            pe.wait_ge(stacked[n].sem, stacked[n].val(t + 1))
                        if isinstance(t, int) and t + 1 < 2:
                            pe.wait_ge(ones_in.sem, ones_in.val(t + 1))
                        maxi = ("m", t + 1, qs[1 - par], ks[1 - par], S, None)
                    beside(attn, maxi, in_x)
                    t = again(pe, t)
                    attn = maxi = None
                    wait_block(pe, max_ok["m"], t + 1)
                    if on_(t - 2):
                        pe.wait_ge(drained["cv"].sem, drained["cv"].val(t - 2))
                        pe.wait_ge(stacked["cm"].sem, stacked["cm"].val(t - 2))
                        attn = ("c", t - 2, cqs[par], cks[par], cvaug[par], SC, mbias[par], ("s", t))
                    if on_(t - 1):
                        for n in ("cq", "ck"):
                            pe.wait_ge(stacked[n].sem, stacked[n].val(t - 1))
                        if isinstance(t, int) and t - 1 < 2:
                            pe.wait_ge(ones_in.sem, ones_in.val(2 + t - 1))
                        pe.wait_ge(mb_ok.sem, mb_ok.val(t - 1))
                        maxi = ("cm", t - 1, cqs[1 - par], cks[1 - par], SC, mbias[1 - par])
                    beside(attn, maxi, in_y)

                def gate():
                    pe.wait_ge(drained[user[0][0]].sem, user[0][1])
                    pe.wait_ge(gate_set.sem, 6)
                    nc.tensor.transpose(wb[0][:, 0:E], sim_u[:], ident[0:E, 0:E]).then_inc(gate_mm.sem, 1)
                    pe.wait_ge(gate_ev.sem, 1)
                    nc.tensor.matmul(wb[0][:, 0:E], wp_n[:], simT[:], start=True, stop=True).then_inc(gate_mm.sem, 1)
                    pe.wait_ge(gate_ev.sem, 2)

                steps(pe, body, {-1: gate})

        phase_a.close()
        phase_b(nc, ctx, sb, sem, dict(ident=ident, tab=tab, wf=wf, xs_d=xs_d, out=out, b1=b1, b2=b2,
                                       h_banks=[sc_m[0][:], sc_m[1][:], sc_a[0][:], sc_a[1][:]],
                                       y_banks=pv, x_bank=wb[0], t_bank=wb[1]))


def phase_b(nc, ctx, sb, sem, a):
    ident, tab, wf = a["ident"], a["tab"], a["wf"]
    h_banks, y_banks, x_bank, t_bank = a["h_banks"], a["y_banks"], a["x_bank"], a["t_bank"]
    xs_d, out, b1, b2 = a["xs_d"], a["out"], a["b1"], a["b2"]
    phase = ctx.enter_context(ExitStack())

    def sa(name, shape, dt=F32):
        return phase.enter_context(nc.sbuf_tensor(name, shape, dt))

    wh, wl, vh, vl = ([sa(f"{n}{i}", [128, F], F32R) for i in range(2)] for n in ("wh", "wl", "vh", "vl"))
    xg = [sa(f"xg{i}", [128, TQ, DW]) for i in range(2)]
    number = [sa(f"number{i}", [128, TQ], I32) for i in range(2)]
    weight = [sa(f"weight{i}", [128, TQ]) for i in range(2)]
    row = [sa(f"row{i}", [128, TQ], I32) for i in range(2)]
    bias = [sa(f"bias{i}", [128, FC]) for i in range(2)]
    bias2 = [sa(f"bias2_{i}", [128, 1]) for i in range(2)]
    xh, xl = ([sa(f"{n}{i}", [128, TS], F32R) for i in range(2)] for n in ("xh", "xl"))
    g = [sa(f"g{c}", [128, TS]) for c in range(FC)]
    gh, gl = ([sa(f"{n}{c}", [128, TS], F32R) for c in range(FC)] for n in ("gh", "gl"))
    yT = sa("yT", [128, TS])
    yo = [sa(f"yo{i}", [128, TQ, D]) for i in range(2)]

    wh_ok, wl_ok, vl_ok = sem("wh_ok"), sem("wl_ok"), sem("vl_ok", 2)
    xg_in, y_st = ([sem(f"{n}{i}", per) for i in range(2)] for n, per in (("xg_in", 16), ("y_st", 16 * TQ)))
    read = sem("read", 2)
    bias_in, bias2_in = ([sem(f"{n}{i}", 16) for i in range(2)] for n in ("bias_in", "bias2_in"))
    xT_f, xh_ok, xl_ok = sem("xT_f"), sem("xh_ok"), sem("xl_ok")
    h_f, gl_ok, w2_done = (sem(n, FC) for n in ("h_f", "gl_ok", "w2_done"))
    g_ok = sem("g_ok", 2 * FC)
    yT_ok, back_f, yo_ok = sem("yT_ok"), sem("back_f"), sem("yo_ok", 2)

    def hi32(ap):
        return ap.bitcast(F32)

    def tiles(engine, body):
        body(0, 0)
        body(0, 1)
        with engine.Fori(1, NT // 2) as j:
            body(j, 0)
            body(j, 1)
        body(NT // 2, 0)

    def ago(j, par, n):
        back = n // 2 + (1 if par < n % 2 else 0)
        return None if isinstance(j, int) and 2 * j + par < n else (j - back, (par - n) % 2)

    with nc.Block() as block:
        @block.sync
        def _(sp):
            def body(j, par):
                i = 2 * j + par
                two = ago(j, par, 2)
                if two:
                    sp.wait_ge(xT_f.sem, xT_f.val(i - 2))
                    sp.wait_ge(read.sem, read.val(i - 2))
                start = sp.value_load(tab[0:1, 1, bass.ds(i, 1)], min_val=0, max_val=SLOTS - TS)
                sp.dma_start(xg[par][:], xs_d[bass.ds(start, TS)].rearrange("(p c) w -> p c w", c=TQ))\
                    .then_inc(xg_in[par].sem, 16)
                e = sp.value_load(tab[0:1, 0, bass.ds(i, 1)], min_val=0, max_val=E - 1)
                if two:
                    sp.wait_ge(g_ok.sem, g_ok.val(i - 2))
                sp.dma_start(bias[par][:], b1[e]).then_inc(bias_in[par].sem, 16)
                if not isinstance(i, int) or i >= 1:
                    second_bias(*ago(j, par, 1))

            def second_bias(j, par):
                i = 2 * j + par
                e = sp.value_load(tab[0:1, 0, bass.ds(i, 1)], min_val=0, max_val=E - 1)
                if ago(j, par, 2):
                    sp.wait_ge(yT_ok.sem, yT_ok.val(i - 2))
                sp.dma_start(bias2[par][:], b2[e].unsqueeze(1)).then_inc(bias2_in[par].sem, 16)

            tiles(sp, body)
            second_bias(NT // 2, 0)

        @block.gpsimd
        def _(pool):
            def body(j, par):
                i, one = 2 * j + par, ago(j, par, 1)
                pool.wait_ge(yo_ok.sem, yo_ok.val(i))
                if one:
                    pool.wait_ge(y_st[one[1]].sem, y_st[one[1]].val(one[0]))
                pool.nop(nofuse=True)
                for c in range(TQ):
                    nc.gpsimd.indirect_dma_start(out=out, in_=yo[par][:, c, :], in_offset=None, compute_op=ALU.add,
                                                 out_offset=bass.IndirectOffsetOnAxis(ap=row[par][:, c:c + 1], axis=0))\
                        .then_inc(y_st[par].sem, 16)

            tiles(pool, body)
            for par, last in ((0, NT // 2), (1, NT // 2 - 1)):
                pool.wait_ge(y_st[par].sem, y_st[par].val(last))

        @block.scalar
        def _(act):
            def split_w(j, par):
                e = act.value_load(tab[0:1, 0, bass.ds(2 * j + par, 1)], min_val=0, max_val=E - 1)
                two = ago(j, par, 2)
                if two:
                    act.wait_ge(h_f.sem, h_f.val(2 * j + par - 2))
                    act.nop(nofuse=True)
                nc.scalar.activation(wh[par][:], wf[:, e, 0, :], ACT.Copy).then_inc(wh_ok.sem, 1)

            def high(j, par):
                act.wait_ge(xT_f.sem, xT_f.val(2 * j + par))
                two = ago(j, par, 2)
                if two:
                    act.wait_ge(h_f.sem, h_f.val(2 * j + par - 2))
                nc.scalar.activation(xh[par][:], x_bank[:], ACT.Copy).then_inc(xh_ok.sem, 1)

            def add_b2(j, par):
                i = 2 * j + par
                act.wait_ge(bias2_in[par].sem, bias2_in[par].val(j))
                act.wait_ge(w2_done.sem, w2_done.val(i))
                if not isinstance(i, int) or i >= 1:
                    act.wait_ge(back_f.sem, back_f.val(i - 1))
                nc.scalar.activation(yT[:], y_banks[par][:], ACT.Identity, bias=bias2[par][:]).then_inc(yT_ok.sem, 1)

            def body(j, par):
                i, one = 2 * j + par, ago(j, par, 1)
                nxt = (j, 1) if par == 0 else (j + 1, 0)
                more_tiles = not isinstance(i, int) or i < NT - 1
                act.wait_ge(bias_in[par].sem, bias_in[par].val(j))
                for c in range(FC):
                    act.wait_ge(h_f.sem, h_f.val(i, c + 1))
                    if one:
                        act.wait_ge(w2_done.sem, w2_done.val(i - 1, c + 1))
                    for part in (gh[c], g[c]):
                        nc.scalar.activation(part[:], h_banks[c], ACT.Gelu, bias=bias[par][:, c:c + 1]).then_inc(g_ok.sem, 1)
                    if c == 0 and more_tiles:
                        split_w(*nxt)
                    if c == 1 and more_tiles:
                        high(*nxt)
                    if c == 1 and one:
                        add_b2(*one)

            split_w(0, 0)
            high(0, 0)
            tiles(act, body)
            add_b2(NT // 2, 0)

        @block.vector
        def _(dve):
            def low(j, par):
                i = 2 * j + par
                dve.wait_ge(xh_ok.sem, xh_ok.val(i))
                nc.vector.tensor_tensor(out=xl[par][:], in0=x_bank[:], in1=hi32(xh[par][:]), op=ALU.subtract)\
                    .then_inc(xl_ok.sem, 1)

            def split_w(j, par):
                e = dve.value_load(tab[0:1, 0, bass.ds(2 * j + par, 1)], min_val=0, max_val=E - 1)
                dve.wait_ge(wh_ok.sem, wh_ok.val(2 * j + par))
                nc.vector.tensor_tensor(out=wl[par][:], in0=wf[:, e, 0, :], in1=hi32(wh[par][:]), op=ALU.subtract)\
                    .then_inc(wl_ok.sem, 1)

            def split_v(j, par):
                i = 2 * j + par
                e = dve.value_load(tab[0:1, 0, bass.ds(i, 1)], min_val=0, max_val=E - 1)
                if ago(j, par, 2):
                    dve.wait_ge(w2_done.sem, w2_done.val(i - 2))
                nc.vector.tensor_copy(vh[par][:], wf[:, e, 1, :]).then_inc(vl_ok.sem, 1)
                dve.wait_ge(vl_ok.sem, vl_ok.val(i, 1))
                nc.vector.tensor_tensor(out=vl[par][:], in0=wf[:, e, 1, :], in1=hi32(vh[par][:]), op=ALU.subtract)\
                    .then_inc(vl_ok.sem, 1)

            def low_g(j, par, c):
                i = 2 * j + par
                dve.wait_ge(g_ok.sem, g_ok.val(i, 2 * c + 2))
                nc.vector.tensor_tensor(out=gl[c][:], in0=g[c][:], in1=hi32(gh[c][:]), op=ALU.subtract).then_inc(gl_ok.sem, 1)

            def read_slots(j, par):
                dve.wait_ge(xg_in[par].sem, xg_in[par].val(j))
                if ago(j, par, 2):
                    dve.wait_ge(yo_ok.sem, yo_ok.val(2 * j + par - 2))
                nc.vector.tensor_copy(number[par][:], xg[par][:, :, D].bitcast(I32)).then_inc(read.sem, 1)
                nc.vector.tensor_copy(weight[par][:], xg[par][:, :, D + 1]).then_inc(read.sem, 1)

            def result(j, par):
                i = 2 * j + par
                dve.wait_ge(read.sem, read.val(i))
                two = ago(j, par, 2)
                if two:
                    dve.wait_ge(y_st[par].sem, y_st[par].val(two[0]))
                nc.vector.tensor_copy(row[par][:], number[par][:]).then_inc(yo_ok.sem, 1)
                dve.wait_ge(back_f.sem, back_f.val(i))
                nc.vector.tensor_tensor(out=yo[par][:], in0=t_bank[:].rearrange("p (c d) -> p c d", c=TQ),
                                        in1=weight[par][:].unsqueeze(2).broadcast_to([128, TQ, D]),
                                        op=ALU.mult).then_inc(yo_ok.sem, 1)

            split_w(0, 0)
            split_v(0, 0)
            low(0, 0)
            read_slots(0, 0)

            def body(j, par):
                one = ago(j, par, 1)
                nxt = (j, 1) if par == 0 else (j + 1, 0)
                more_tiles = not isinstance(j, int) or 2 * j + par < NT - 1
                low_g(j, par, 0)
                if more_tiles:
                    split_w(*nxt)
                low_g(j, par, 1)
                if more_tiles:
                    low(*nxt)
                low_g(j, par, 2)
                low_g(j, par, 3)
                if one:
                    result(*one)
                if more_tiles:
                    split_v(*nxt)
                    read_slots(*nxt)

            tiles(dve, body)
            result(NT // 2, 0)

        @block.tensor
        def _(pe):
            def front(j, par):
                pe.wait_ge(xg_in[par].sem, xg_in[par].val(j))
                for c in range(TQ):
                    i = nc.tensor.transpose(x_bank[:, c * 128:(c + 1) * 128], xg[par][:, c, 0:D], ident[:])
                i.then_inc(xT_f.sem, 1)

            def back(j, par):
                i = 2 * j + par
                pe.wait_ge(yT_ok.sem, yT_ok.val(i))
                if not isinstance(i, int) or i >= 1:
                    pe.wait_ge(yo_ok.sem, yo_ok.val(i - 1))
                for c in range(TQ):
                    last = nc.tensor.transpose(t_bank[:, c * 128:(c + 1) * 128], yT[:, c * 128:(c + 1) * 128], ident[:])
                last.then_inc(back_f.sem, 1)

            def body(j, par):
                i, one = 2 * j + par, ago(j, par, 1)
                pe.wait_ge(wl_ok.sem, wl_ok.val(i))
                pe.wait_ge(xl_ok.sem, xl_ok.val(i))

                def up(c):
                    if one:
                        pe.wait_ge(g_ok.sem, g_ok.val(i - 1, 2 * c + 2))
                    w = slice(c * 128, (c + 1) * 128)
                    nc.tensor.matmul(h_banks[c], wh[par][:, w], xh[par][:], start=True, stop=False)
                    nc.tensor.matmul(h_banks[c], wh[par][:, w], xl[par][:], start=False, stop=False)
                    nc.tensor.matmul(h_banks[c], wl[par][:, w], xh[par][:], start=False, stop=True).then_inc(h_f.sem, 1)

                up(0)
                if one:
                    down(*one, 2)
                    rest(*one, 2)
                up(1)
                if one:
                    down(*one, 3)
                    rest(*one, 3)
                if not isinstance(i, int) or i < NT - 1:
                    front(*((j, 1) if par == 0 else (j + 1, 0)))
                up(2)
                down(j, par, 0)
                up(3)
                rest(j, par, 0)
                down(j, par, 1)
                if one:
                    back(*one)
                rest(j, par, 1)

            def down(j, par, c):
                i, o, w = 2 * j + par, y_banks[par][:], slice(c * 128, (c + 1) * 128)
                if c == 0:
                    pe.wait_ge(vl_ok.sem, vl_ok.val(i))
                if c == 0 and ago(j, par, 2):
                    pe.wait_ge(yT_ok.sem, yT_ok.val(i - 2))
                pe.wait_ge(g_ok.sem, g_ok.val(i, 2 * c + 1))
                nc.tensor.matmul(o, vh[par][:, w], gh[c][:], start=(c == 0), stop=False)
                nc.tensor.matmul(o, vl[par][:, w], gh[c][:], start=False, stop=False)

            def rest(j, par, c):
                pe.wait_ge(gl_ok.sem, gl_ok.val(2 * j + par, c + 1))
                nc.tensor.matmul(y_banks[par][:], vh[par][:, c * 128:(c + 1) * 128], gl[c][:], start=False,
                                 stop=(c == FC - 1)).then_inc(w2_done.sem, 1)

            front(0, 0)
            tiles(pe, body)
            for c in (2, 3):
                down(NT // 2, 0, c)
                rest(NT // 2, 0, c)
            back(NT // 2, 0)

    phase.close()


_OUT = ("out_dram", (B * S + TS, D))


def kernel(x, ctx_1024, mask_BxSxS2_if1, L0_attn_Wq, L0_attn_Wk, L0_attn_Wv, L0_attn_Wff, L0_attn_bff, L0_xattn_Wq,
           L0_xattn_bq, L0_xattn_Wk, L0_xattn_bk, L0_xattn_Wv, L0_xattn_bv, L0_xattn_Wo, L0_xattn_bo, L0_ffn_Wp,
           L0_ffn_sim_matrix, L0_ffn_temperature, L0_ffn_W1, L0_ffn_b1, L0_ffn_W2, L0_ffn_b2):
    import numpy as np
    import concourse.bacc as bacc
    from concourse.bass_utils import run_bass_kernel_spmd

    by_place = np.array([h * DH + i for i in range(DH) for h in range(H)])
    by_slot = np.array([(HG * g + 4 * u + c) * DH + i for u in range(2) for g in range(2) for c in range(4)
                        for i in range(DH)])
    a = np.asarray
    arrays = {
        "x": a(x), "ctx": a(ctx_1024), "mask": a(mask_BxSxS2_if1),
        "Wq": a(L0_attn_Wq).T[:, by_place], "Wk": a(L0_attn_Wk).T[:, by_place], "Wv": a(L0_attn_Wv).T,
        "Wff": a(L0_attn_Wff).T[by_slot], "bff": a(L0_attn_bff),
        "xWq": a(L0_xattn_Wq).T[:, by_place], "xbq": a(L0_xattn_bq)[by_place],
        "xWk": a(L0_xattn_Wk).T[:, by_place], "xbk": a(L0_xattn_bk)[by_place],
        "xWv": a(L0_xattn_Wv).T, "xbv": a(L0_xattn_bv), "xWo": a(L0_xattn_Wo).T[by_slot], "xbo": a(L0_xattn_bo),
        "Wp": a(L0_ffn_Wp), "WpT": a(L0_ffn_Wp).T, "sim": a(L0_ffn_sim_matrix),
        "temp": a(L0_ffn_temperature).reshape(1),
        "W1": a(L0_ffn_W1), "b1": a(L0_ffn_b1).reshape(E, FC, 128).transpose(0, 2, 1), "W2": a(L0_ffn_W2), "b2": a(L0_ffn_b2),
    }
    nc = bacc.Bacc("TRN2", target_bir_lowering=False, num_devices=1)
    fed, args = {}, []
    for name, value in arrays.items():
        value = np.ascontiguousarray(value)
        fed[f"{name}_dram"] = value
        args.append(nc.dram_tensor(f"{name}_dram", value.shape, mybir.dt.from_np(value.dtype), kind="ExternalInput").ap())
    out = nc.dram_tensor(_OUT[0], _OUT[1], F32, kind="ExternalOutput").ap()
    program(nc, *args, out)
    result = run_bass_kernel_spmd(nc, [fed], core_ids=[0])
    return result.results[0][_OUT[0]][:B * S].reshape(B, S, D)
```
